# Optimizing a Trainium2 kernel written in Bass

```python
import numpy as np
import jax
import jax.numpy as jnp

def _softmax(x, axis=-1):
    return jax.nn.softmax(x, axis=axis)

def _gelu(x):
    return jax.nn.gelu(x, approximate=True)

def _silu(x):
    return jax.nn.silu(x)

def _sigmoid(x):
    return jax.nn.sigmoid(x)

def _layernorm(x, axis=-1, eps=1e-05):
    m = jnp.mean(x, axis=axis, keepdims=True)
    v = jnp.var(x, axis=axis, keepdims=True)
    return (x - m) / jnp.sqrt(v + eps)

def _scatter_add(tgt, idx, src, axis=0):
    return tgt.at[idx].add(src)

def _segment_sum(src, seg, n):
    return jax.ops.segment_sum(src, seg, n)
kernel_name = 'mk_xattn_ffn_d2_seqx_r8_54e696'

def setup_inputs(seed: int=0):
    np.random.seed(seed)
    _w = jnp.asarray

    def _rec_inputs():
        import jax
        import jax.numpy as jnp
        _rk = jax.random.key(seed)
        x = -0.0002928 + 1 * jax.random.normal(jax.random.fold_in(_rk, 1), (32, 128, 128), jnp.float32)
        _lenS = 128 - jax.random.randint(jax.random.fold_in(_rk, 7), (32,), 0, max(1, 128 // 4) + 1, jnp.int32)
        _lenS2 = 128 - jax.random.randint(jax.random.fold_in(_rk, 8), (32,), 0, max(1, 128 // 4) + 1, jnp.int32)
        _ctx_1024P = jax.random.normal(jax.random.fold_in(_rk, 11), (32, 16, 128), jnp.float32)
        _ctx_1024c = jax.random.dirichlet(jax.random.fold_in(_rk, 511), 0.3 * jnp.ones((16,), jnp.float32), (32, 128))
        _ctx_1024t = jnp.einsum('bsk,bkd->bsd', _ctx_1024c, _ctx_1024P)
        _ctx_1024t = _ctx_1024t * jax.lax.rsqrt(jnp.mean(jnp.square(_ctx_1024t)) + 1e-12) * 0.953939
        ctx_1024 = -1.39393e-06 + 0.999914 * (_ctx_1024t + 0.3 * jax.random.normal(jax.random.fold_in(_rk, 611), (32, 128, 128), jnp.float32))
        return (x, ctx_1024)
    x, ctx_1024 = _rec_inputs()

    def _L0_xattn_setup():
        import jax, jax.numpy as jnp
        import numpy as np
        D_MODEL = 128
        N_HEAD = 16
        N_D = D_MODEL // N_HEAD
        key = jax.random.key(seed)
        ks = jax.random.split(key, 11)
        B, T, D = (2, 256, D_MODEL)
        s = 1.0 / np.sqrt(D)
        return {'q': jax.random.normal(ks[0], (B, T, D), jnp.float32), 'k': jax.random.normal(ks[1], (B, T, D), jnp.float32), 'v': jax.random.normal(ks[2], (B, T, D), jnp.float32), 'w_q': jax.random.normal(ks[3], (D, D), jnp.float32) * s, 'b_q': jax.random.normal(ks[4], (D,), jnp.float32) * 0.01, 'w_k': jax.random.normal(ks[5], (D, D), jnp.float32) * s, 'b_k': jax.random.normal(ks[6], (D,), jnp.float32) * 0.01, 'w_v': jax.random.normal(ks[7], (D, D), jnp.float32) * s, 'b_v': jax.random.normal(ks[8], (D,), jnp.float32) * 0.01, 'w_o': jax.random.normal(ks[9], (D, D), jnp.float32) * s, 'b_o': jax.random.normal(ks[10], (D,), jnp.float32) * 0.01}
    _L0_xattn_all = _L0_xattn_setup()
    _L0_xattn_in = {k: v for k, v in _L0_xattn_all.items() if k in ('w_q', 'b_q', 'w_k', 'b_k', 'w_v', 'b_v', 'w_o', 'b_o')}
    del _L0_xattn_all

    def _L0_ffn_setup():
        import jax, jax.numpy as jnp
        import numpy as np
        B, S, H, E = (2, 1024, 128, 8)
        SCALE = 0.5
        key = jax.random.key(seed)
        k1, k2 = jax.random.split(key)
        x = jax.random.normal(k1, (B, S, H), dtype=jnp.float32)
        gate_w = jax.random.normal(k2, (E, H), dtype=jnp.float32) * 0.02
        coeff = SCALE * (1.0 + 0.05 * jnp.arange(E, dtype=jnp.float32))
        expert_w = coeff[:, None, None] * jnp.eye(H, dtype=jnp.float32)
        return {'x': x, 'gate_w': gate_w, 'expert_w': expert_w}
    _L0_ffn_all = _L0_ffn_setup()
    _L0_ffn_in = {k: v for k, v in _L0_ffn_all.items() if k in ('gate_w', 'expert_w')}
    del _L0_ffn_all

    def _L1_xattn_setup():
        import jax, jax.numpy as jnp
        import numpy as np
        HIDDEN = 128
        HEADS = 16
        HEAD_DIM = HIDDEN // HEADS
        key = jax.random.key(seed)
        ks = jax.random.split(key, 11)
        B, T, D = (2, 256, HIDDEN)
        s = 1.0 / np.sqrt(D)
        return {'query': jax.random.normal(ks[0], (B, T, D), jnp.float32), 'key': jax.random.normal(ks[1], (B, T, D), jnp.float32), 'value': jax.random.normal(ks[2], (B, T, D), jnp.float32), 'Wq': jax.random.normal(ks[3], (D, D), jnp.float32) * s, 'bq': jnp.zeros((D,), jnp.float32), 'Wk': jax.random.normal(ks[4], (D, D), jnp.float32) * s, 'bk': jnp.zeros((D,), jnp.float32), 'Wv': jax.random.normal(ks[5], (D, D), jnp.float32) * s, 'bv': jnp.zeros((D,), jnp.float32), 'Wo': jax.random.normal(ks[6], (D, D), jnp.float32) * s, 'bo': jnp.zeros((D,), jnp.float32)}
    _L1_xattn_all = _L1_xattn_setup()
    _L1_xattn_in = {k: v for k, v in _L1_xattn_all.items() if k in ('Wq', 'bq', 'Wk', 'bk', 'Wv', 'bv', 'Wo', 'bo')}
    del _L1_xattn_all

    def _L1_ffn_setup():
        import jax, jax.numpy as jnp
        import numpy as np
        NUM_EXPERTS = 8
        TOP_K = 2
        B, T, D, F = (4, 256, 128, 352)
        key = jax.random.key(seed)
        ks = jax.random.split(key, 5)
        return {'x': jax.random.normal(ks[0], (B, T, D), dtype=jnp.float32), 'router_w': jax.random.normal(ks[1], (D, NUM_EXPERTS), dtype=jnp.float32) * 0.02, 'gate_proj': jax.random.normal(ks[2], (NUM_EXPERTS, D, F), dtype=jnp.float32) * 0.02, 'up_proj': jax.random.normal(ks[3], (NUM_EXPERTS, D, F), dtype=jnp.float32) * 0.02, 'down_proj': jax.random.normal(ks[4], (NUM_EXPERTS, F, D), dtype=jnp.float32) * 0.02}
    _L1_ffn_all = _L1_ffn_setup()
    _L1_ffn_in = {k: v for k, v in _L1_ffn_all.items() if k in ('router_w', 'gate_proj', 'up_proj', 'down_proj')}
    del _L1_ffn_all
    return {'x': x, 'ctx_1024': ctx_1024, 'L0_xattn_w_q': _L0_xattn_in['w_q'], 'L0_xattn_b_q': _L0_xattn_in['b_q'], 'L0_xattn_w_k': _L0_xattn_in['w_k'], 'L0_xattn_b_k': _L0_xattn_in['b_k'], 'L0_xattn_w_v': _L0_xattn_in['w_v'], 'L0_xattn_b_v': _L0_xattn_in['b_v'], 'L0_xattn_w_o': _L0_xattn_in['w_o'], 'L0_xattn_b_o': _L0_xattn_in['b_o'], 'L0_ffn_gate_w': _L0_ffn_in['gate_w'], 'L0_ffn_expert_w': _L0_ffn_in['expert_w'], 'L1_xattn_Wq': _L1_xattn_in['Wq'], 'L1_xattn_bq': _L1_xattn_in['bq'], 'L1_xattn_Wk': _L1_xattn_in['Wk'], 'L1_xattn_bk': _L1_xattn_in['bk'], 'L1_xattn_Wv': _L1_xattn_in['Wv'], 'L1_xattn_bv': _L1_xattn_in['bv'], 'L1_xattn_Wo': _L1_xattn_in['Wo'], 'L1_xattn_bo': _L1_xattn_in['bo'], 'L1_ffn_router_w': _L1_ffn_in['router_w'], 'L1_ffn_gate_proj': _L1_ffn_in['gate_proj'], 'L1_ffn_up_proj': _L1_ffn_in['up_proj'], 'L1_ffn_down_proj': _L1_ffn_in['down_proj']}

def reference(x, ctx_1024, L0_xattn_w_q, L0_xattn_b_q, L0_xattn_w_k, L0_xattn_b_k, L0_xattn_w_v, L0_xattn_b_v, L0_xattn_w_o, L0_xattn_b_o, L0_ffn_gate_w, L0_ffn_expert_w, L1_xattn_Wq, L1_xattn_bq, L1_xattn_Wk, L1_xattn_bk, L1_xattn_Wv, L1_xattn_bv, L1_xattn_Wo, L1_xattn_bo, L1_ffn_router_w, L1_ffn_gate_proj, L1_ffn_up_proj, L1_ffn_down_proj):
    import jax
    import jax.numpy as jnp

    def _L0_xattn_ref(q, k, v, w_q, b_q, w_k, b_k, w_v, b_v, w_o, b_o):
        import jax, jax.numpy as jnp
        import numpy as np
        D_MODEL = 128
        N_HEAD = 16
        N_D = D_MODEL // N_HEAD
        B, T, D = q.shape
        H, Dh = (N_HEAD, N_D)
        qp = q @ w_q.T + b_q
        kp = k @ w_k.T + b_k
        vp = v @ w_v.T + b_v
        qh = qp.reshape(B, T, H, Dh).transpose(0, 2, 1, 3)
        kh = kp.reshape(B, T, H, Dh).transpose(0, 2, 1, 3)
        vh = vp.reshape(B, T, H, Dh).transpose(0, 2, 1, 3)
        scale = 1.0 / jnp.sqrt(jnp.asarray(Dh, qh.dtype))
        score = jnp.einsum('bhqd,bhkd->bhqk', qh, kh) * scale
        attn = jax.nn.softmax(score, axis=-1)
        out = jnp.einsum('bhqk,bhkd->bhqd', attn, vh)
        out = out.transpose(0, 2, 1, 3).reshape(B, T, D)
        return out @ w_o.T + b_o

    def _L0_ffn_ref(x, gate_w, expert_w):
        import jax, jax.numpy as jnp
        import numpy as np
        B, S, H, E = (2, 1024, 128, 8)
        SCALE = 0.5
        scores = jnp.einsum('bsh,eh->bse', x, gate_w)
        chosen = jnp.argmax(scores, axis=-1)
        onehot = jax.nn.one_hot(chosen, gate_w.shape[0], dtype=x.dtype)
        expert_out = jnp.einsum('bsh,efh->bsef', x, expert_w)
        return x + jnp.einsum('bsef,bse->bsf', expert_out, onehot)

    def _L1_xattn_ref(query, key, value, Wq, bq, Wk, bk, Wv, bv, Wo, bo):
        import jax, jax.numpy as jnp
        import numpy as np
        HIDDEN = 128
        HEADS = 16
        HEAD_DIM = HIDDEN // HEADS
        B, Tq, D = query.shape
        Tk = key.shape[1]
        H, Hd = (HEADS, HEAD_DIM)
        Q = (query @ Wq + bq).reshape(B, Tq, H, Hd).transpose(0, 2, 1, 3)
        K = (key @ Wk + bk).reshape(B, Tk, H, Hd).transpose(0, 2, 1, 3)
        V = (value @ Wv + bv).reshape(B, Tk, H, Hd).transpose(0, 2, 1, 3)
        scale = jnp.sqrt(jnp.asarray(Hd, Q.dtype))
        scores = jnp.einsum('bhqd,bhkd->bhqk', Q, K) / scale
        causal = jnp.triu(jnp.ones((Tq, Tk), bool), k=1)
        scores = jnp.where(causal[None, None], jnp.asarray(-jnp.inf, scores.dtype), scores)
        attn = jax.nn.softmax(scores, axis=-1)
        out = jnp.einsum('bhqk,bhkd->bhqd', attn, V)
        out = out.transpose(0, 2, 1, 3).reshape(B, Tq, D)
        return out @ Wo + bo

    def _L1_ffn_ref(x, router_w, gate_proj, up_proj, down_proj):
        import jax, jax.numpy as jnp
        import numpy as np
        NUM_EXPERTS = 8
        TOP_K = 2
        B, T, D, F = (4, 256, 128, 352)
        scores = jnp.einsum('btd,de->bte', x, router_w).astype(jnp.float32)
        probs = jax.nn.softmax(scores, axis=-1)
        routing_weights, routing_idx = jax.lax.top_k(probs, TOP_K)
        routing_weights = (routing_weights / jnp.sum(routing_weights, axis=-1, keepdims=True)).astype(x.dtype)
        one_hot = jax.nn.one_hot(routing_idx, NUM_EXPERTS, dtype=x.dtype)
        expert_w = jnp.einsum('btke,btk->bte', one_hot, routing_weights)
        dispatched = jnp.einsum('btd,btke->bted', x, one_hot)
        gate = jnp.einsum('bted,edf->btef', dispatched, gate_proj)
        up = jnp.einsum('bted,edf->btef', dispatched, up_proj)
        acts = jax.nn.silu(gate) * up
        expert_out = jnp.einsum('btef,efd->bted', acts, down_proj)
        return jnp.einsum('bted,bte->btd', expert_out, expert_w)
    x = x + _L0_xattn_ref(_layernorm(x, axis=-1), ctx_1024, ctx_1024, L0_xattn_w_q, L0_xattn_b_q, L0_xattn_w_k, L0_xattn_b_k, L0_xattn_w_v, L0_xattn_b_v, L0_xattn_w_o, L0_xattn_b_o)
    x = x + _L0_ffn_ref(_layernorm(x, axis=-1), L0_ffn_gate_w, L0_ffn_expert_w)
    x = x + _L1_xattn_ref(_layernorm(x, axis=-1), ctx_1024, ctx_1024, L1_xattn_Wq, L1_xattn_bq, L1_xattn_Wk, L1_xattn_bk, L1_xattn_Wv, L1_xattn_bv, L1_xattn_Wo, L1_xattn_bo)
    x = x + _L1_ffn_ref(_layernorm(x, axis=-1), L1_ffn_router_w, L1_ffn_gate_proj, L1_ffn_up_proj, L1_ffn_down_proj)
    return x

_drawn_inputs = setup_inputs


def setup_inputs(seed=0):
    import zlib

    import numpy as np

    out = dict(_drawn_inputs(seed))
    spreads = {'L1_xattn_bq': (0.0, 0.8),
     'L1_xattn_bk': (0.0, 0.8),
     'L1_xattn_bv': (0.0, 0.1),
     'L1_xattn_bo': (0.0, 0.1)}
    factors = {'L0_xattn_b_q': 8.0,
     'L0_xattn_b_k': 8.0,
     'L0_xattn_b_v': 5.698,
     'L0_xattn_b_o': 5.574,
     'L0_ffn_gate_w': 2.702,
     'L1_ffn_router_w': 8.0,
     'L1_ffn_gate_proj': 8.0,
     'L1_ffn_up_proj': 8.0,
     'L1_ffn_down_proj': 8.0}
    for name, (base, spread) in spreads.items():
        noise = np.random.default_rng([zlib.crc32(name.encode()), seed]).standard_normal(out[name].shape)
        drawn = base * np.exp(spread * noise) if base else spread * noise
        out[name] = jnp.asarray(drawn.astype(out[name].dtype))
    for name, factor in factors.items():
        out[name] = (out[name] * factor).astype(out[name].dtype)
    return out
```

```python
from contextlib import ExitStack

import concourse.bass as bass
from concourse import mybir

ALU = mybir.AluOpType
ACT = mybir.ActivationFunctionType
AX_X = mybir.AxisListType.X
F32 = mybir.dt.float32
BF16 = mybir.dt.bfloat16

B = 32
T = 128
D = 128
H = 16
DH = D // H
G = 4
NG = B // G
GT = G * T
VW = DH + 1
Q_PARTS = (0, 0, 0, 1, 1, 2)
K_PARTS = (0, 1, 2, 0, 1, 0)
PROD = DH * len(Q_PARTS)
ROWS = PROD + 2
C4 = 4
NC = H // C4
E = 8
F = 352
FCH = ((0, 128), (128, 128), (256, 96))
NEG = -1e30
EPS = 1e-5


def earlier(count):
    return max(count, 0) if isinstance(count, int) else count


class Group:

    def __init__(self, turn, p):
        self.turn, self.p, self.n = turn, p, turn * 2 + p

    def after(self):
        return Group(self.turn, 1) if self.p == 0 else Group(self.turn + 1, 0)

    def before(self):
        return Group(self.turn, 0) if self.p == 1 else Group(self.turn - 1, 1)


class Seq:

    def __init__(self, g, b):
        self.g, self.b, self.m, self.p, self.turn = g, b, g.n * G + b, b % 2, g.n * (G // 2) + b // 2

    def ahead(self, k):
        if 0 <= self.b + k < G:
            return Seq(self.g, self.b + k)
        return Seq(self.g.after(), self.b + k - G) if k > 0 else Seq(self.g.before(), self.b + k + G)


def k_parity(e, f):
    return (e * len(FCH) + f) % 2


def all_groups(eng, body):
    body(Group(0, 0))
    body(Group(0, 1))
    with eng.Fori(1, NG // 2) as i:
        body(Group(i, 0))
        body(Group(i, 1))


def middle_groups(eng, body):
    with eng.Fori(0, NG // 2 - 1) as i:
        body(Group(i, 1))
        body(Group(i + 1, 0))


FIRST, LAST = Group(0, 0), Group(NG // 2 - 1, 1)


def build(nc, a, out):
    ctx = ExitStack()

    in_use = []
    def sem(name):
        in_use.append(nc.alloc_semaphore(name=name))
        return in_use[-1]

    def clear_semaphores():
        nc.clear_and_free_semaphores(in_use)
        nc.all_engine_barrier()
        in_use.clear()

    def scratch(name, shape, dt):
        return nc.dram_tensor(name, shape, dt, kind="Internal").ap()

    with ctx:
        def sb(name, shape, dt=F32, to=ctx):
            return to.enter_context(nc.sbuf_tensor(name, shape, dt))

        bank = [ctx.enter_context(nc.psum_tensor(f"bank{i}", [128, 512], F32)) for i in range(8)]

        q_parts = scratch("q_parts", (3, D, B * T), BF16)
        k_parts = scratch("k_parts", (2, 3, D, B * T), BF16)
        v_ones = scratch("v_ones", (2, B, T, H * VW), F32)
        x_attn0 = scratch("x_attn0", (B, T, D), F32)
        x_ffn0 = scratch("x_ffn0", (B, T, D), F32)
        x_attn1 = scratch("x_attn1", (B, T, D), F32)

        ident = sb("ident", [128, 128])
        ident4 = sb("ident4", [128, 4, 128], BF16)
        future = sb("future", [128, 128], BF16)
        wq = [sb(f"wq{l}", [128, D]) for l in range(2)]
        wk = [sb(f"wk{l}", [128, D]) for l in range(2)]
        wv = [sb(f"wv{l}", [128, D]) for l in range(2)]
        wo = [sb(f"wo{l}", [128, D]) for l in range(2)]
        bq = [sb(f"bq{l}", [128, 1]) for l in range(2)]
        bk = [sb(f"bk{l}", [128, 1]) for l in range(2)]
        bv = [sb(f"bv{l}", [128, D]) for l in range(2)]
        bo = [sb(f"bo{l}", [128, D]) for l in range(2)]
        expert0_w = sb("expert0_w", [128, E, D])
        gate0_w = sb("gate0_w", [128, E])
        minus_half, epsilon = sb("minus_half", [128, G]), sb("epsilon", [128, G])
        pool_cell, dve_cell = sb("pool_cell", [128, NC]), sb("dve_cell", [128, 1])
        rank = sb("expert_rank", [128, G, E])
        rank = sb("rank", [128, G, E])

        def prepare():
            loaded, zeroed, ones_set = sem("p_loaded"), sem("p_zeroed"), sem("p_ones")
            turned, kept, made = sem("p_turned"), sem("p_kept"), sem("p_made")
            with ExitStack() as own, nc.Block() as block:
                w_raw = [sb(f"w_raw{i}", [128, D], to=own) for i in range(4)]
                e_raw = sb("e_raw", [128, E, D], to=own)
                g_raw = sb("g_raw", [E, D], to=own)
                loads = [(w_raw[i][:], a[n]) for i, n in enumerate(
                    ("L0_xattn_w_q", "L0_xattn_w_k", "L0_xattn_w_v", "L0_xattn_w_o"))]
                loads += [(g_raw[:], a["L0_ffn_gate_w"]),
                          (e_raw[:], a["L0_ffn_expert_w"].rearrange("e f h -> f e h")),
                          (wq[1][:], a["L1_xattn_Wq"]), (wk[1][:], a["L1_xattn_Wk"]),
                          (wv[1][:], a["L1_xattn_Wv"]), (wo[1][:], a["L1_xattn_Wo"])]
                for l, pre in enumerate(("L0_xattn_b_", "L1_xattn_b")):
                    loads += [(bq[l][:], a[pre + "q"].unsqueeze(1)), (bk[l][:], a[pre + "k"].unsqueeze(1)),
                              (bv[l][:], a[pre + "v"].partition_broadcast(128)),
                              (bo[l][:], a[pre + "o"].partition_broadcast(128))]

                @block.sync
                def _(sp):
                    for to, src in loads:
                        sp.dma_start(to, src).then_inc(loaded, 16)
                    sp.wait_ge(loaded, 16 * len(loads))

                @block.gpsimd
                def _(pool):
                    pool.memset(ident[:], 0.0).then_inc(zeroed, 1)
                    pool.memset(ident4[:], 0.0).then_inc(zeroed, 1)
                    pool.memset(future[:], 0.0).then_inc(zeroed, 1)
                    pool.memset(minus_half[:], -0.5).then_inc(made, 1)
                    pool.memset(epsilon[:], EPS)
                    pool.memset(pool_cell[:], 0.0)
                    for e in range(E):
                        pool.memset(rank[:, :, e], float(E - e))
                    pool.wait_ge(zeroed, 3)
                    pool.affine_select(out=ident[:], in_=ident[:], compare_op=ALU.not_equal, fill=1.0, base=0,
                                       pattern=[[-1, 128]], channel_multiplier=1).then_inc(made, 1)
                    pool.affine_select(out=ident4[:], in_=ident4[:], compare_op=ALU.not_equal, fill=1.0, base=0,
                                       pattern=[[0, 4], [-1, 128]], channel_multiplier=1).then_inc(made, 1)
                    pool.affine_select(out=future[:], in_=future[:], compare_op=ALU.is_ge, fill=NEG, base=0,
                                       pattern=[[1, 128]], channel_multiplier=-1).then_inc(made, 1)

                @block.tensor
                def _(pe):
                    pe.wait_ge(loaded, 16 * len(loads))
                    pe.wait_ge(made, 4)
                    for i in range(4):
                        pe.transpose(bank[0][:, i * D:(i + 1) * D], w_raw[i][:], ident[:])
                    for e in range(E):
                        pe.transpose(bank[1 + e // 4][:, e % 4 * D:(e % 4 + 1) * D], e_raw[:, e, :], ident[:])
                    pe.transpose(bank[3][:, 0:E], g_raw[:], ident[0:E, 0:E]).then_inc(turned, 1)

                @block.vector
                def _(dve):
                    dve.wait_ge(turned, 1)
                    for i, w in enumerate((wq, wk, wv, wo)):
                        dve.tensor_copy(w[0][:], bank[0][:, i * D:(i + 1) * D])
                    for c in range(2):
                        dve.tensor_copy(expert0_w[:, 4 * c:4 * c + 4, :], bank[1 + c][:].rearrange("p (e d) -> p e d", e=4))
                    dve.tensor_copy(gate0_w[:], bank[3][:, 0:E]).then_inc(kept, 1)

        def layernorm_dve(dve, src, stats, mv, xn, rstd, s_in, n_in, s_stats, s_mv, s_rstd, s_xn, n):
            dve.wait_ge(s_in, n_in)
            for t in range(G):
                last = dve.bn_stats(stats[:, t, :], src[:, t, :])
            last.then_inc(s_stats, 1)
            dve.wait_ge(s_stats, n + 1)
            dve.memset(dve_cell[:], 0.0)
            for t in range(G):
                last = dve.bn_aggr(mv[:, t, :], stats[:, t, :])
            last.then_inc(s_mv, 1)
            dve.wait_ge(s_rstd, n + 1)
            for t in range(G):
                last = dve.tensor_scalar(xn[:, t, :], src[:, t, :], mv[:, t, 0:1], rstd[:, t:t + 1],
                                         ALU.subtract, ALU.mult)
            last.then_inc(s_xn, 1)

        def rstd_pool(pool, mv, veps, rstd, s_mv, s_veps, s_rstd, n):
            pool.wait_ge(s_mv, n + 1)
            pool.tensor_tensor(veps[:], mv[:, :, 1], epsilon[:], ALU.add).then_inc(s_veps, 1)
            pool.wait_ge(s_veps, n + 1)
            pool.tensor_tensor(rstd[:], veps[:], minus_half[:], ALU.pow).then_inc(s_rstd, 1)

        def project_keys_values():
            ctx_in, turned, kept = [sem(f"kv_ctx{p}") for p in range(2)], sem("kv_turned"), sem("kv_kept")
            k_ps, v_ps = sem("kv_k_ps"), sem("kv_v_ps")
            part0, rest0, part1, part2 = sem("kv_part0"), sem("kv_rest0"), sem("kv_part1"), sem("kv_part2")
            v_done, ones = sem("kv_v_done"), sem("kv_ones")
            k_out, v_out = ([[sem(f"kv_{k}{p}{l}") for l in range(2)] for p in range(2)] for k in ("k_out", "v_out"))
            with ExitStack() as own, nc.Block() as block:
                c_in = [sb(f"c_in{p}", [128, G, D], to=own) for p in range(2)]
                c_t = [sb(f"c_t{p}", [128, GT], to=own) for p in range(2)]
                parts = [[sb(f"kparts{p}{l}", [128, 3, GT], BF16, own) for l in range(2)] for p in range(2)]
                rest = [sb(f"krest{l}", [128, GT], to=own) for l in range(2)]
                vals = [[sb(f"vals{p}{l}", [128, G * H, VW], to=own) for l in range(2)] for p in range(2)]
                t_bank, k_bank, v_bank = bank[0:2], bank[2:4], bank[4:6]

                @block.sync
                def _(sp):
                    def load(g):
                        n, p = g.n, g.p
                        sp.wait_ge(turned, earlier(n - 1))
                        sp.dma_start(c_in[p][:], a["ctx_1024"][bass.ds(n * G, G)].rearrange("b t d -> t b d")
                                     ).then_inc(ctx_in[p], 16)
                    all_groups(sp, load)

                @block.tensor
                def _(pe):
                    def body(g):
                        n, p = g.n, g.p
                        pe.wait_ge(ctx_in[p], g.turn * 16 + 16)
                        pe.wait_ge(kept, earlier(n - 1))
                        for t in range(G):
                            mm = pe.transpose(t_bank[p][:, t * T:(t + 1) * T], c_in[p][:, t, :], ident[:])
                        mm.then_inc(turned, 1)
                        pe.wait_ge(kept, n + 1)
                        for l in range(2):
                            pe.wait_ge(rest0, earlier(n * 2 + l - 1))
                            pe.matmul(k_bank[l][:], wk[l][:], c_t[p][:], start=True, stop=True).then_inc(k_ps, 1)
                            pe.wait_ge(v_done, earlier(n * 2 + l - 1))
                            for t in range(G):
                                mm = pe.matmul(v_bank[l][:, t * D:(t + 1) * D], c_t[p][:, t * T:(t + 1) * T],
                                               wv[l][:], start=True, stop=True)
                            mm.then_inc(v_ps, 1)
                    all_groups(pe, body)

                @block.scalar
                def _(act):
                    def body(g):
                        n, p = g.n, g.p
                        act.wait_ge(turned, n + 1)
                        act.wait_ge(v_ps, earlier(n * 2 - 2))
                        act.copy(c_t[p][:], t_bank[p][:]).then_inc(kept, 1)
                        for l in range(2):
                            act.wait_ge(k_ps, n * 2 + l + 1)
                            act.wait_ge(k_out[p][l], earlier(g.turn * 16))
                            act.activation(parts[p][l][:, 0, :], k_bank[l][:], ACT.Identity, bias=bk[l][:]
                                           ).then_inc(part0, 1)
                            act.wait_ge(rest0, n * 2 + l + 1)
                            act.copy(parts[p][l][:, 1, :], rest[l][:]).then_inc(part1, 1)
                            act.wait_ge(part2, n * 2 + l + 1)
                            act.dma_start(k_parts[l][:, :, bass.ds(n * GT, GT)].rearrange("c r t -> r c t"),
                                          parts[p][l][:]).then_inc(k_out[p][l], 16)
                    all_groups(act, body)
                    for p in range(2):
                        for l in range(2):
                            act.wait_ge(k_out[p][l], 16 * (NG // 2))

                @block.vector
                def _(dve):
                    for p in range(2):
                        for l in range(2):
                            dve.memset(vals[p][l][:], 1.0).then_inc(ones, 1)
                    dve.wait_ge(ones, 4)

                    def body(g):
                        n, p = g.n, g.p
                        for l in range(2):
                            dve.wait_ge(part0, n * 2 + l + 1)
                            dve.wait_ge(part2, earlier(n * 2 + l - 1))
                            dve.scalar_tensor_tensor(out=rest[l][:], in0=k_bank[l][:], scalar=bk[l][:],
                                                     in1=parts[p][l][:, 0, :], op0=ALU.add,
                                                     op1=ALU.subtract).then_inc(rest0, 1)
                            dve.wait_ge(v_ps, n * 2 + l + 1)
                            dve.wait_ge(v_out[p][l], earlier(g.turn * 16))
                            dve.tensor_tensor(
                                vals[p][l][:, :, 0:DH], v_bank[l][:].rearrange("t (h d) -> t h d", d=DH),
                                bv[l][:].unsqueeze(1).broadcast_to([128, G, D]).rearrange("t b (h d) -> t b h d", d=DH),
                                ALU.add).then_inc(v_done, 1)
                    all_groups(dve, body)

                @block.gpsimd
                def _(pool):
                    def body(g):
                        n, p = g.n, g.p
                        for l in range(2):
                            pool.wait_ge(part1, n * 2 + l + 1)
                            pool.tensor_tensor(parts[p][l][:, 2, :], rest[l][:], parts[p][l][:, 1, :], ALU.subtract
                                               ).then_inc(part2, 1)
                        for l in range(2):
                            pool.wait_ge(v_done, n * 2 + l + 1)
                            pool.dma_start(v_ones[l][bass.ds(n * G, G)].rearrange("b t c -> t b c"),
                                           vals[p][l][:].rearrange("t (b h) c -> t b (h c)", b=G)
                                           ).then_inc(v_out[p][l], 16)
                    all_groups(pool, body)
                    for p in range(2):
                        for l in range(2):
                            pool.wait_ge(v_out[p][l], 16 * (NG // 2))

        def project_queries(l, x_src):
            s = lambda name: sem(f"q{l}_{name}")
            x_in, stats_s, mv_s, veps_s, rstd_s, xn_s = [s("x0"), s("x1")], s("stats"), s("mv"), s("veps"), s("rstd"), s("xn")
            turned, kept, q_ps = s("turned"), s("kept"), s("q_ps")
            part0, rest0, part1, part2, q_out = s("part0"), s("rest0"), s("part1"), s("part2"), [s("out0"), s("out1")]
            with ExitStack() as own, nc.Block() as block:
                x_g = [sb(f"qx{l}{p}", [128, G, D], to=own) for p in range(2)]
                xn = [sb(f"qxn{l}{p}", [128, G, D], to=own) for p in range(2)]
                xn_t = [sb(f"qxt{l}{p}", [128, GT], to=own) for p in range(2)]
                stats = [sb(f"qst{l}{p}", [128, G, 6], to=own) for p in range(2)]
                mv = [sb(f"qmv{l}{p}", [128, G, 2], to=own) for p in range(2)]
                veps = [sb(f"qve{l}{p}", [128, G], to=own) for p in range(2)]
                rstd = [sb(f"qrs{l}{p}", [128, G], to=own) for p in range(2)]
                parts = [sb(f"qparts{l}{p}", [128, 3, GT], BF16, own) for p in range(2)]
                rest = [sb(f"qrest{l}{p}", [128, GT], to=own) for p in range(2)]
                t_bank, q_bank = bank[0:2], bank[2:4]

                @block.sync
                def _(sp):
                    def load(g):
                        n, p = g.n, g.p
                        sp.wait_ge(xn_s, earlier(n - 1))
                        sp.dma_start(x_g[p][:], x_src[bass.ds(n * G, G)].rearrange("b t d -> t b d")
                                     ).then_inc(x_in[p], 16)
                    all_groups(sp, load)

                @block.gpsimd
                def _(pool):
                    def body(g):
                        n, p = g.n, g.p
                        rstd_pool(pool, mv[p], veps[p], rstd[p], mv_s, veps_s, rstd_s, n)
                        pool.wait_ge(part1, n + 1)
                        pool.tensor_tensor(parts[p][:, 2, :], rest[p][:], parts[p][:, 1, :], ALU.subtract
                                           ).then_inc(part2, 1)
                    all_groups(pool, body)

                @block.vector
                def _(dve):
                    def body(g):
                        n, p = g.n, g.p
                        dve.wait_ge(turned, earlier(n - 1))
                        layernorm_dve(dve, x_g[p], stats[p], mv[p], xn[p], rstd[p], x_in[p], g.turn * 16 + 16,
                                      stats_s, mv_s, rstd_s, xn_s, n)
                        dve.wait_ge(part0, n + 1)
                        dve.scalar_tensor_tensor(out=rest[p][:], in0=q_bank[p][:], scalar=bq[l][:],
                                                 in1=parts[p][:, 0, :], op0=ALU.add, op1=ALU.subtract
                                                 ).then_inc(rest0, 1)
                    all_groups(dve, body)

                @block.tensor
                def _(pe):
                    def body(g):
                        n, p = g.n, g.p
                        pe.wait_ge(xn_s, n + 1)
                        pe.wait_ge(kept, earlier(n - 1))
                        for t in range(G):
                            mm = pe.transpose(t_bank[p][:, t * T:(t + 1) * T], xn[p][:, t, :], ident[:])
                        mm.then_inc(turned, 1)
                        pe.wait_ge(kept, n + 1)
                        pe.wait_ge(rest0, earlier(n - 1))
                        pe.matmul(q_bank[p][:], wq[l][:], xn_t[p][:], start=True, stop=True).then_inc(q_ps, 1)
                    all_groups(pe, body)

                @block.scalar
                def _(act):
                    def body(g):
                        n, p = g.n, g.p
                        act.wait_ge(turned, n + 1)
                        act.wait_ge(q_ps, earlier(n - 1))
                        act.copy(xn_t[p][:], t_bank[p][:]).then_inc(kept, 1)
                        act.wait_ge(q_ps, n + 1)
                        act.wait_ge(q_out[p], earlier(g.turn * 16))
                        act.activation(parts[p][:, 0, :], q_bank[p][:], ACT.Identity, bias=bq[l][:]).then_inc(part0, 1)
                        act.wait_ge(rest0, n + 1)
                        act.copy(parts[p][:, 1, :], rest[p][:]).then_inc(part1, 1)
                        act.wait_ge(part2, n + 1)
                        act.dma_start(q_parts[:, :, bass.ds(n * GT, GT)].rearrange("c r t -> r c t"),
                                      parts[p][:]).then_inc(q_out[p], 16)
                    all_groups(act, body)
                    for p in range(2):
                        act.wait_ge(q_out[p], 16 * (NG // 2))

        def attention(l, x_src, x_dst):
            causal = l == 1
            scale = DH ** -0.5
            s = lambda name: sem(f"a{l}_{name}")
            qk_in, vx_in, mt_in, x_out = ([s(f"{k}{p}") for p in range(2)] for k in ("qk_in", "vx_in", "mt_in", "x_out"))
            s_ps, max_s, hi_s, split_s = s("s_ps"), s("max"), s("hi"), s("split")
            mt_ps, mt_s = s("mt_ps"), s("mt")
            st_ps, exp_s, masked_s, pv_s = s("st_ps"), s("exp"), s("masked"), s("pv")
            ot_s, oq_ps, rec_s, norm_s, on_ps, on_s = s("ot"), s("oq_ps"), s("rec"), s("norm"), s("on_ps"), s("on")
            y_ps, y_s, biased_s, ones_s, zero_s = s("y_ps"), s("y"), s("biased"), s("ones"), s("zero")
            probs_s = masked_s if causal else exp_s
            QK_IN, VX_IN = 16 * 2 * len(Q_PARTS), 16 * 2
            with ExitStack() as own, nc.Block() as block:
                qq = [sb(f"qq{l}{p}", [ROWS, H, GT], BF16, own) for p in range(2)]
                kk = [sb(f"kk{l}{p}", [ROWS, H, GT], BF16, own) for p in range(2)]
                vv = [sb(f"vv{l}{p}", [128, G, H * VW], to=own) for p in range(2)]
                xx = [sb(f"xx{l}{p}", [128, G, D], to=own) for p in range(2)]
                neg_max = [sb(f"nm{l}{p}", [128, H], to=own) for p in range(2)]
                max_parts = [sb(f"mp{l}{p}", [128, 2 * H], BF16, own) for p in range(2)]
                max_t = [sb(f"mt{l}{p}", [2 * H, T], BF16, own) for p in range(2)]
                probs = [sb(f"pr{l}{c}", [128, C4 * T], to=own) for c in range(NC)]
                o_t = [sb(f"ot{l}{p}", [128, C4 * T], to=own) for p in range(2)]
                rec = [sb(f"rc{l}{p}", [128, H], to=own) for p in range(2)]
                o_n = [sb(f"on{l}{p}", [128, D], to=own) for p in range(2)]
                o_nt = [sb(f"ont{l}{p}", [128, T], to=own) for p in range(2)]
                s_bank, st_bank, o_bank, oq_bank, m_bank = bank[0:2], bank[2:4], bank[4:6], bank[6], bank[7]
                max_bank = m_bank[0:2 * H, 0:T // 2].bitcast(BF16)

                @block.sync
                def _(sp):
                    def load_qk(g):
                        sp.wait_ge(st_ps, earlier((g.n - 1) * G * NC))
                        for side, src, which in ((qq, q_parts, Q_PARTS), (kk, k_parts[l], K_PARTS)):
                            for r, part in enumerate(which):
                                sp.dma_start(side[g.p][r * DH:(r + 1) * DH, :, :],
                                             src[part].rearrange("(h d) t -> d h t", d=DH)[:, :, bass.ds(g.n * GT, GT)]
                                             ).then_inc(qk_in[g.p], 16)

                    def load_vx(g):
                        sp.wait_ge(pv_s, earlier((g.n - 1) * G * NC))
                        sp.dma_start(vv[g.p][:], v_ones[l][bass.ds(g.n * G, G)].rearrange("b t c -> t b c")
                                     ).then_inc(vx_in[g.p], 16)
                        sp.wait_ge(x_out[g.p], earlier(g.turn * 16))
                        sp.dma_start(xx[g.p][:], x_src[bass.ds(g.n * G, G)].rearrange("b t d -> t b d")
                                     ).then_inc(vx_in[g.p], 16)

                    def store(g):
                        sp.wait_ge(y_s, (g.n + 1) * G)
                        sp.dma_start(x_dst[bass.ds(g.n * G, G)].rearrange("b t d -> t b d"), xx[g.p][:]
                                     ).then_inc(x_out[g.p], 16)

                    def place_maxima(q):
                        sp.wait_ge(mt_s, q.m + 1)
                        sp.dma_start(qq[q.g.p][PROD:ROWS, :, q.b * T:(q.b + 1) * T], max_t[q.p][:]
                                     ).then_inc(mt_in[q.p], 16)

                    def body(g, first=False, last=False):
                        for b in range(G):
                            if b == 0 and not last:
                                load_qk(g.after())
                            if b == 1 and not first:
                                store(g.before())
                            if b == 1 and not last:
                                load_vx(g.after())
                            if not (last and b + 2 >= G):
                                place_maxima(Seq(g, b).ahead(2))

                    sp.wait_ge(ones_s, 2)
                    load_qk(FIRST)
                    load_vx(FIRST)
                    for b in range(2):
                        place_maxima(Seq(FIRST, b))
                    body(FIRST, first=True)
                    middle_groups(sp, body)
                    body(LAST, last=True)
                    store(LAST)
                    for p in range(2):
                        sp.wait_ge(x_out[p], 16 * (NG // 2))

                @block.tensor
                def _(pe):
                    def scores(q, c):
                        if c == 0 and q.b == 0:
                            pe.wait_ge(qk_in[q.g.p], (q.g.turn + 1) * QK_IN)
                        pe.wait_ge(max_s, earlier(q.m * NC + c - 1))
                        to, t = s_bank[c % 2], slice(q.b * T, (q.b + 1) * T)
                        if causal:
                            pe.matmul(to[:], future[:], ident4[:].rearrange("p a b -> p (a b)"), start=True, stop=True)
                        for j in range(C4):
                            mm = pe.matmul(to[:, j * T:(j + 1) * T], qq[q.g.p][0:PROD, c * C4 + j, t],
                                           kk[q.g.p][0:PROD, c * C4 + j, t], start=not causal, stop=True,
                                           skip_group_check=causal)
                        mm.then_inc(s_ps, 1)

                    def turn_maxima(q):
                        pe.wait_ge(split_s, q.m + 1)
                        pe.wait_ge(mt_s, earlier(q.m))
                        pe.wait_ge(y_s, earlier(q.m - 2))
                        pe.transpose(max_bank, max_parts[q.p][:], ident4[:, 0, :]).then_inc(mt_ps, 1)

                    def scores_t(q, c):
                        if c == 0:
                            pe.wait_ge(mt_in[q.p], (q.turn + 1) * 16)
                        pe.wait_ge(exp_s, earlier(q.m * NC + c - 1))
                        t = slice(q.b * T, (q.b + 1) * T)
                        for j in range(C4):
                            mm = pe.matmul(st_bank[c % 2][:, j * T:(j + 1) * T], kk[q.g.p][0:ROWS, c * C4 + j, t],
                                           qq[q.g.p][0:ROWS, c * C4 + j, t], start=True, stop=True)
                        mm.then_inc(st_ps, 1)

                    def mix(q, c):
                        if c == 0 and q.b == 0:
                            pe.wait_ge(vx_in[q.g.p], (q.g.turn + 1) * VX_IN)
                        if c == 0:
                            pe.wait_ge(ot_s, earlier(q.m - 1))
                        pe.wait_ge(probs_s, q.m * NC + c + 1)
                        for j in range(C4):
                            h = c * C4 + j
                            mm = pe.matmul(o_bank[q.p][32 * j:32 * j + VW, c * T:(c + 1) * T],
                                           vv[q.g.p][:, q.b, h * VW:(h + 1) * VW], probs[c][:, j * T:(j + 1) * T],
                                           start=True, stop=True)
                        mm.then_inc(pv_s, 1)

                    def turn_output(q):
                        pe.wait_ge(ot_s, q.m + 1)
                        pe.wait_ge(norm_s, earlier(q.m))
                        for c in range(NC):
                            mm = pe.transpose(oq_bank[:, c * T:(c + 1) * T], o_t[q.p][:, c * T:(c + 1) * T], ident[:])
                        mm.then_inc(oq_ps, 1)

                    def turn_normalised(q):
                        pe.wait_ge(norm_s, q.m + 1)
                        pe.wait_ge(mt_s, min(q.m + 3, B) if isinstance(q.m, int) else q.m + 3)
                        pe.transpose(m_bank[:, 0:T], o_n[q.p][:], ident[:]).then_inc(on_ps, 1)

                    def project(q):
                        pe.wait_ge(on_s, q.m + 1)
                        pe.matmul(m_bank[:, 0:D], o_nt[q.p][:], wo[l][:], start=True, stop=True).then_inc(y_ps, 1)

                    def body(g, first=False, last=False):
                        for b in range(G):
                            q = Seq(g, b)
                            past = None if first and b == 0 else q.ahead(-1)
                            to_come = None if last and b + 2 >= G else q.ahead(2)
                            for c in range(NC):
                                scores_t(q, c)
                                if to_come:
                                    scores(to_come, c)
                                if c:
                                    mix(q, c - 1)
                                elif past:
                                    mix(past, NC - 1)
                                if c == 1 and past:
                                    turn_output(past)
                                if c == 2 and past:
                                    turn_normalised(past)
                                if c == 3 and past:
                                    project(past)
                            if to_come:
                                turn_maxima(to_come)

                    pe.wait_ge(zero_s, 1)
                    for p in range(2):
                        pe.matmul(o_bank[p][:], probs[0][:, 0:128], probs[0][:], start=True, stop=True)
                    for b in range(2):
                        for c in range(NC):
                            scores(Seq(FIRST, b), c)
                        turn_maxima(Seq(FIRST, b))
                    body(FIRST, first=True)
                    middle_groups(pe, body)
                    body(LAST, last=True)
                    end = Seq(LAST, G - 1)
                    mix(end, NC - 1)
                    turn_output(end)
                    turn_normalised(end)
                    project(end)

                @block.scalar
                def _(act):
                    def exponential(q, c):
                        act.wait_ge(st_ps, q.m * NC + c + 1)
                        act.wait_ge(pv_s, earlier((q.m - 1) * NC + c + 1))
                        act.activation(probs[c][:], st_bank[c % 2][:], ACT.Exp, scale=scale).then_inc(exp_s, 1)

                    def keep_output(q):
                        act.wait_ge(pv_s, (q.m + 1) * NC)
                        act.wait_ge(oq_ps, earlier(q.m - 1))
                        act.copy(o_t[q.p][:], o_bank[q.p][:]).then_inc(ot_s, 1)

                    def keep_normalised(q):
                        act.wait_ge(on_ps, q.m + 1)
                        act.wait_ge(y_ps, earlier(q.m - 1))
                        act.copy(o_nt[q.p][:], m_bank[:, 0:T]).then_inc(on_s, 1)

                    def keep_maxima(q):
                        act.wait_ge(mt_ps, q.m + 1)
                        act.wait_ge(mt_in[q.p], earlier(q.turn * 16))
                        act.copy(max_t[q.p][:], max_bank).then_inc(mt_s, 1)

                    def body(g, first=False, last=False):
                        for b in range(G):
                            q = Seq(g, b)
                            past = None if first and b == 0 else q.ahead(-1)
                            exponential(q, 0)
                            if past:
                                keep_output(past)
                            exponential(q, 1)
                            exponential(q, 2)
                            if past:
                                keep_normalised(past)
                            exponential(q, 3)
                            if not (last and b + 2 >= G):
                                keep_maxima(q.ahead(2))

                    for b in range(2):
                        keep_maxima(Seq(FIRST, b))
                    body(FIRST, first=True)
                    middle_groups(act, body)
                    body(LAST, last=True)
                    keep_output(Seq(LAST, G - 1))
                    keep_normalised(Seq(LAST, G - 1))

                @block.vector
                def _(dve):
                    def reduce_chunk(q, c):
                        dve.wait_ge(s_ps, q.m * NC + c + 1)
                        if c == 0:
                            dve.wait_ge(split_s, earlier(q.m - 1))
                        dve.tensor_reduce(neg_max[q.p][:, c * C4:(c + 1) * C4],
                                          s_bank[c % 2][:].rearrange("q (h k) -> q h k", h=C4), AX_X, ALU.max,
                                          negate=True).then_inc(max_s, 1)

                    def cut_maxima(q):
                        dve.wait_ge(max_s, (q.m + 1) * NC)
                        dve.wait_ge(mt_ps, earlier(q.m - 1))
                        dve.tensor_copy(max_parts[q.p][:, 0:H], neg_max[q.p][:]).then_inc(hi_s, 1)
                        dve.wait_ge(hi_s, q.m + 1)
                        dve.tensor_tensor(max_parts[q.p][:, H:2 * H], neg_max[q.p][:], max_parts[q.p][:, 0:H],
                                          ALU.subtract).then_inc(split_s, 1)

                    def normalise(q):
                        view = oq_bank[:].rearrange("q (h w) -> q h w", w=32)
                        dve.wait_ge(oq_ps, q.m + 1)
                        dve.reciprocal(rec[q.p][:].unsqueeze(2), view[:, :, DH:DH + 1]).then_inc(rec_s, 1)
                        dve.wait_ge(rec_s, q.m + 1)
                        dve.wait_ge(on_ps, earlier(q.m - 1))
                        dve.tensor_tensor(o_n[q.p][:].rearrange("q (h d) -> q h d", d=DH), view[:, :, 0:DH],
                                          rec[q.p][:].unsqueeze(2).broadcast_to([128, H, DH]), ALU.mult
                                          ).then_inc(norm_s, 1)

                    def add(q):
                        dve.wait_ge(y_ps, q.m + 1)
                        dve.wait_ge(biased_s, q.g.n + 1)
                        rows = xx[q.g.p][:, q.b, :]
                        dve.tensor_tensor(rows, m_bank[:, 0:D], rows, ALU.add).then_inc(y_s, 1)

                    def body(g, first=False, last=False):
                        for b in range(G):
                            q = Seq(g, b)
                            past = None if first and b == 0 else q.ahead(-1)
                            to_come = None if last and b + 2 >= G else q.ahead(2)
                            if to_come:
                                reduce_chunk(to_come, 0)
                                reduce_chunk(to_come, 1)
                            if past:
                                normalise(past)
                            if to_come:
                                reduce_chunk(to_come, 2)
                                reduce_chunk(to_come, 3)
                                cut_maxima(to_come)
                            if past:
                                add(past)

                    for p in range(2):
                        dve.memset(kk[p][32:ROWS, :, :], 1.0).then_inc(ones_s, 1)
                    dve.memset(probs[0][:], 0.0).then_inc(zero_s, 1)
                    for b in range(2):
                        for c in range(NC):
                            reduce_chunk(Seq(FIRST, b), c)
                        cut_maxima(Seq(FIRST, b))
                    body(FIRST, first=True)
                    middle_groups(dve, body)
                    body(LAST, last=True)
                    normalise(Seq(LAST, G - 1))
                    add(Seq(LAST, G - 1))

                @block.gpsimd
                def _(pool):
                    def bias(g):
                        pool.wait_ge(vx_in[g.p], (g.turn + 1) * VX_IN)
                        pool.tensor_tensor(xx[g.p][:], xx[g.p][:], bo[l][:].unsqueeze(1).broadcast_to([128, G, D]),
                                           ALU.add).then_inc(biased_s, 1)

                    def mask(q, c):
                        pool.wait_ge(exp_s, q.m * NC + c + 1)
                        pool.tensor_tensor(pool_cell[:, c:c + 1], epsilon[:, 0:1], epsilon[:, 0:1], ALU.mult)
                        pool.affine_select(out=probs[c][:], in_=probs[c][:], compare_op=ALU.is_ge, fill=0.0, base=0,
                                           pattern=[[0, C4], [1, T]], channel_multiplier=-1).then_inc(masked_s, 1)

                    def body(g):
                        bias(g)
                        if causal:
                            for b in range(G):
                                for c in range(NC):
                                    mask(Seq(g, b), c)
                    all_groups(pool, body)

        def experts0(x_src, x_dst):
            s = lambda name: sem(f"e0_{name}")
            x_in, x_out = ([s(f"{k}{p}") for p in range(2)] for k in ("x_in", "x_out"))
            stats_s, mv_s, veps_s, rstd_s, xn_s, sum_s = s("stats"), s("mv"), s("veps"), s("rstd"), s("xn"), s("sum")
            turned, kept, sc_ps = s("turned"), s("kept"), s("sc_ps")
            top_s, tie_s, rank_s, best_s, hot_s = s("top"), s("tie"), s("rank"), s("best"), s("hot")
            hot_ps, chosen_s, y_ps, y_s, z_ps, z_s = s("hot_ps"), s("chosen"), s("y_ps"), s("y"), s("z_ps"), s("z")
            with ExitStack() as own, nc.Block() as block:
                two = lambda name, shape, dt=F32: [sb(f"e0{name}{p}", shape, dt, own) for p in range(2)]
                x_g, xn, xn_t = two("x", [128, G, D]), two("xn", [128, G, D]), two("xt", [128, GT])
                stats, mv, veps, rstd = two("st", [128, G, 6]), two("mv", [128, G, 2]), two("ve", [128, G]), two("rs", [128, G])
                top, best = two("top", [128, G]), two("best", [128, G])
                tie, ranked = two("tie", [128, G, E]), two("rk", [128, G, E])
                hot = two("hot", [128, G, E], BF16)
                chosen, y_t = two("ch", [128, GT]), two("y", [128, GT])
                t_bank, sc_bank, hot_bank, y_bank, z_bank = bank[0], bank[1], bank[2:4], bank[4:6], bank[6]

                @block.sync
                def _(sp):
                    def load(g):
                        sp.wait_ge(x_out[g.p], earlier(g.turn * 16))
                        sp.dma_start(x_g[g.p][:], x_src[bass.ds(g.n * G, G)].rearrange("b t d -> t b d")
                                     ).then_inc(x_in[g.p], 16)

                    def store(g):
                        sp.wait_ge(z_s, g.n + 1)
                        sp.dma_start(x_dst[bass.ds(g.n * G, G)].rearrange("b t d -> t b d"), x_g[g.p][:]
                                     ).then_inc(x_out[g.p], 16)

                    def body(g):
                        store(g.before())
                        load(g.after())
                    load(FIRST)
                    load(FIRST.after())
                    middle_groups(sp, body)
                    store(LAST.before())
                    store(LAST)
                    for p in range(2):
                        sp.wait_ge(x_out[p], 16 * (NG // 2))

                @block.gpsimd
                def _(pool):
                    def body(g):
                        rstd_pool(pool, mv[g.p], veps[g.p], rstd[g.p], mv_s, veps_s, rstd_s, g.n)
                        pool.wait_ge(xn_s, g.n + 1)
                        pool.tensor_tensor(x_g[g.p][:], x_g[g.p][:], xn[g.p][:], ALU.add).then_inc(sum_s, 1)
                    all_groups(pool, body)

                @block.vector
                def _(dve):
                    def normalise(g):
                        dve.wait_ge(turned, earlier(g.n - 1))
                        dve.wait_ge(sum_s, earlier(g.n - 1))
                        layernorm_dve(dve, x_g[g.p], stats[g.p], mv[g.p], xn[g.p], rstd[g.p], x_in[g.p],
                                      g.turn * 16 + 16, stats_s, mv_s, rstd_s, xn_s, g.n)

                    def route(g):
                        view, p = sc_bank[:, 0:G * E].rearrange("t (g e) -> t g e", e=E), g.p
                        dve.wait_ge(sc_ps, g.n + 1)
                        dve.tensor_reduce(top[p][:], view, AX_X, ALU.max).then_inc(top_s, 1)
                        dve.wait_ge(top_s, g.n + 1)
                        dve.tensor_tensor(tie[p][:], view, top[p][:].unsqueeze(2).broadcast_to([128, G, E]), ALU.is_ge
                                          ).then_inc(tie_s, 1)
                        dve.wait_ge(tie_s, g.n + 1)
                        dve.tensor_tensor(ranked[p][:], tie[p][:], rank[:], ALU.mult).then_inc(rank_s, 1)
                        dve.wait_ge(rank_s, g.n + 1)
                        dve.tensor_reduce(best[p][:], ranked[p][:], AX_X, ALU.max).then_inc(best_s, 1)
                        dve.wait_ge(best_s, g.n + 1)
                        dve.wait_ge(hot_ps, earlier((g.n - 1) * E))
                        dve.tensor_tensor(hot[p][:], ranked[p][:], best[p][:].unsqueeze(2).broadcast_to([128, G, E]),
                                          ALU.is_equal).then_inc(hot_s, 1)

                    def choose(g, e):
                        k = g.n * E + e
                        dve.wait_ge(hot_ps, k + 1)
                        dve.wait_ge(y_ps, earlier(k - 1))
                        dve.tensor_tensor(chosen[e % 2][:], hot_bank[e % 2][:], xn_t[g.p][:], ALU.mult).then_inc(chosen_s, 1)

                    def add(g):
                        dve.wait_ge(z_ps, g.n + 1)
                        dve.wait_ge(sum_s, g.n + 1)
                        dve.tensor_tensor(x_g[g.p][:], z_bank[:].rearrange("t (g d) -> t g d", g=G), x_g[g.p][:], ALU.add
                                          ).then_inc(z_s, 1)

                    def back(g, ahead):
                        for e in range(E):
                            choose(g, e)
                            if e == 1 and ahead:
                                normalise(ahead)
                            if e == 5 and ahead:
                                route(ahead)
                        add(g)

                    normalise(FIRST)
                    route(FIRST)
                    back(FIRST, FIRST.after())
                    middle_groups(dve, lambda g: back(g, g.after()))
                    back(LAST, None)

                @block.tensor
                def _(pe):
                    def turn(g):
                        pe.wait_ge(xn_s, g.n + 1)
                        pe.wait_ge(kept, earlier(g.n))
                        for t in range(G):
                            mm = pe.transpose(t_bank[:, t * T:(t + 1) * T], xn[g.p][:, t, :], ident[:])
                        mm.then_inc(turned, 1)

                    def score(g):
                        pe.wait_ge(kept, g.n + 1)
                        pe.wait_ge(tie_s, earlier(g.n))
                        for t in range(G):
                            mm = pe.matmul(sc_bank[:, t * E:(t + 1) * E], xn_t[g.p][:, t * T:(t + 1) * T], gate0_w[:],
                                           start=True, stop=True)
                        mm.then_inc(sc_ps, 1)

                    def spread(g, e):
                        k = g.n * E + e
                        if e == 0:
                            pe.wait_ge(hot_s, g.n + 1)
                        pe.wait_ge(chosen_s, earlier(k - 1))
                        for t in range(G):
                            mm = pe.matmul(hot_bank[e % 2][:, t * T:(t + 1) * T],
                                           hot[g.p][:, t, e:e + 1].broadcast_to([128, 128]), ident4[:, 0, :],
                                           start=True, stop=True)
                        mm.then_inc(hot_ps, 1)

                    def expert(g, e):
                        k = g.n * E + e
                        pe.wait_ge(chosen_s, k + 1)
                        if e == 0:
                            pe.wait_ge(y_s, earlier(g.n - 1))
                        pe.matmul(y_bank[g.p][:], expert0_w[:, e, :], chosen[e % 2][:], start=(e == 0), stop=(e == E - 1)
                                  ).then_inc(y_ps, 1)

                    def turn_back(g):
                        pe.wait_ge(y_s, g.n + 1)
                        pe.wait_ge(z_s, earlier(g.n))
                        for t in range(G):
                            mm = pe.transpose(z_bank[:, t * T:(t + 1) * T], y_t[g.p][:, t * T:(t + 1) * T], ident[:])
                        mm.then_inc(z_ps, 1)

                    def back(g, ahead):
                        spread(g, 0)
                        for e in range(E):
                            if e + 1 < E:
                                spread(g, e + 1)
                            expert(g, e)
                            if e == 2 and ahead:
                                turn(ahead)
                            if e == 3 and ahead:
                                score(ahead)
                        turn_back(g)

                    turn(FIRST)
                    score(FIRST)
                    back(FIRST, FIRST.after())
                    middle_groups(pe, lambda g: back(g, g.after()))
                    back(LAST, None)

                @block.scalar
                def _(act):
                    def keep_turned(g):
                        act.wait_ge(turned, g.n + 1)
                        act.wait_ge(sc_ps, earlier(g.n - 1))
                        act.wait_ge(chosen_s, earlier((g.n - 1) * E))
                        act.copy(xn_t[g.p][:], t_bank[:]).then_inc(kept, 1)

                    def keep_sum(g):
                        act.wait_ge(y_ps, (g.n + 1) * E)
                        act.wait_ge(z_ps, earlier(g.n - 1))
                        act.copy(y_t[g.p][:], y_bank[g.p][:]).then_inc(y_s, 1)

                    keep_turned(FIRST)

                    def body(g):
                        keep_turned(g.after())
                        keep_sum(g)
                    body(FIRST)
                    middle_groups(act, body)
                    keep_sum(LAST)

        def experts1(x_src, x_dst):
            s = lambda name: sem(f"e1_{name}")
            x_in, x_out = ([s(f"{k}{p}") for p in range(2)] for k in ("x_in", "x_out"))
            w_in = s("w_in")
            stats_s, mv_s, veps_s, rstd_s, xn_s = s("stats"), s("mv"), s("veps"), s("rstd"), s("xn")
            turned, kept, sc_ps, small, exp_s = s("turned"), s("kept"), s("sc_ps"), s("small"), s("exp")
            weights_s, gate_ps, up_ps, silu_s, act_s, down_ps, sum_s = (
                s(k) for k in ("weights", "gate_ps", "up_ps", "silu", "act", "down_ps", "sum"))
            NF = len(FCH)
            STEPS = 19
            with ExitStack() as own, nc.Block() as block:
                two = lambda name, shape, dt=F32: [sb(f"e1{name}{p}", shape, dt, own) for p in range(2)]
                gate_w, up_w = sb("gate_w", [128, E, F], to=own), sb("up_w", [128, E, F], to=own)
                down_w = sb("down_w", [128, E, NF, D], to=own)
                router_w = sb("router_w", [128, E], to=own)
                x_g, xn, xn_t = two("x", [128, G, D]), two("xn", [128, G, D]), two("xt", [128, GT])
                stats, mv, veps, rstd = two("st", [128, G, 6]), two("mv", [128, G, 2]), two("ve", [128, G]), two("rs", [128, G])
                shifted, probs = two("sh", [128, G, E]), two("pr", [128, G, E])
                work = sb("e1work", [128, 6, G, E], to=own)
                col = sb("e1col", [128, 8, G], to=own)
                weights = two("w", [128, G, E])
                silu = two("si", [128, GT])
                acts = [[sb(f"e1act{p}{f}", [128, GT], to=own) for f in range(NF)] for p in range(2)]
                t_bank, sc_bank, gate_bank, up_bank, down_bank = bank[0], bank[1], bank[2:4], bank[4:6], bank[6:8]

                @block.sync
                def _(sp):
                    def load(g):
                        sp.wait_ge(x_out[g.p], earlier(g.turn * 16))
                        sp.dma_start(x_g[g.p][:], x_src[bass.ds(g.n * G, G)].rearrange("b t d -> t b d")
                                     ).then_inc(x_in[g.p], 16)

                    def store(g):
                        sp.wait_ge(sum_s, (g.n + 1) * E * G)
                        sp.dma_start(x_dst[bass.ds(g.n * G, G)].rearrange("b t d -> t b d"), x_g[g.p][:]
                                     ).then_inc(x_out[g.p], 16)

                    def body(g):
                        store(g.before())
                        load(g.after())
                    load(FIRST)
                    sp.dma_start(router_w[:], a["L1_ffn_router_w"]).then_inc(w_in, 16)
                    sp.dma_start(gate_w[:], a["L1_ffn_gate_proj"].rearrange("e d f -> d e f")).then_inc(w_in, 16)
                    sp.dma_start(up_w[:], a["L1_ffn_up_proj"].rearrange("e d f -> d e f")).then_inc(w_in, 16)
                    for f, (f0, fn) in enumerate(FCH):
                        sp.dma_start(down_w[0:fn, :, f, :],
                                     a["L1_ffn_down_proj"][:, f0:f0 + fn, :].rearrange("e f d -> f e d")).then_inc(w_in, 16)
                    load(FIRST.after())
                    middle_groups(sp, body)
                    store(LAST.before())
                    store(LAST)
                    for p in range(2):
                        sp.wait_ge(x_out[p], 16 * (NG // 2))

                @block.gpsimd
                def _(pool):
                    all_groups(pool, lambda g: rstd_pool(pool, mv[g.p], veps[g.p], rstd[g.p], mv_s, veps_s, rstd_s, g.n))

                @block.vector
                def _(dve):
                    def normalise(g):
                        dve.wait_ge(turned, earlier(g.n - 1))
                        layernorm_dve(dve, x_g[g.p], stats[g.p], mv[g.p], xn[g.p], rstd[g.p], x_in[g.p],
                                      g.turn * 16 + 16, stats_s, mv_s, rstd_s, xn_s, g.n)

                    def wide(column):
                        return col[:, column, :].unsqueeze(2).broadcast_to([128, G, E])

                    def route(g):
                        view, p = sc_bank[:, 0:G * E].rearrange("t (g e) -> t g e", e=E), g.p
                        done = [g.n * STEPS]

                        def step(ins):
                            ins.then_inc(small, 1)
                            done[0] = done[0] + 1
                            dve.wait_ge(small, done[0])

                        dve.wait_ge(sc_ps, g.n + 1)
                        step(dve.tensor_reduce(col[:, 0, :], view, AX_X, ALU.max))
                        step(dve.tensor_tensor(shifted[p][:], view, wide(0), ALU.subtract))
                        dve.wait_ge(exp_s, g.n + 1)
                        step(dve.tensor_reduce(col[:, 1, :], probs[p][:], AX_X, ALU.add))
                        step(dve.reciprocal(col[:, 2, :], col[:, 1, :]))
                        step(dve.tensor_tensor(work[:, 0], probs[p][:], wide(2), ALU.mult))
                        for k in range(2):
                            left = work[:, 0] if k == 0 else work[:, 4]
                            step(dve.tensor_reduce(col[:, 3 + k, :], left, AX_X, ALU.max))
                            step(dve.tensor_tensor(work[:, 1], left, wide(3 + k), ALU.is_ge))
                            step(dve.tensor_tensor(work[:, 1], work[:, 1], rank[:], ALU.mult))
                            step(dve.tensor_reduce(col[:, 5, :], work[:, 1], AX_X, ALU.max))
                            dve.tensor_tensor(work[:, 2 + k], work[:, 1], wide(5), ALU.is_equal)
                            if k == 0:
                                step(dve.tensor_tensor(work[:, 5], work[:, 1], wide(5), ALU.is_equal))
                                step(dve.scalar_tensor_tensor(out=work[:, 4], in0=work[:, 5], scalar=-2.0, in1=work[:, 0],
                                                              op0=ALU.mult, op1=ALU.add))
                        step(dve.tensor_tensor(col[:, 6, :], col[:, 3, :], col[:, 4, :], ALU.add))
                        step(dve.reciprocal(col[:, 7, :], col[:, 6, :]))
                        step(dve.tensor_tensor(work[:, 5], work[:, 2], work[:, 3], ALU.add))
                        step(dve.tensor_tensor(work[:, 1], work[:, 5], work[:, 0], ALU.mult))
                        dve.wait_ge(sum_s, earlier((g.n - 1) * E * G))
                        dve.tensor_tensor(weights[p][:], work[:, 1], wide(7), ALU.mult).then_inc(weights_s, 1)

                    def activate(g, e, f):
                        k = (g.n * E + e) * NF + f
                        fn = FCH[f][1]
                        dve.wait_ge(silu_s, k + 1)
                        dve.wait_ge(up_ps, k + 1)
                        dve.wait_ge(down_ps, earlier(g.n * E + e - 1))
                        dve.tensor_tensor(acts[e % 2][f][0:fn, :], up_bank[k_parity(e, f)][0:fn, :], silu[k_parity(e, f)][0:fn, :],
                                          ALU.mult).then_inc(act_s, 1)

                    def add(g, e):
                        if e == 0:
                            dve.wait_ge(weights_s, g.n + 1)
                        dve.wait_ge(down_ps, g.n * E + e + 1)
                        for t in range(G):
                            if e:
                                dve.wait_ge(sum_s, earlier((g.n * E + e - 1) * G + t + 1))
                            dve.scalar_tensor_tensor(out=x_g[g.p][:, t, :], in0=down_bank[e % 2][:, t * D:(t + 1) * D],
                                                     scalar=weights[g.p][:, t, e:e + 1], in1=x_g[g.p][:, t, :],
                                                     op0=ALU.mult, op1=ALU.add).then_inc(sum_s, 1)

                    def back(g, ahead):
                        for e in range(E):
                            for f in range(NF):
                                activate(g, e, f)
                            if e:
                                add(g, e - 1)
                            if e == 1 and ahead:
                                normalise(ahead)
                            if e == 4 and ahead:
                                route(ahead)
                        add(g, E - 1)

                    normalise(FIRST)
                    route(FIRST)
                    back(FIRST, FIRST.after())
                    middle_groups(dve, lambda g: back(g, g.after()))
                    back(LAST, None)

                @block.tensor
                def _(pe):
                    def turn(g):
                        pe.wait_ge(xn_s, g.n + 1)
                        pe.wait_ge(kept, earlier(g.n))
                        for t in range(G):
                            mm = pe.transpose(t_bank[:, t * T:(t + 1) * T], xn[g.p][:, t, :], ident[:])
                        mm.then_inc(turned, 1)

                    def score(g):
                        pe.wait_ge(kept, g.n + 1)
                        for t in range(G):
                            mm = pe.matmul(sc_bank[:, t * E:(t + 1) * E], xn_t[g.p][:, t * T:(t + 1) * T], router_w[:],
                                           start=True, stop=True)
                        mm.then_inc(sc_ps, 1)

                    def gate_up(g, e, f):
                        k = (g.n * E + e) * NF + f
                        f0, fn = FCH[f]
                        i = k_parity(e, f)
                        pe.wait_ge(silu_s, earlier(k - 1))
                        pe.matmul(gate_bank[i][0:fn, :], gate_w[:, e, f0:f0 + fn], xn_t[g.p][:], start=True, stop=True
                                  ).then_inc(gate_ps, 1)
                        pe.wait_ge(act_s, earlier(k - 1))
                        pe.matmul(up_bank[i][0:fn, :], up_w[:, e, f0:f0 + fn], xn_t[g.p][:], start=True, stop=True
                                  ).then_inc(up_ps, 1)

                    def down(g, e):
                        pe.wait_ge(act_s, (g.n * E + e + 1) * NF)
                        pe.wait_ge(sum_s, earlier((g.n * E + e - 1) * G))
                        for t in range(G):
                            for f, (f0, fn) in enumerate(FCH):
                                mm = pe.matmul(down_bank[e % 2][:, t * D:(t + 1) * D], acts[e % 2][f][0:fn, t * T:(t + 1) * T],
                                               down_w[0:fn, e, f, :], start=(f == 0), stop=(f == NF - 1))
                        mm.then_inc(down_ps, 1)

                    def back(g, ahead):
                        for e in range(E):
                            for f in range(NF):
                                gate_up(g, e, f)
                                if f == 0 and e:
                                    down(g, e - 1)
                            if e == 2 and ahead:
                                turn(ahead)
                            if e == 3 and ahead:
                                score(ahead)
                        down(g, E - 1)

                    pe.wait_ge(w_in, 16 * (3 + NF))
                    turn(FIRST)
                    score(FIRST)
                    back(FIRST, FIRST.after())
                    middle_groups(pe, lambda g: back(g, g.after()))
                    back(LAST, None)

                @block.scalar
                def _(act):
                    def keep_turned(g):
                        act.wait_ge(turned, g.n + 1)
                        act.wait_ge(sc_ps, earlier(g.n - 1))
                        act.wait_ge(up_ps, earlier((g.n - 1) * E * NF))
                        act.copy(xn_t[g.p][:], t_bank[:]).then_inc(kept, 1)

                    def exponential(g):
                        act.wait_ge(small, g.n * STEPS + 2)
                        act.activation(probs[g.p][:], shifted[g.p][:], ACT.Exp).then_inc(exp_s, 1)

                    def gate(g, e, f):
                        k = (g.n * E + e) * NF + f
                        fn = FCH[f][1]
                        i = k_parity(e, f)
                        act.wait_ge(gate_ps, k + 1)
                        act.wait_ge(act_s, earlier(k - 1))
                        act.activation(silu[i][0:fn, :], gate_bank[i][0:fn, :], ACT.Silu).then_inc(silu_s, 1)

                    def back(g, ahead):
                        for e in range(E):
                            for f in range(NF):
                                gate(g, e, f)
                            if e == 2 and ahead:
                                keep_turned(ahead)
                            if e == 4 and ahead:
                                exponential(ahead)

                    keep_turned(FIRST)
                    exponential(FIRST)
                    back(FIRST, FIRST.after())
                    middle_groups(act, lambda g: back(g, g.after()))
                    back(LAST, None)

        prepare()
        project_keys_values()
        project_queries(0, a["x"])
        attention(0, a["x"], x_attn0)
        experts0(x_attn0, x_ffn0)
        clear_semaphores()
        project_queries(1, x_ffn0)
        attention(1, x_ffn0, x_attn1)
        experts1(x_attn1, out)


INS = ["x", "ctx_1024",
       "L0_xattn_w_q", "L0_xattn_b_q", "L0_xattn_w_k", "L0_xattn_b_k", "L0_xattn_w_v", "L0_xattn_b_v",
       "L0_xattn_w_o", "L0_xattn_b_o", "L0_ffn_gate_w", "L0_ffn_expert_w",
       "L1_xattn_Wq", "L1_xattn_bq", "L1_xattn_Wk", "L1_xattn_bk", "L1_xattn_Wv", "L1_xattn_bv",
       "L1_xattn_Wo", "L1_xattn_bo", "L1_ffn_router_w", "L1_ffn_gate_proj", "L1_ffn_up_proj", "L1_ffn_down_proj"]


def kernel(**inputs):
    import numpy as np
    import concourse.bacc as bacc
    from concourse.bass_utils import run_bass_kernel_spmd

    nc = bacc.Bacc("TRN2", target_bir_lowering=False, num_devices=1)
    arrays, aps = {}, {}
    for name in INS:
        arrays[name] = np.ascontiguousarray(inputs[name])
        aps[name] = nc.dram_tensor(name, arrays[name].shape, mybir.dt.from_np(arrays[name].dtype), kind="ExternalInput").ap()
    out = nc.dram_tensor("out", (B, T, D), F32, kind="ExternalOutput").ap()
    build(nc, aps, out)
    ran = run_bass_kernel_spmd(nc, [arrays], core_ids=[0])
    return ran.results[0]["out"]
```

```python
from contextlib import ExitStack

import concourse.bass as bass
from concourse import mybir

ALU = mybir.AluOpType
ACT = mybir.ActivationFunctionType
AX_X = mybir.AxisListType.X
F32 = mybir.dt.float32
BF16 = mybir.dt.bfloat16

B = 32
T = 128
D = 128
H = 16
DH = D // H
G = 4
NG = B // G
GT = G * T
VW = DH + 1
Q_PARTS = (0, 0, 0, 1, 1, 2)
K_PARTS = (0, 1, 2, 0, 1, 0)
PROD = DH * len(Q_PARTS)
ROWS = PROD + 2
C4 = 4
NC = H // C4
E = 8
F = 352
FCH = ((0, 128), (128, 128), (256, 96))
NEG = -1e30
EPS = 1e-5


def earlier(count):
    return max(count, 0) if isinstance(count, int) else count


class Group:

    def __init__(self, turn, p):
        self.turn, self.p, self.n = turn, p, turn * 2 + p

    def after(self):
        return Group(self.turn, 1) if self.p == 0 else Group(self.turn + 1, 0)

    def before(self):
        return Group(self.turn, 0) if self.p == 1 else Group(self.turn - 1, 1)


class Seq:

    def __init__(self, g, b):
        self.g, self.b, self.m, self.p, self.turn = g, b, g.n * G + b, b % 2, g.n * (G // 2) + b // 2

    def ahead(self, k):
        if 0 <= self.b + k < G:
            return Seq(self.g, self.b + k)
        return Seq(self.g.after(), self.b + k - G) if k > 0 else Seq(self.g.before(), self.b + k + G)


def k_parity(e, f):
    return (e * len(FCH) + f) % 2


def all_groups(eng, body):
    body(Group(0, 0))
    body(Group(0, 1))
    with eng.Fori(1, NG // 2) as i:
        body(Group(i, 0))
        body(Group(i, 1))


def middle_groups(eng, body):
    body(Group(0, 1))
    body(Group(1, 0))
    with eng.Fori(1, NG // 2 - 1) as i:
        body(Group(i, 1))
        body(Group(i + 1, 0))


FIRST, LAST = Group(0, 0), Group(NG // 2 - 1, 1)


def build(nc, a, out):
    ctx = ExitStack()

    in_use = []
    def sem(name):
        in_use.append(nc.alloc_semaphore(name=name))
        return in_use[-1]

    def clear_semaphores():
        nc.clear_and_free_semaphores(in_use)
        nc.all_engine_barrier()
        in_use.clear()

    def scratch(name, shape, dt):
        return nc.dram_tensor(name, shape, dt, kind="Internal").ap()

    with ctx:
        def sb(name, shape, dt=F32, to=ctx):
            return to.enter_context(nc.sbuf_tensor(name, shape, dt))

        bank = [ctx.enter_context(nc.psum_tensor(f"bank{i}", [128, 512], F32)) for i in range(8)]

        q_parts = scratch("q_parts", (3, D, B * T), BF16)
        k_parts = scratch("k_parts", (2, 3, D, B * T), BF16)
        v_ones = scratch("v_ones", (2, B, T, H * VW), F32)
        x_attn0 = scratch("x_attn0", (B, T, D), F32)
        x_ffn0 = scratch("x_ffn0", (B, T, D), F32)
        x_attn1 = scratch("x_attn1", (B, T, D), F32)

        ident = sb("ident", [128, 128])
        ident4 = sb("ident4", [128, 4, 128], BF16)
        future = sb("future", [128, 128], BF16)
        wq = [sb(f"wq{l}", [128, D]) for l in range(2)]
        wk = [sb(f"wk{l}", [128, D]) for l in range(2)]
        wv = [sb(f"wv{l}", [128, D]) for l in range(2)]
        wo = [sb(f"wo{l}", [128, D]) for l in range(2)]
        bq = [sb(f"bq{l}", [128, 1]) for l in range(2)]
        bk = [sb(f"bk{l}", [128, 1]) for l in range(2)]
        bv = [sb(f"bv{l}", [128, D]) for l in range(2)]
        bo = [sb(f"bo{l}", [128, D]) for l in range(2)]
        expert0_w = sb("expert0_w", [128, E, D])
        gate0_w = sb("gate0_w", [128, E])
        minus_half, epsilon = sb("minus_half", [128, G]), sb("epsilon", [128, G])
        pool_cell, dve_cell = sb("pool_cell", [128, NC]), sb("dve_cell", [128, 1])
        rank = sb("expert_rank", [128, G, E])

        def prepare():
            loaded, zeroed, ones_set = sem("p_loaded"), sem("p_zeroed"), sem("p_ones")
            turned, kept, made = sem("p_turned"), sem("p_kept"), sem("p_made")
            with ExitStack() as own, nc.Block() as block:
                w_raw = [sb(f"w_raw{i}", [128, D], to=own) for i in range(4)]
                e_raw = sb("e_raw", [128, E, D], to=own)
                g_raw = sb("g_raw", [E, D], to=own)
                loads = [(w_raw[i][:], a[n]) for i, n in enumerate(
                    ("L0_xattn_w_q", "L0_xattn_w_k", "L0_xattn_w_v", "L0_xattn_w_o"))]
                loads += [(g_raw[:], a["L0_ffn_gate_w"]),
                          (e_raw[:], a["L0_ffn_expert_w"].rearrange("e f h -> f e h")),
                          (wq[1][:], a["L1_xattn_Wq"]), (wk[1][:], a["L1_xattn_Wk"]),
                          (wv[1][:], a["L1_xattn_Wv"]), (wo[1][:], a["L1_xattn_Wo"])]
                for l, pre in enumerate(("L0_xattn_b_", "L1_xattn_b")):
                    loads += [(bq[l][:], a[pre + "q"].unsqueeze(1)), (bk[l][:], a[pre + "k"].unsqueeze(1)),
                              (bv[l][:], a[pre + "v"].partition_broadcast(128)),
                              (bo[l][:], a[pre + "o"].partition_broadcast(128))]

                @block.sync
                def _(sp):
                    for to, src in loads:
                        sp.dma_start(to, src).then_inc(loaded, 16)
                    sp.wait_ge(loaded, 16 * len(loads))

                @block.gpsimd
                def _(pool):
                    pool.memset(ident[:], 0.0).then_inc(zeroed, 1)
                    pool.memset(ident4[:], 0.0).then_inc(zeroed, 1)
                    pool.memset(future[:], 0.0).then_inc(zeroed, 1)
                    pool.memset(minus_half[:], -0.5).then_inc(made, 1)
                    pool.memset(epsilon[:], EPS)
                    pool.memset(pool_cell[:], 0.0)
                    for e in range(E):
                        pool.memset(rank[:, :, e], float(E - e))
                    pool.wait_ge(zeroed, 3)
                    pool.affine_select(out=ident[:], in_=ident[:], compare_op=ALU.not_equal, fill=1.0, base=0,
                                       pattern=[[-1, 128]], channel_multiplier=1).then_inc(made, 1)
                    pool.affine_select(out=ident4[:], in_=ident4[:], compare_op=ALU.not_equal, fill=1.0, base=0,
                                       pattern=[[0, 4], [-1, 128]], channel_multiplier=1).then_inc(made, 1)
                    pool.affine_select(out=future[:], in_=future[:], compare_op=ALU.is_ge, fill=NEG, base=0,
                                       pattern=[[1, 128]], channel_multiplier=-1).then_inc(made, 1)

                @block.tensor
                def _(pe):
                    pe.wait_ge(loaded, 16 * len(loads))
                    pe.wait_ge(made, 4)
                    for i in range(4):
                        pe.transpose(bank[0][:, i * D:(i + 1) * D], w_raw[i][:], ident[:])
                    for e in range(E):
                        pe.transpose(bank[1 + e // 4][:, e % 4 * D:(e % 4 + 1) * D], e_raw[:, e, :], ident[:])
                    pe.transpose(bank[3][:, 0:E], g_raw[:], ident[0:E, 0:E]).then_inc(turned, 1)

                @block.vector
                def _(dve):
                    dve.wait_ge(turned, 1)
                    for i, w in enumerate((wq, wk, wv, wo)):
                        dve.tensor_copy(w[0][:], bank[0][:, i * D:(i + 1) * D])
                    for c in range(2):
                        dve.tensor_copy(expert0_w[:, 4 * c:4 * c + 4, :], bank[1 + c][:].rearrange("p (e d) -> p e d", e=4))
                    dve.tensor_copy(gate0_w[:], bank[3][:, 0:E]).then_inc(kept, 1)

        def row_stats(dve, g, src, ln):
            for t in range(G):
                last = dve.bn_stats(ln.stats[g.p][:, t, :], src[:, t, :])
            last.then_inc(ln.stats_s, 1)
            dve.wait_ge(ln.stats_s, g.n + 1)
            dve.memset(dve_cell[:], 0.0)
            for t in range(G):
                last = dve.bn_aggr(ln.mv[g.p][:, t, :], ln.stats[g.p][:, t, :])
            last.then_inc(ln.mv_s, 1)

        def row_rstd(pool, g, ln):
            pool.wait_ge(ln.mv_s, g.n + 1)
            pool.tensor_tensor(ln.veps[g.p][:], ln.mv[g.p][:, :, 1], epsilon[:], ALU.add).then_inc(ln.veps_s, 1)
            pool.wait_ge(ln.veps_s, g.n + 1)
            pool.tensor_tensor(ln.rstd[g.p][:], ln.veps[g.p][:], minus_half[:], ALU.pow).then_inc(ln.rstd_s, 1)

        def row_apply(dve, g, src, ln):
            dve.wait_ge(ln.rstd_s, g.n + 1)
            for t in range(G):
                last = dve.tensor_scalar(ln.xn[g.p][:, t, :], src[:, t, :], ln.mv[g.p][:, t, 0:1],
                                         ln.rstd[g.p][:, t:t + 1], ALU.subtract, ALU.mult)
            last.then_inc(ln.xn_s, 1)

        class Norm:
            def __init__(self, name, own):
                two = lambda k, shape: [sb(f"{name}_{k}{p}", shape, to=own) for p in range(2)]
                self.stats, self.mv = two("stats", [128, G, 6]), two("mv", [128, G, 2])
                self.veps, self.rstd, self.xn = two("veps", [128, G]), two("rstd", [128, G]), two("xn", [128, G, D])
                self.stats_s, self.mv_s, self.veps_s, self.rstd_s, self.xn_s = (
                    sem(f"{name}_{k}") for k in ("stats", "mv", "veps", "rstd", "xn"))

        def rows(x, g):
            return x[bass.ds(g.n * G, G)].rearrange("b t d -> t b d")

        def project():
            KEYS = 2
            x_in, c_in = [sem(f"pj_x_in{p}") for p in range(2)], [sem(f"pj_c_in{p}") for p in range(2)]
            c_turned, x_turned, c_kept, x_kept = sem("pj_c_turned"), sem("pj_x_turned"), sem("pj_c_kept"), sem("pj_x_kept")
            kq_ps, v_ps, ones = sem("pj_kq_ps"), sem("pj_v_ps"), sem("pj_ones")
            part0, rest0, part1, part2, v_s = sem("pj_part0"), sem("pj_rest0"), sem("pj_part1"), sem("pj_part2"), sem("pj_v")
            kq_out = [[sem(f"pj_kq_out{p}{i}") for i in range(3)] for p in range(2)]
            v_out = [[sem(f"pj_v_out{p}{l}") for l in range(2)] for p in range(2)]
            with ExitStack() as own, nc.Block() as block:
                two = lambda k, shape, dt=F32: [sb(f"pj_{k}{p}", shape, dt, own) for p in range(2)]
                ln = Norm("pj_ln", own)
                c_g, x_g, c_t, x_t = two("c", [128, G, D]), two("x", [128, G, D]), two("ct", [128, GT]), two("xt", [128, GT])
                parts = [[sb(f"pj_parts{p}{i}", [128, 3, GT], BF16, own) for i in range(3)] for p in range(2)]
                rest = [sb(f"pj_rest{i}", [128, GT], to=own) for i in range(3)]
                vals = [[sb(f"pj_vals{p}{l}", [128, G * H, VW], to=own) for l in range(2)] for p in range(2)]
                ct_bank, xt_bank, kq_bank, v_bank = bank[0], bank[1], bank[2:5], bank[5:7]
                items = [(wk[0], bk[0], k_parts[0]), (wk[1], bk[1], k_parts[1]), (wq[0], bq[0], q_parts)]

                @block.sync
                def _(sp):
                    def load(g):
                        sp.wait_ge(c_turned, earlier(g.n - 1))
                        sp.dma_start(c_g[g.p][:], rows(a["ctx_1024"], g)).then_inc(c_in[g.p], 16)
                        sp.wait_ge(ln.xn_s, earlier(g.n - 1))
                        sp.dma_start(x_g[g.p][:], rows(a["x"], g)).then_inc(x_in[g.p], 16)

                    def store(g):
                        for i, (_, _, to) in enumerate(items):
                            sp.wait_ge(part2, g.n * 3 + i + 1)
                            sp.dma_start(to[:, :, bass.ds(g.n * GT, GT)].rearrange("c r t -> r c t"), parts[g.p][i][:]
                                         ).then_inc(kq_out[g.p][i], 16)
                        for l in range(2):
                            sp.wait_ge(v_s, g.n * 2 + l + 1)
                            sp.dma_start(v_ones[l][bass.ds(g.n * G, G)].rearrange("b t c -> t b c"),
                                         vals[g.p][l][:].rearrange("t (b h) c -> t b (h c)", b=G)
                                         ).then_inc(v_out[g.p][l], 16)

                    def body(g):
                        load(g.after())
                        store(g)
                    load(FIRST)
                    body(FIRST)
                    middle_groups(sp, body)
                    store(LAST)
                    for p in range(2):
                        for s in kq_out[p] + v_out[p]:
                            sp.wait_ge(s, 16 * (NG // 2))

                @block.tensor
                def _(pe):
                    def turn(g):
                        pe.wait_ge(c_in[g.p], g.turn * 16 + 16)
                        pe.wait_ge(c_kept, earlier(g.n))
                        for t in range(G):
                            mm = pe.transpose(ct_bank[:, t * T:(t + 1) * T], c_g[g.p][:, t, :], ident[:])
                        mm.then_inc(c_turned, 1)
                        pe.wait_ge(ln.xn_s, g.n + 1)
                        pe.wait_ge(x_kept, earlier(g.n))
                        for t in range(G):
                            mm = pe.transpose(xt_bank[:, t * T:(t + 1) * T], ln.xn[g.p][:, t, :], ident[:])
                        mm.then_inc(x_turned, 1)

                    def products(g):
                        for i, (w, _, _) in enumerate(items):
                            if i < KEYS:
                                pe.wait_ge(c_kept, g.n + 1)
                            else:
                                pe.wait_ge(x_kept, g.n + 1)
                            pe.wait_ge(rest0, earlier((g.n - 1) * 3 + i + 1))
                            pe.matmul(kq_bank[i][:], w[:], (c_t if i < KEYS else x_t)[g.p][:], start=True, stop=True
                                      ).then_inc(kq_ps, 1)
                        for l in range(2):
                            pe.wait_ge(v_s, earlier((g.n - 1) * 2 + l + 1))
                            for t in range(G):
                                mm = pe.matmul(v_bank[l][:, t * D:(t + 1) * D], c_t[g.p][:, t * T:(t + 1) * T], wv[l][:],
                                               start=True, stop=True)
                            mm.then_inc(v_ps, 1)

                    def body(g):
                        products(g)
                        turn(g.after())
                    turn(FIRST)
                    body(FIRST)
                    middle_groups(pe, body)
                    products(LAST)

                @block.scalar
                def _(act):
                    def keep(g):
                        act.wait_ge(c_turned, g.n + 1)
                        act.wait_ge(v_ps, earlier((g.n - 1) * 2))
                        act.copy(c_t[g.p][:], ct_bank[:]).then_inc(c_kept, 1)
                        act.wait_ge(x_turned, g.n + 1)
                        act.wait_ge(kq_ps, earlier((g.n - 1) * 3))
                        act.copy(x_t[g.p][:], xt_bank[:]).then_inc(x_kept, 1)

                    def first_parts(g):
                        for i, (_, b, _) in enumerate(items):
                            act.wait_ge(kq_ps, g.n * 3 + i + 1)
                            act.wait_ge(kq_out[g.p][i], earlier(g.turn * 16))
                            act.activation(parts[g.p][i][:, 0, :], kq_bank[i][:], ACT.Identity, bias=b[:]).then_inc(part0, 1)

                    def second_parts(g):
                        for i in range(3):
                            act.wait_ge(rest0, g.n * 3 + i + 1)
                            act.copy(parts[g.p][i][:, 1, :], rest[i][:]).then_inc(part1, 1)

                    def body(g):
                        first_parts(g)
                        second_parts(g)
                        keep(g.after())
                    keep(FIRST)
                    body(FIRST)
                    middle_groups(act, body)
                    first_parts(LAST)
                    second_parts(LAST)

                @block.vector
                def _(dve):
                    def stats(g):
                        dve.wait_ge(x_in[g.p], g.turn * 16 + 16)
                        row_stats(dve, g, x_g[g.p], ln)

                    def apply(g):
                        dve.wait_ge(x_turned, earlier(g.n - 1))
                        row_apply(dve, g, x_g[g.p], ln)

                    def rests(g):
                        for i, (_, b, _) in enumerate(items):
                            dve.wait_ge(part0, g.n * 3 + i + 1)
                            dve.wait_ge(part2, earlier((g.n - 1) * 3 + i + 1))
                            dve.scalar_tensor_tensor(out=rest[i][:], in0=kq_bank[i][:], scalar=b[:],
                                                     in1=parts[g.p][i][:, 0, :], op0=ALU.add, op1=ALU.subtract
                                                     ).then_inc(rest0, 1)

                    def values(g):
                        for l in range(2):
                            dve.wait_ge(v_ps, g.n * 2 + l + 1)
                            dve.wait_ge(v_out[g.p][l], earlier(g.turn * 16))
                            dve.tensor_tensor(
                                vals[g.p][l][:, :, 0:DH], v_bank[l][:].rearrange("t (h d) -> t h d", d=DH),
                                bv[l][:].unsqueeze(1).broadcast_to([128, G, D]).rearrange("t b (h d) -> t b h d", d=DH),
                                ALU.add).then_inc(v_s, 1)

                    for p in range(2):
                        for l in range(2):
                            dve.memset(vals[p][l][:], 1.0).then_inc(ones, 1)
                    dve.wait_ge(ones, 4)
                    stats(FIRST)
                    apply(FIRST)

                    def body(g):
                        rests(g)
                        stats(g.after())
                        values(g)
                        apply(g.after())
                    body(FIRST)
                    middle_groups(dve, body)
                    rests(LAST)
                    values(LAST)

                @block.gpsimd
                def _(pool):
                    def cut(g, i):
                        pool.wait_ge(part1, g.n * 3 + i + 1)
                        pool.tensor_tensor(parts[g.p][i][:, 2, :], rest[i][:], parts[g.p][i][:, 1, :], ALU.subtract
                                           ).then_inc(part2, 1)

                    def body(g):
                        cut(g, 0)
                        cut(g, 1)
                        row_rstd(pool, g.after(), ln)
                        cut(g, 2)
                    row_rstd(pool, FIRST, ln)
                    body(FIRST)
                    middle_groups(pool, body)
                    for i in range(3):
                        cut(LAST, i)

        def attention(l, x_src, x_dst):
            causal = l == 1
            scale = DH ** -0.5
            s = lambda name: sem(f"a{l}_{name}")
            qk_in, vx_in, mt_in, x_out = ([s(f"{k}{p}") for p in range(2)] for k in ("qk_in", "vx_in", "mt_in", "x_out"))
            s_ps, max_s, hi_s, split_s = s("s_ps"), s("max"), s("hi"), s("split")
            mt_ps, mt_s = s("mt_ps"), s("mt")
            st_ps, exp_s, masked_s, pv_s = s("st_ps"), s("exp"), s("masked"), s("pv")
            ot_s, oq_ps, rec_s, norm_s, on_ps, on_s = s("ot"), s("oq_ps"), s("rec"), s("norm"), s("on_ps"), s("on")
            y_ps, y_s, biased_s, ones_s, zero_s = s("y_ps"), s("y"), s("biased"), s("ones"), s("zero")
            probs_s = masked_s if causal else exp_s
            QK_IN, VX_IN = 16 * 2 * len(Q_PARTS), 16 * 2
            with ExitStack() as own, nc.Block() as block:
                qq = [sb(f"qq{l}{p}", [ROWS, H, GT], BF16, own) for p in range(2)]
                kk = [sb(f"kk{l}{p}", [ROWS, H, GT], BF16, own) for p in range(2)]
                vv = [sb(f"vv{l}{p}", [128, G, H * VW], to=own) for p in range(2)]
                xx = [sb(f"xx{l}{p}", [128, G, D], to=own) for p in range(2)]
                neg_max = [sb(f"nm{l}{p}", [128, H], to=own) for p in range(2)]
                max_parts = [sb(f"mp{l}{p}", [128, 2 * H], BF16, own) for p in range(2)]
                max_t = [sb(f"mt{l}{p}", [2 * H, T], BF16, own) for p in range(2)]
                probs = [sb(f"pr{l}{c}", [128, C4 * T], to=own) for c in range(NC)]
                o_t = [sb(f"ot{l}{p}", [128, C4 * T], to=own) for p in range(2)]
                rec = [sb(f"rc{l}{p}", [128, H], to=own) for p in range(2)]
                o_n = [sb(f"on{l}{p}", [128, D], to=own) for p in range(2)]
                o_nt = [sb(f"ont{l}{p}", [128, T], to=own) for p in range(2)]
                s_bank, st_bank, o_bank, oq_bank, m_bank = bank[0:2], bank[2:4], bank[4:6], bank[6], bank[7]
                max_bank = m_bank[0:2 * H, 0:T // 2].bitcast(BF16)

                @block.sync
                def _(sp):
                    def load_qk(g):
                        sp.wait_ge(st_ps, earlier((g.n - 1) * G * NC))
                        for side, src, which in ((qq, q_parts, Q_PARTS), (kk, k_parts[l], K_PARTS)):
                            for r, part in enumerate(which):
                                sp.dma_start(side[g.p][r * DH:(r + 1) * DH, :, :],
                                             src[part].rearrange("(h d) t -> d h t", d=DH)[:, :, bass.ds(g.n * GT, GT)]
                                             ).then_inc(qk_in[g.p], 16)

                    def load_vx(g):
                        sp.wait_ge(pv_s, earlier((g.n - 1) * G * NC))
                        sp.dma_start(vv[g.p][:], v_ones[l][bass.ds(g.n * G, G)].rearrange("b t c -> t b c")
                                     ).then_inc(vx_in[g.p], 16)
                        sp.wait_ge(x_out[g.p], earlier(g.turn * 16))
                        sp.dma_start(xx[g.p][:], x_src[bass.ds(g.n * G, G)].rearrange("b t d -> t b d")
                                     ).then_inc(vx_in[g.p], 16)

                    def store(g):
                        sp.wait_ge(y_s, (g.n + 1) * G)
                        sp.dma_start(x_dst[bass.ds(g.n * G, G)].rearrange("b t d -> t b d"), xx[g.p][:]
                                     ).then_inc(x_out[g.p], 16)

                    def place_maxima(q):
                        sp.wait_ge(mt_s, q.m + 1)
                        sp.dma_start(qq[q.g.p][PROD:ROWS, :, q.b * T:(q.b + 1) * T], max_t[q.p][:]
                                     ).then_inc(mt_in[q.p], 16)

                    def body(g, first=False, last=False):
                        for b in range(G):
                            if b == 0 and not last:
                                load_qk(g.after())
                            if b == 1 and not first:
                                store(g.before())
                            if b == 1 and not last:
                                load_vx(g.after())
                            if not (last and b + 1 >= G):
                                place_maxima(Seq(g, b).ahead(1))

                    sp.wait_ge(ones_s, 2)
                    load_qk(FIRST)
                    load_vx(FIRST)
                    place_maxima(Seq(FIRST, 0))
                    body(FIRST, first=True)
                    middle_groups(sp, body)
                    body(LAST, last=True)
                    store(LAST)
                    for p in range(2):
                        sp.wait_ge(x_out[p], 16 * (NG // 2))

                @block.tensor
                def _(pe):
                    def scores(q, c):
                        if c == 0 and q.b == 0:
                            pe.wait_ge(qk_in[q.g.p], (q.g.turn + 1) * QK_IN)
                        pe.wait_ge(max_s, earlier(q.m * NC + c - 1))
                        to, t = s_bank[c % 2], slice(q.b * T, (q.b + 1) * T)
                        if causal:
                            pe.matmul(to[:], future[:], ident4[:].rearrange("p a b -> p (a b)"), start=True, stop=True)
                        for j in range(C4):
                            mm = pe.matmul(to[:, j * T:(j + 1) * T], qq[q.g.p][0:PROD, c * C4 + j, t],
                                           kk[q.g.p][0:PROD, c * C4 + j, t], start=not causal, stop=True,
                                           skip_group_check=causal)
                        mm.then_inc(s_ps, 1)

                    def turn_maxima(q):
                        pe.wait_ge(split_s, q.m + 1)
                        pe.wait_ge(mt_s, earlier(q.m))
                        pe.wait_ge(y_s, earlier(q.m - 2))
                        pe.transpose(max_bank, max_parts[q.p][:], ident4[:, 0, :]).then_inc(mt_ps, 1)

                    def scores_t(q, c):
                        if c == 0:
                            pe.wait_ge(mt_in[q.p], (q.turn + 1) * 16)
                        pe.wait_ge(exp_s, earlier(q.m * NC + c - 1))
                        t = slice(q.b * T, (q.b + 1) * T)
                        for j in range(C4):
                            mm = pe.matmul(st_bank[c % 2][:, j * T:(j + 1) * T], kk[q.g.p][0:ROWS, c * C4 + j, t],
                                           qq[q.g.p][0:ROWS, c * C4 + j, t], start=True, stop=True)
                        mm.then_inc(st_ps, 1)

                    def mix(q, c):
                        if c == 0 and q.b == 0:
                            pe.wait_ge(vx_in[q.g.p], (q.g.turn + 1) * VX_IN)
                        if c == 0:
                            pe.wait_ge(ot_s, earlier(q.m - 1))
                        pe.wait_ge(probs_s, q.m * NC + c + 1)
                        for j in range(C4):
                            h = c * C4 + j
                            mm = pe.matmul(o_bank[q.p][32 * j:32 * j + VW, c * T:(c + 1) * T],
                                           vv[q.g.p][:, q.b, h * VW:(h + 1) * VW], probs[c][:, j * T:(j + 1) * T],
                                           start=True, stop=True)
                        mm.then_inc(pv_s, 1)

                    def turn_output(q):
                        pe.wait_ge(ot_s, q.m + 1)
                        pe.wait_ge(norm_s, earlier(q.m))
                        for c in range(NC):
                            mm = pe.transpose(oq_bank[:, c * T:(c + 1) * T], o_t[q.p][:, c * T:(c + 1) * T], ident[:])
                        mm.then_inc(oq_ps, 1)

                    def turn_normalised(q):
                        pe.wait_ge(norm_s, q.m + 1)
                        pe.wait_ge(mt_s, min(q.m + 3, B) if isinstance(q.m, int) else q.m + 3)
                        pe.transpose(m_bank[:, 0:T], o_n[q.p][:], ident[:]).then_inc(on_ps, 1)

                    def project(q):
                        pe.wait_ge(on_s, q.m + 1)
                        pe.matmul(m_bank[:, 0:D], o_nt[q.p][:], wo[l][:], start=True, stop=True).then_inc(y_ps, 1)

                    def body(g, first=False, last=False):
                        for b in range(G):
                            q = Seq(g, b)
                            past = None if first and b == 0 else q.ahead(-1)
                            following = None if last and b + 1 >= G else q.ahead(1)
                            to_come = None if last and b + 2 >= G else q.ahead(2)
                            for c in range(NC):
                                scores_t(q, c)
                                if to_come:
                                    scores(to_come, c)
                                if c:
                                    mix(q, c - 1)
                                elif past:
                                    mix(past, NC - 1)
                                if c == 0 and following:
                                    turn_maxima(following)
                                if c == 1 and past:
                                    turn_output(past)
                                if c == 2 and past:
                                    turn_normalised(past)
                                if c == 3 and past:
                                    project(past)

                    pe.wait_ge(zero_s, 1)
                    for p in range(2):
                        pe.matmul(o_bank[p][:], probs[0][:, 0:128], probs[0][:], start=True, stop=True)
                    for b in range(2):
                        for c in range(NC):
                            scores(Seq(FIRST, b), c)
                        if b == 0:
                            turn_maxima(Seq(FIRST, b))
                    body(FIRST, first=True)
                    middle_groups(pe, body)
                    body(LAST, last=True)
                    end = Seq(LAST, G - 1)
                    mix(end, NC - 1)
                    turn_output(end)
                    turn_normalised(end)
                    project(end)

                @block.scalar
                def _(act):
                    def exponential(q, c):
                        act.wait_ge(st_ps, q.m * NC + c + 1)
                        act.wait_ge(pv_s, earlier((q.m - 1) * NC + c + 1))
                        act.activation(probs[c][:], st_bank[c % 2][:], ACT.Exp, scale=scale).then_inc(exp_s, 1)

                    def keep_output(q):
                        act.wait_ge(pv_s, (q.m + 1) * NC)
                        act.wait_ge(oq_ps, earlier(q.m - 1))
                        act.copy(o_t[q.p][:], o_bank[q.p][:]).then_inc(ot_s, 1)

                    def keep_normalised(q):
                        act.wait_ge(on_ps, q.m + 1)
                        act.wait_ge(y_ps, earlier(q.m - 1))
                        act.copy(o_nt[q.p][:], m_bank[:, 0:T]).then_inc(on_s, 1)

                    def keep_maxima(q):
                        act.wait_ge(mt_ps, q.m + 1)
                        act.wait_ge(mt_in[q.p], earlier(q.turn * 16))
                        act.copy(max_t[q.p][:], max_bank).then_inc(mt_s, 1)

                    def body(g, first=False, last=False):
                        for b in range(G):
                            q = Seq(g, b)
                            past = None if first and b == 0 else q.ahead(-1)
                            exponential(q, 0)
                            if past:
                                keep_output(past)
                            if not (last and b + 1 >= G):
                                keep_maxima(q.ahead(1))
                            exponential(q, 1)
                            exponential(q, 2)
                            if past:
                                keep_normalised(past)
                            exponential(q, 3)

                    keep_maxima(Seq(FIRST, 0))
                    body(FIRST, first=True)
                    middle_groups(act, body)
                    body(LAST, last=True)
                    keep_output(Seq(LAST, G - 1))
                    keep_normalised(Seq(LAST, G - 1))

                @block.vector
                def _(dve):
                    def reduce_chunk(q, c):
                        dve.wait_ge(s_ps, q.m * NC + c + 1)
                        if c == 0:
                            dve.wait_ge(split_s, earlier(q.m - 1))
                        dve.tensor_reduce(neg_max[q.p][:, c * C4:(c + 1) * C4],
                                          s_bank[c % 2][:].rearrange("q (h k) -> q h k", h=C4), AX_X, ALU.max,
                                          negate=True).then_inc(max_s, 1)

                    def cut_maxima(q):
                        dve.wait_ge(max_s, (q.m + 1) * NC)
                        dve.wait_ge(mt_ps, earlier(q.m - 1))
                        dve.tensor_copy(max_parts[q.p][:, 0:H], neg_max[q.p][:]).then_inc(hi_s, 1)
                        dve.wait_ge(hi_s, q.m + 1)
                        dve.tensor_tensor(max_parts[q.p][:, H:2 * H], neg_max[q.p][:], max_parts[q.p][:, 0:H],
                                          ALU.subtract).then_inc(split_s, 1)

                    def normalise(q):
                        view = oq_bank[:].rearrange("q (h w) -> q h w", w=32)
                        dve.wait_ge(oq_ps, q.m + 1)
                        dve.reciprocal(rec[q.p][:].unsqueeze(2), view[:, :, DH:DH + 1]).then_inc(rec_s, 1)
                        dve.wait_ge(rec_s, q.m + 1)
                        dve.wait_ge(on_ps, earlier(q.m - 1))
                        dve.tensor_tensor(o_n[q.p][:].rearrange("q (h d) -> q h d", d=DH), view[:, :, 0:DH],
                                          rec[q.p][:].unsqueeze(2).broadcast_to([128, H, DH]), ALU.mult
                                          ).then_inc(norm_s, 1)

                    def add(q):
                        dve.wait_ge(y_ps, q.m + 1)
                        dve.wait_ge(biased_s, q.g.n + 1)
                        rows = xx[q.g.p][:, q.b, :]
                        dve.tensor_tensor(rows, m_bank[:, 0:D], rows, ALU.add).then_inc(y_s, 1)

                    def body(g, first=False, last=False):
                        for b in range(G):
                            q = Seq(g, b)
                            past = None if first and b == 0 else q.ahead(-1)
                            to_come = None if last and b + 2 >= G else q.ahead(2)
                            if to_come:
                                reduce_chunk(to_come, 0)
                                reduce_chunk(to_come, 1)
                            if past:
                                normalise(past)
                            if to_come:
                                reduce_chunk(to_come, 2)
                                reduce_chunk(to_come, 3)
                                cut_maxima(to_come)
                            if past:
                                add(past)

                    for p in range(2):
                        dve.memset(kk[p][32:ROWS, :, :], 1.0).then_inc(ones_s, 1)
                    dve.memset(probs[0][:], 0.0).then_inc(zero_s, 1)
                    for b in range(2):
                        for c in range(NC):
                            reduce_chunk(Seq(FIRST, b), c)
                        cut_maxima(Seq(FIRST, b))
                    body(FIRST, first=True)
                    middle_groups(dve, body)
                    body(LAST, last=True)
                    normalise(Seq(LAST, G - 1))
                    add(Seq(LAST, G - 1))

                @block.gpsimd
                def _(pool):
                    def bias(g):
                        pool.wait_ge(vx_in[g.p], (g.turn + 1) * VX_IN)
                        pool.tensor_tensor(xx[g.p][:], xx[g.p][:], bo[l][:].unsqueeze(1).broadcast_to([128, G, D]),
                                           ALU.add).then_inc(biased_s, 1)

                    def mask(q, c):
                        pool.wait_ge(exp_s, q.m * NC + c + 1)
                        pool.tensor_tensor(pool_cell[:, c:c + 1], epsilon[:, 0:1], epsilon[:, 0:1], ALU.mult)
                        pool.affine_select(out=probs[c][:], in_=probs[c][:], compare_op=ALU.is_ge, fill=0.0, base=0,
                                           pattern=[[0, C4], [1, T]], channel_multiplier=-1).then_inc(masked_s, 1)

                    def body(g):
                        bias(g)
                        if causal:
                            for b in range(G):
                                for c in range(NC):
                                    mask(Seq(g, b), c)
                    all_groups(pool, body)

        def experts0(x_src, x_dst):
            s = lambda name: sem(f"e0_{name}")
            x_in, x_out, q_out = ([s(f"{k}{p}") for p in range(2)] for k in ("x_in", "x_out", "q_out"))
            sum_s, turned, kept, sc_ps = s("sum"), s("turned"), s("kept"), s("sc_ps")
            top_s, tie_s, rank_s, best_s, hot_s = s("top"), s("tie"), s("rank"), s("best"), s("hot")
            hot_ps, chosen_s, y_ps, y_s, z_ps, z_s = s("hot_ps"), s("chosen"), s("y_ps"), s("y"), s("z_ps"), s("z")
            q_turned, q_kept, q_ps = s("q_turned"), s("q_kept"), s("q_ps")
            part0, rest0, part1, part2 = s("part0"), s("rest0"), s("part1"), s("part2")
            with ExitStack() as own, nc.Block() as block:
                two = lambda name, shape, dt=F32: [sb(f"e0{name}{p}", shape, dt, own) for p in range(2)]
                ln, q_ln = Norm("e0_ln", own), Norm("e0_qln", own)
                x_g, x_sum, xn_t, q_t = (two(k, [128, G * D]) for k in ("x", "xs", "xt", "qt"))
                top, best = two("top", [128, G]), two("best", [128, G])
                tie, ranked = two("tie", [128, G, E]), two("rk", [128, G, E])
                hot = two("hot", [128, G, E], BF16)
                chosen, y_t = two("ch", [128, GT]), sb("e0y", [128, GT], to=own)
                parts, rest = two("parts", [128, 3, GT], BF16), sb("e0rest", [128, GT], to=own)
                t_bank, sc_bank, hot_bank, y_bank, z_bank, qt_bank, q_bank = (
                    bank[0], bank[1], bank[2:4], bank[4], bank[5], bank[6], bank[7])

                def by_seq(tile):
                    return tile[:].rearrange("t (g d) -> t g d", g=G)

                @block.sync
                def _(sp):
                    def load(g):
                        sp.wait_ge(sum_s, earlier(g.n - 1))
                        sp.dma_start(by_seq(x_g[g.p]), rows(x_src, g)).then_inc(x_in[g.p], 16)

                    def store(g):
                        sp.wait_ge(z_s, g.n + 1)
                        sp.dma_start(rows(x_dst, g), by_seq(x_sum[g.p])).then_inc(x_out[g.p], 16)

                    def store_queries(g):
                        sp.wait_ge(part2, g.n + 1)
                        sp.dma_start(q_parts[:, :, bass.ds(g.n * GT, GT)].rearrange("c r t -> r c t"), parts[g.p][:]
                                     ).then_inc(q_out[g.p], 16)

                    load(FIRST)
                    load(FIRST.after())
                    store(FIRST)

                    def body(g):
                        load(g.after())
                        store_queries(g.before())
                        store(g)
                    middle_groups(sp, body)
                    store_queries(LAST.before())
                    store(LAST)
                    store_queries(LAST)
                    for p in range(2):
                        sp.wait_ge(x_out[p], 16 * (NG // 2))
                        sp.wait_ge(q_out[p], 16 * (NG // 2))

                @block.gpsimd
                def _(pool):
                    def add_rows(g):
                        pool.wait_ge(ln.xn_s, g.n + 1)
                        pool.wait_ge(q_ln.xn_s, earlier(g.n - 1))
                        pool.wait_ge(x_out[g.p], earlier(g.turn * 16))
                        pool.tensor_tensor(x_sum[g.p][:], x_g[g.p][:], ln.xn[g.p][:].rearrange("t g d -> t (g d)"), ALU.add
                                           ).then_inc(sum_s, 1)

                    def cut(g):
                        pool.wait_ge(part1, g.n + 1)
                        pool.tensor_tensor(parts[g.p][:, 2, :], rest[:], parts[g.p][:, 1, :], ALU.subtract).then_inc(part2, 1)

                    row_rstd(pool, FIRST, ln)
                    add_rows(FIRST)
                    row_rstd(pool, FIRST.after(), ln)
                    add_rows(FIRST.after())

                    def body(g, last=False):
                        row_rstd(pool, g.before(), q_ln)
                        if not last:
                            row_rstd(pool, g.after(), ln)
                            add_rows(g.after())
                        cut(g.before())
                    middle_groups(pool, body)
                    body(LAST, last=True)
                    row_rstd(pool, LAST, q_ln)
                    cut(LAST)

                @block.vector
                def _(dve):
                    def stats(g):
                        dve.wait_ge(x_in[g.p], g.turn * 16 + 16)
                        row_stats(dve, g, by_seq(x_g[g.p]), ln)

                    def apply(g):
                        dve.wait_ge(turned, earlier(g.n - 1))
                        dve.wait_ge(sum_s, earlier(g.n - 1))
                        row_apply(dve, g, by_seq(x_g[g.p]), ln)

                    def route(g):
                        view, p = sc_bank[:, 0:G * E].rearrange("t (g e) -> t g e", e=E), g.p
                        dve.wait_ge(sc_ps, g.n + 1)
                        dve.tensor_reduce(top[p][:], view, AX_X, ALU.max).then_inc(top_s, 1)
                        dve.wait_ge(top_s, g.n + 1)
                        dve.tensor_tensor(tie[p][:], view, top[p][:].unsqueeze(2).broadcast_to([128, G, E]), ALU.is_ge
                                          ).then_inc(tie_s, 1)
                        dve.wait_ge(tie_s, g.n + 1)
                        dve.tensor_tensor(ranked[p][:], tie[p][:], rank[:], ALU.mult).then_inc(rank_s, 1)
                        dve.wait_ge(rank_s, g.n + 1)
                        dve.tensor_reduce(best[p][:], ranked[p][:], AX_X, ALU.max).then_inc(best_s, 1)
                        dve.wait_ge(best_s, g.n + 1)
                        dve.wait_ge(hot_ps, earlier((g.n - 1) * E))
                        dve.tensor_tensor(hot[p][:], ranked[p][:], best[p][:].unsqueeze(2).broadcast_to([128, G, E]),
                                          ALU.is_equal).then_inc(hot_s, 1)

                    def choose(g, e):
                        dve.wait_ge(hot_ps, g.n * E + e + 1)
                        dve.wait_ge(y_ps, earlier(g.n * E + e - 1))
                        dve.tensor_tensor(chosen[e % 2][:], hot_bank[e % 2][:], xn_t[g.p][:], ALU.mult).then_inc(chosen_s, 1)

                    def add(g):
                        dve.wait_ge(z_ps, g.n + 1)
                        dve.wait_ge(sum_s, g.n + 1)
                        dve.tensor_tensor(x_sum[g.p][:], z_bank[:], x_sum[g.p][:], ALU.add).then_inc(z_s, 1)

                    def query_stats(g):
                        dve.wait_ge(z_s, g.n + 1)
                        row_stats(dve, g, by_seq(x_sum[g.p]), q_ln)

                    def query_apply(g):
                        dve.wait_ge(q_turned, earlier(g.n))
                        row_apply(dve, g, by_seq(x_sum[g.p]), q_ln)

                    def query_rest(g):
                        dve.wait_ge(part0, g.n + 1)
                        dve.wait_ge(part2, earlier(g.n))
                        dve.scalar_tensor_tensor(out=rest[:], in0=q_bank[:], scalar=bq[1][:], in1=parts[g.p][:, 0, :],
                                                 op0=ALU.add, op1=ALU.subtract).then_inc(rest0, 1)

                    def body(g, first=False, last=False):
                        choose(g, 0)
                        if not first:
                            query_stats(g.before())
                        choose(g, 1)
                        if not last:
                            stats(g.after())
                        choose(g, 2)
                        if not first:
                            query_apply(g.before())
                        choose(g, 3)
                        if not last:
                            apply(g.after())
                        choose(g, 4)
                        choose(g, 5)
                        if not first:
                            query_rest(g.before())
                        choose(g, 6)
                        choose(g, 7)
                        if not last:
                            route(g.after())
                        add(g)

                    stats(FIRST)
                    apply(FIRST)
                    route(FIRST)
                    body(FIRST, first=True)
                    middle_groups(dve, body)
                    body(LAST, last=True)
                    query_stats(LAST)
                    query_apply(LAST)
                    query_rest(LAST)

                @block.tensor
                def _(pe):
                    def turn(g):
                        pe.wait_ge(ln.xn_s, g.n + 1)
                        pe.wait_ge(kept, earlier(g.n))
                        for t in range(G):
                            mm = pe.transpose(t_bank[:, t * T:(t + 1) * T], ln.xn[g.p][:, t, :], ident[:])
                        mm.then_inc(turned, 1)

                    def score(g):
                        pe.wait_ge(kept, g.n + 1)
                        pe.wait_ge(tie_s, earlier(g.n))
                        for t in range(G):
                            mm = pe.matmul(sc_bank[:, t * E:(t + 1) * E], xn_t[g.p][:, t * T:(t + 1) * T], gate0_w[:],
                                           start=True, stop=True)
                        mm.then_inc(sc_ps, 1)

                    def spread(g, e):
                        if e == 0:
                            pe.wait_ge(hot_s, g.n + 1)
                        pe.wait_ge(chosen_s, earlier(g.n * E + e - 1))
                        for t in range(G):
                            mm = pe.matmul(hot_bank[e % 2][:, t * T:(t + 1) * T],
                                           hot[g.p][:, t, e:e + 1].broadcast_to([128, 128]), ident4[:, 0, :],
                                           start=True, stop=True)
                        mm.then_inc(hot_ps, 1)

                    def expert(g, e):
                        pe.wait_ge(chosen_s, g.n * E + e + 1)
                        if e == 0:
                            pe.wait_ge(y_s, earlier(g.n))
                        pe.matmul(y_bank[:], expert0_w[:, e, :], chosen[e % 2][:], start=(e == 0), stop=(e == E - 1)
                                  ).then_inc(y_ps, 1)

                    def turn_back(g):
                        pe.wait_ge(y_s, g.n + 1)
                        pe.wait_ge(z_s, earlier(g.n))
                        for t in range(G):
                            mm = pe.transpose(z_bank[:, t * T:(t + 1) * T], y_t[:, t * T:(t + 1) * T], ident[:])
                        mm.then_inc(z_ps, 1)

                    def turn_queries(g):
                        pe.wait_ge(q_ln.xn_s, g.n + 1)
                        pe.wait_ge(q_kept, earlier(g.n))
                        for t in range(G):
                            mm = pe.transpose(qt_bank[:, t * T:(t + 1) * T], q_ln.xn[g.p][:, t, :], ident[:])
                        mm.then_inc(q_turned, 1)

                    def queries(g):
                        pe.wait_ge(q_kept, g.n + 1)
                        pe.wait_ge(rest0, earlier(g.n))
                        pe.matmul(q_bank[:], wq[1][:], q_t[g.p][:], start=True, stop=True).then_inc(q_ps, 1)

                    def body(g, first=False, last=False):
                        if first:
                            spread(g, 0)
                        spread(g, 1)
                        for e in range(E):
                            expert(g, e)
                            if e + 2 < E:
                                spread(g, e + 2)
                            if e == 3 and not first:
                                turn_queries(g.before())
                            if e == 4 and not first:
                                queries(g.before())
                            if e == 4 and not last:
                                turn(g.after())
                            if e == 6 and not last:
                                score(g.after())
                        turn_back(g)
                        if not last:
                            spread(g.after(), 0)

                    turn(FIRST)
                    score(FIRST)
                    body(FIRST, first=True)
                    middle_groups(pe, body)
                    body(LAST, last=True)
                    turn_queries(LAST)
                    queries(LAST)

                @block.scalar
                def _(act):
                    def keep_turned(g):
                        act.wait_ge(turned, g.n + 1)
                        act.wait_ge(sc_ps, earlier(g.n - 1))
                        act.wait_ge(chosen_s, earlier((g.n - 1) * E))
                        act.copy(xn_t[g.p][:], t_bank[:]).then_inc(kept, 1)

                    def keep_sum(g):
                        act.wait_ge(y_ps, (g.n + 1) * E)
                        act.wait_ge(z_ps, earlier(g.n))
                        act.copy(y_t[:], y_bank[:]).then_inc(y_s, 1)

                    def query_parts(g):
                        act.wait_ge(q_ps, g.n + 1)
                        act.wait_ge(q_out[g.p], earlier(g.turn * 16))
                        act.activation(parts[g.p][:, 0, :], q_bank[:], ACT.Identity, bias=bq[1][:]).then_inc(part0, 1)

                    def query_second(g):
                        act.wait_ge(rest0, g.n + 1)
                        act.copy(parts[g.p][:, 1, :], rest[:]).then_inc(part1, 1)

                    def keep_queries(g):
                        act.wait_ge(q_turned, g.n + 1)
                        act.wait_ge(q_ps, earlier(g.n))
                        act.copy(q_t[g.p][:], qt_bank[:]).then_inc(q_kept, 1)

                    def body(g, first=False, last=False):
                        if not first:
                            keep_queries(g.before())
                            query_parts(g.before())
                        if not last:
                            keep_turned(g.after())
                        if not first:
                            query_second(g.before())
                        keep_sum(g)

                    keep_turned(FIRST)
                    body(FIRST, first=True)
                    middle_groups(act, body)
                    body(LAST, last=True)
                    keep_queries(LAST)
                    query_parts(LAST)
                    query_second(LAST)

        def experts1(x_src, x_dst):
            s = lambda name: sem(f"e1_{name}")
            x_in, x_out = ([s(f"{k}{p}") for p in range(2)] for k in ("x_in", "x_out"))
            w_in = s("w_in")
            turned, kept, sc_ps, small, exp_s = s("turned"), s("kept"), s("sc_ps"), s("small"), s("exp")
            weights_s, gate_ps, up_ps, silu_s, act_s, down_ps, sum_s = (
                s(k) for k in ("weights", "gate_ps", "up_ps", "silu", "act", "down_ps", "sum"))
            NF = len(FCH)
            STEPS = 19
            with ExitStack() as own, nc.Block() as block:
                two = lambda name, shape, dt=F32: [sb(f"e1{name}{p}", shape, dt, own) for p in range(2)]
                gate_w, up_w = sb("gate_w", [128, E, F], to=own), sb("up_w", [128, E, F], to=own)
                down_w = sb("down_w", [128, E, NF, D], to=own)
                router_w = sb("router_w", [128, E], to=own)
                ln = Norm("e1_ln", own)
                x_g, x_sum, xn_t = two("x", [128, G, D]), two("xs", [128, G, D]), two("xt", [128, GT])
                shifted, probs = two("sh", [128, G, E]), two("pr", [128, G, E])
                work = sb("e1work", [128, 6, G, E], to=own)
                col = sb("e1col", [128, 8, G], to=own)
                weights = two("w", [128, G, E])
                silu = two("si", [128, GT])
                acts = [[sb(f"e1act{p}{f}", [128, GT], to=own) for f in range(NF)] for p in range(2)]
                t_bank, sc_bank, gate_bank, up_bank, down_bank = bank[0], bank[1], bank[2:4], bank[4:6], bank[6:8]

                @block.sync
                def _(sp):
                    def load(g):
                        sp.wait_ge(sum_s, earlier(((g.n - 2) * E + 1) * G))
                        sp.dma_start(x_g[g.p][:], x_src[bass.ds(g.n * G, G)].rearrange("b t d -> t b d")
                                     ).then_inc(x_in[g.p], 16)

                    def store(g):
                        sp.wait_ge(sum_s, (g.n + 1) * E * G)
                        sp.dma_start(x_dst[bass.ds(g.n * G, G)].rearrange("b t d -> t b d"), x_sum[g.p][:]
                                     ).then_inc(x_out[g.p], 16)

                    def body(g):
                        load(g.after())
                        store(g)
                    load(FIRST)
                    sp.dma_start(router_w[:], a["L1_ffn_router_w"]).then_inc(w_in, 16)
                    sp.dma_start(gate_w[:], a["L1_ffn_gate_proj"].rearrange("e d f -> d e f")).then_inc(w_in, 16)
                    sp.dma_start(up_w[:], a["L1_ffn_up_proj"].rearrange("e d f -> d e f")).then_inc(w_in, 16)
                    for f, (f0, fn) in enumerate(FCH):
                        sp.dma_start(down_w[0:fn, :, f, :],
                                     a["L1_ffn_down_proj"][:, f0:f0 + fn, :].rearrange("e f d -> f e d")).then_inc(w_in, 16)
                    load(FIRST.after())
                    store(FIRST)
                    middle_groups(sp, body)
                    store(LAST)
                    for p in range(2):
                        sp.wait_ge(x_out[p], 16 * (NG // 2))

                @block.gpsimd
                def _(pool):
                    all_groups(pool, lambda g: row_rstd(pool, g, ln))

                @block.vector
                def _(dve):
                    def stats(g):
                        dve.wait_ge(x_in[g.p], g.turn * 16 + 16)
                        row_stats(dve, g, x_g[g.p], ln)

                    def apply(g):
                        dve.wait_ge(turned, earlier(g.n - 1))
                        row_apply(dve, g, x_g[g.p], ln)

                    def wide(column):
                        return col[:, column, :].unsqueeze(2).broadcast_to([128, G, E])

                    def route(g):
                        view, p = sc_bank[:, 0:G * E].rearrange("t (g e) -> t g e", e=E), g.p
                        done = [g.n * STEPS]

                        def step(ins):
                            ins.then_inc(small, 1)
                            done[0] = done[0] + 1
                            dve.wait_ge(small, done[0])

                        dve.wait_ge(sc_ps, g.n + 1)
                        step(dve.tensor_reduce(col[:, 0, :], view, AX_X, ALU.max))
                        step(dve.tensor_tensor(shifted[p][:], view, wide(0), ALU.subtract))
                        dve.wait_ge(exp_s, g.n + 1)
                        step(dve.tensor_reduce(col[:, 1, :], probs[p][:], AX_X, ALU.add))
                        step(dve.reciprocal(col[:, 2, :], col[:, 1, :]))
                        step(dve.tensor_tensor(work[:, 0], probs[p][:], wide(2), ALU.mult))
                        for k in range(2):
                            left = work[:, 0] if k == 0 else work[:, 4]
                            step(dve.tensor_reduce(col[:, 3 + k, :], left, AX_X, ALU.max))
                            step(dve.tensor_tensor(work[:, 1], left, wide(3 + k), ALU.is_ge))
                            step(dve.tensor_tensor(work[:, 1], work[:, 1], rank[:], ALU.mult))
                            step(dve.tensor_reduce(col[:, 5, :], work[:, 1], AX_X, ALU.max))
                            dve.tensor_tensor(work[:, 2 + k], work[:, 1], wide(5), ALU.is_equal)
                            if k == 0:
                                step(dve.tensor_tensor(work[:, 5], work[:, 1], wide(5), ALU.is_equal))
                                step(dve.scalar_tensor_tensor(out=work[:, 4], in0=work[:, 5], scalar=-2.0, in1=work[:, 0],
                                                              op0=ALU.mult, op1=ALU.add))
                        step(dve.tensor_tensor(col[:, 6, :], col[:, 3, :], col[:, 4, :], ALU.add))
                        step(dve.reciprocal(col[:, 7, :], col[:, 6, :]))
                        step(dve.tensor_tensor(work[:, 5], work[:, 2], work[:, 3], ALU.add))
                        step(dve.tensor_tensor(work[:, 1], work[:, 5], work[:, 0], ALU.mult))
                        dve.wait_ge(sum_s, earlier((g.n - 1) * E * G))
                        dve.tensor_tensor(weights[p][:], work[:, 1], wide(7), ALU.mult).then_inc(weights_s, 1)

                    def activate(g, e, f):
                        k = (g.n * E + e) * NF + f
                        fn = FCH[f][1]
                        dve.wait_ge(silu_s, k + 1)
                        dve.wait_ge(up_ps, k + 1)
                        dve.wait_ge(down_ps, earlier(g.n * E + e - 1))
                        dve.tensor_tensor(acts[e % 2][f][0:fn, :], up_bank[k_parity(e, f)][0:fn, :], silu[k_parity(e, f)][0:fn, :],
                                          ALU.mult).then_inc(act_s, 1)

                    def add(g, e):
                        if e == 0:
                            dve.wait_ge(weights_s, g.n + 1)
                            dve.wait_ge(x_out[g.p], earlier(g.turn * 16))
                        dve.wait_ge(down_ps, g.n * E + e + 1)
                        for t in range(G):
                            if e:
                                dve.wait_ge(sum_s, earlier((g.n * E + e - 1) * G + t + 1))
                            dve.scalar_tensor_tensor(out=x_sum[g.p][:, t, :], in0=down_bank[e % 2][:, t * D:(t + 1) * D],
                                                     scalar=weights[g.p][:, t, e:e + 1],
                                                     in1=(x_sum if e else x_g)[g.p][:, t, :],
                                                     op0=ALU.mult, op1=ALU.add).then_inc(sum_s, 1)

                    def back(g, ahead):
                        for e in range(E):
                            for f in range(NF):
                                activate(g, e, f)
                            if e:
                                add(g, e - 1)
                            if e == 1 and ahead:
                                stats(ahead)
                            if e == 2 and ahead:
                                apply(ahead)
                            if e == 4 and ahead:
                                route(ahead)
                        add(g, E - 1)

                    stats(FIRST)
                    apply(FIRST)
                    route(FIRST)
                    back(FIRST, FIRST.after())
                    middle_groups(dve, lambda g: back(g, g.after()))
                    back(LAST, None)

                @block.tensor
                def _(pe):
                    def turn(g):
                        pe.wait_ge(ln.xn_s, g.n + 1)
                        pe.wait_ge(kept, earlier(g.n))
                        for t in range(G):
                            mm = pe.transpose(t_bank[:, t * T:(t + 1) * T], ln.xn[g.p][:, t, :], ident[:])
                        mm.then_inc(turned, 1)

                    def score(g):
                        pe.wait_ge(kept, g.n + 1)
                        for t in range(G):
                            mm = pe.matmul(sc_bank[:, t * E:(t + 1) * E], xn_t[g.p][:, t * T:(t + 1) * T], router_w[:],
                                           start=True, stop=True)
                        mm.then_inc(sc_ps, 1)

                    def gate_up(g, e, f):
                        k = (g.n * E + e) * NF + f
                        f0, fn = FCH[f]
                        i = k_parity(e, f)
                        pe.wait_ge(silu_s, earlier(k - 1))
                        pe.matmul(gate_bank[i][0:fn, :], gate_w[:, e, f0:f0 + fn], xn_t[g.p][:], start=True, stop=True
                                  ).then_inc(gate_ps, 1)
                        pe.wait_ge(act_s, earlier(k - 1))
                        pe.matmul(up_bank[i][0:fn, :], up_w[:, e, f0:f0 + fn], xn_t[g.p][:], start=True, stop=True
                                  ).then_inc(up_ps, 1)

                    def down(g, e):
                        pe.wait_ge(act_s, (g.n * E + e + 1) * NF)
                        pe.wait_ge(sum_s, earlier((g.n * E + e - 1) * G))
                        for t in range(G):
                            for f, (f0, fn) in enumerate(FCH):
                                mm = pe.matmul(down_bank[e % 2][:, t * D:(t + 1) * D], acts[e % 2][f][0:fn, t * T:(t + 1) * T],
                                               down_w[0:fn, e, f, :], start=(f == 0), stop=(f == NF - 1))
                        mm.then_inc(down_ps, 1)

                    def back(g, ahead):
                        for e in range(E):
                            for f in range(NF):
                                gate_up(g, e, f)
                                if f == 0 and e:
                                    down(g, e - 1)
                            if e == 2 and ahead:
                                turn(ahead)
                            if e == 3 and ahead:
                                score(ahead)
                        down(g, E - 1)

                    pe.wait_ge(w_in, 16 * (3 + NF))
                    turn(FIRST)
                    score(FIRST)
                    back(FIRST, FIRST.after())
                    middle_groups(pe, lambda g: back(g, g.after()))
                    back(LAST, None)

                @block.scalar
                def _(act):
                    def keep_turned(g):
                        act.wait_ge(turned, g.n + 1)
                        act.wait_ge(sc_ps, earlier(g.n - 1))
                        act.wait_ge(up_ps, earlier((g.n - 1) * E * NF))
                        act.copy(xn_t[g.p][:], t_bank[:]).then_inc(kept, 1)

                    def exponential(g):
                        act.wait_ge(small, g.n * STEPS + 2)
                        act.activation(probs[g.p][:], shifted[g.p][:], ACT.Exp).then_inc(exp_s, 1)

                    def gate(g, e, f):
                        k = (g.n * E + e) * NF + f
                        fn = FCH[f][1]
                        i = k_parity(e, f)
                        act.wait_ge(gate_ps, k + 1)
                        act.wait_ge(act_s, earlier(k - 1))
                        act.activation(silu[i][0:fn, :], gate_bank[i][0:fn, :], ACT.Silu).then_inc(silu_s, 1)

                    def back(g, ahead):
                        for e in range(E):
                            for f in range(NF):
                                gate(g, e, f)
                            if e == 2 and ahead:
                                keep_turned(ahead)
                            if e == 4 and ahead:
                                exponential(ahead)

                    keep_turned(FIRST)
                    exponential(FIRST)
                    back(FIRST, FIRST.after())
                    middle_groups(act, lambda g: back(g, g.after()))
                    back(LAST, None)

        prepare()
        project()
        attention(0, a["x"], x_attn0)
        experts0(x_attn0, x_ffn0)
        clear_semaphores()
        attention(1, x_ffn0, x_attn1)
        experts1(x_attn1, out)


INS = ["x", "ctx_1024",
       "L0_xattn_w_q", "L0_xattn_b_q", "L0_xattn_w_k", "L0_xattn_b_k", "L0_xattn_w_v", "L0_xattn_b_v",
       "L0_xattn_w_o", "L0_xattn_b_o", "L0_ffn_gate_w", "L0_ffn_expert_w",
       "L1_xattn_Wq", "L1_xattn_bq", "L1_xattn_Wk", "L1_xattn_bk", "L1_xattn_Wv", "L1_xattn_bv",
       "L1_xattn_Wo", "L1_xattn_bo", "L1_ffn_router_w", "L1_ffn_gate_proj", "L1_ffn_up_proj", "L1_ffn_down_proj"]


def kernel(**inputs):
    import numpy as np
    import concourse.bacc as bacc
    from concourse.bass_utils import run_bass_kernel_spmd

    nc = bacc.Bacc("TRN2", target_bir_lowering=False, num_devices=1)
    arrays, aps = {}, {}
    for name in INS:
        arrays[name] = np.ascontiguousarray(inputs[name])
        aps[name] = nc.dram_tensor(name, arrays[name].shape, mybir.dt.from_np(arrays[name].dtype), kind="ExternalInput").ap()
    out = nc.dram_tensor("out", (B, T, D), F32, kind="ExternalOutput").ap()
    build(nc, aps, out)
    ran = run_bass_kernel_spmd(nc, [arrays], core_ids=[0])
    return ran.results[0]["out"]
```

```python
from contextlib import ExitStack

import concourse.bass as bass
from concourse import mybir

ALU = mybir.AluOpType
ACT = mybir.ActivationFunctionType
AX_X = mybir.AxisListType.X
F32 = mybir.dt.float32
BF16 = mybir.dt.bfloat16
FP16 = mybir.dt.float16
I32 = mybir.dt.int32

B = 32
T = 128
D = 128
H = 16
DH = D // H
G = 4
NG = B // G
GT = G * T
VW = 3 * DH + 1
Q_PARTS = (0, 0, 0, 1, 1, 2)
K_PARTS = (0, 1, 2, 0, 1, 0)
PROD = DH * len(Q_PARTS)
ROWS = 128
MAX_ROW = ROWS - 2
C4 = 4
NC = H // C4
E = 8
F = 352
FCH = ((0, 128), (128, 128), (256, 96))
SLOTS = 2 * B + E
ROW = D + 2
SPARE = 2 * B * T
NEG = -1e30
EPS = 1e-5


def earlier(count):
    return max(count, 0) if isinstance(count, int) else count


class Group:

    def __init__(self, turn, p):
        self.turn, self.p, self.n = turn, p, turn * 2 + p

    def after(self):
        return Group(self.turn, 1) if self.p == 0 else Group(self.turn + 1, 0)

    def before(self):
        return Group(self.turn, 0) if self.p == 1 else Group(self.turn - 1, 1)


class Seq:

    def __init__(self, g, b):
        self.g, self.b, self.m, self.p, self.turn = g, b, g.n * G + b, b % 2, g.n * (G // 2) + b // 2

    def ahead(self, k):
        if 0 <= self.b + k < G:
            return Seq(self.g, self.b + k)
        return Seq(self.g.after(), self.b + k - G) if k > 0 else Seq(self.g.before(), self.b + k + G)


def all_groups(eng, body, count=NG):
    body(Group(0, 0))
    body(Group(0, 1))
    with eng.Fori(1, count // 2) as i:
        body(Group(i, 0))
        body(Group(i, 1))


def middle_groups(eng, body, count=NG):
    body(Group(0, 1))
    body(Group(1, 0))
    with eng.Fori(1, count // 2 - 1) as i:
        body(Group(i, 1))
        body(Group(i + 1, 0))


FIRST, LAST = Group(0, 0), Group(NG // 2 - 1, 1)
NQ = SLOTS // G
LAST_TILES = Group(NQ // 2 - 1, 1)


def build(nc, a, out):
    ctx = ExitStack()

    in_use = []
    def sem(name):
        in_use.append(nc.alloc_semaphore(name=name))
        return in_use[-1]

    def clear_semaphores():
        nc.clear_and_free_semaphores(in_use)
        nc.all_engine_barrier()
        in_use.clear()

    def scratch(name, shape, dt):
        return nc.dram_tensor(name, shape, dt, kind="Internal").ap()

    with ctx:
        def sb(name, shape, dt=F32, to=ctx):
            return to.enter_context(nc.sbuf_tensor(name, shape, dt))

        bank = [ctx.enter_context(nc.psum_tensor(f"bank{i}", [128, 512], F32)) for i in range(8)]

        q_parts = scratch("q_parts", (3, D, B * T), BF16)
        k_parts = scratch("k_parts", (2, 3, D, B * T), BF16)
        v_parts = scratch("v_parts", (2, B, T, H * VW), BF16)
        x_attn0 = scratch("x_attn0", (B, T, D), F32)
        x_ffn0 = scratch("x_ffn0", (B, T, D), F32)
        x_attn1 = scratch("x_attn1", (B, T, D), F32)
        x_norm = scratch("x_norm", (B, T, D), F32)
        scores_d = scratch("scores", (T, B * E), F32)
        place_d = scratch("place", (T, B * 2), I32)
        tags_d = scratch("tags", (T, B * 2, 2), I32)
        sorted_in = scratch("sorted_in", (SLOTS * T, ROW), F32)
        results = scratch("results", (SPARE + SLOTS * T, D), F32)

        ident = sb("ident", [128, 128])
        ident4 = sb("ident4", [128, 4, 128], BF16)
        future = sb("future", [128, 128], BF16)
        earlier_tokens = sb("earlier_tokens", [128, 128], BF16)
        all_tokens = sb("all_tokens", [128, 128], BF16)
        tile_no_i, tile_no = sb("tile_no_i", [128, SLOTS], I32), sb("tile_no", [128, SLOTS])
        wq = [sb(f"wq{l}", [128, D]) for l in range(2)]
        wk = [sb(f"wk{l}", [128, D]) for l in range(2)]
        wv = [sb(f"wv{l}", [128, D]) for l in range(2)]
        wo = [sb(f"wo{l}", [128, D]) for l in range(2)]
        bq = [sb(f"bq{l}", [128, 1]) for l in range(2)]
        bk = [sb(f"bk{l}", [128, 1]) for l in range(2)]
        bv = [sb(f"bv{l}", [128, D]) for l in range(2)]
        bo = [sb(f"bo{l}", [128, D]) for l in range(2)]
        expert0_w = sb("expert0_w", [128, E, D])
        gate0_w = sb("gate0_w", [128, E])
        qq = [sb(f"qq{p}", [ROWS, H, GT], BF16) for p in range(2)]
        kk = [sb(f"kk{p}", [ROWS, H, GT], BF16) for p in range(2)]
        minus_half, epsilon = sb("minus_half", [128, G]), sb("epsilon", [128, G])
        pool_cell, dve_cell = sb("pool_cell", [128, NC]), sb("dve_cell", [128, 1])
        rank = sb("expert_rank", [128, G, E])

        early = ExitStack()
        padding = sb("padding", [128, SLOTS, ROW], to=early)

        def prepare():
            loaded, zeroed, ones_set = sem("p_loaded"), sem("p_zeroed"), sem("p_ones")
            turned, kept, made, counted = sem("p_turned"), sem("p_kept"), sem("p_made"), sem("p_counted")
            with ExitStack() as own, nc.Block() as block:
                w_raw = [sb(f"w_raw{i}", [128, D], to=own) for i in range(4)]
                e_raw = sb("e_raw", [128, E, D], to=own)
                g_raw = sb("g_raw", [E, D], to=own)
                loads = [(w_raw[i][:], a[n]) for i, n in enumerate(
                    ("L0_xattn_w_q", "L0_xattn_w_k", "L0_xattn_w_v", "L0_xattn_w_o"))]
                loads += [(g_raw[:], a["L0_ffn_gate_w"]),
                          (e_raw[:], a["L0_ffn_expert_w"].rearrange("e f h -> f e h")),
                          (wq[1][:], a["L1_xattn_Wq"]), (wk[1][:], a["L1_xattn_Wk"]),
                          (wv[1][:], a["L1_xattn_Wv"]), (wo[1][:], a["L1_xattn_Wo"])]
                for l, pre in enumerate(("L0_xattn_b_", "L1_xattn_b")):
                    loads += [(bq[l][:], a[pre + "q"].unsqueeze(1)), (bk[l][:], a[pre + "k"].unsqueeze(1)),
                              (bv[l][:], a[pre + "v"].partition_broadcast(128)),
                              (bo[l][:], a[pre + "o"].partition_broadcast(128))]

                @block.sync
                def _(sp):
                    for to, src in loads:
                        sp.dma_start(to, src).then_inc(loaded, 16)
                    sp.wait_ge(loaded, 16 * len(loads))

                @block.gpsimd
                def _(pool):
                    pool.memset(ident[:], 0.0).then_inc(zeroed, 1)
                    pool.memset(ident4[:], 0.0).then_inc(zeroed, 1)
                    pool.memset(future[:], 0.0).then_inc(zeroed, 1)
                    pool.memset(earlier_tokens[:], 1.0).then_inc(zeroed, 1)
                    pool.memset(all_tokens[:], 1.0)
                    pool.iota(tile_no_i[:], pattern=[[1, SLOTS]], base=0, channel_multiplier=0).then_inc(counted, 1)
                    pool.memset(minus_half[:], -0.5).then_inc(made, 1)
                    pool.memset(epsilon[:], EPS)
                    pool.memset(pool_cell[:], 0.0)
                    for e in range(E):
                        pool.memset(rank[:, :, e], float(E - e))
                    pool.memset(padding[:], 0.0).then_inc(zeroed, 1)
                    pool.wait_ge(zeroed, 5)
                    pool.iota(padding[:, :, ROW - 1:ROW].bitcast(I32), pattern=[[1, SLOTS], [1, 1]], base=SPARE,
                              channel_multiplier=SLOTS)
                    pool.affine_select(out=ident[:], in_=ident[:], compare_op=ALU.not_equal, fill=1.0, base=0,
                                       pattern=[[-1, 128]], channel_multiplier=1).then_inc(made, 1)
                    pool.affine_select(out=ident4[:], in_=ident4[:], compare_op=ALU.not_equal, fill=1.0, base=0,
                                       pattern=[[0, 4], [-1, 128]], channel_multiplier=1).then_inc(made, 1)
                    pool.affine_select(out=future[:], in_=future[:], compare_op=ALU.is_ge, fill=NEG, base=0,
                                       pattern=[[1, 128]], channel_multiplier=-1).then_inc(made, 1)
                    pool.affine_select(out=earlier_tokens[:], in_=earlier_tokens[:], compare_op=ALU.is_gt, fill=0.0,
                                       base=0, pattern=[[1, 128]], channel_multiplier=-1)
                    for p in range(2):
                        pool.memset(qq[p][:], 0.0)

                @block.tensor
                def _(pe):
                    pe.wait_ge(loaded, 16 * len(loads))
                    pe.wait_ge(made, 4)
                    for i in range(4):
                        pe.transpose(bank[0][:, i * D:(i + 1) * D], w_raw[i][:], ident[:])
                    for e in range(E):
                        pe.transpose(bank[1 + e // 4][:, e % 4 * D:(e % 4 + 1) * D], e_raw[:, e, :], ident[:])
                    pe.transpose(bank[3][:, 0:E], g_raw[:], ident[0:E, 0:E]).then_inc(turned, 1)

                @block.vector
                def _(dve):
                    dve.wait_ge(counted, 1)
                    dve.tensor_copy(tile_no[:], tile_no_i[:])
                    for p in range(2):
                        dve.memset(kk[p][:], 1.0)
                    dve.wait_ge(turned, 1)
                    for i, w in enumerate((wq, wk, wv, wo)):
                        dve.tensor_copy(w[0][:], bank[0][:, i * D:(i + 1) * D])
                    for c in range(2):
                        dve.tensor_copy(expert0_w[:, 4 * c:4 * c + 4, :], bank[1 + c][:].rearrange("p (e d) -> p e d", e=4))
                    dve.tensor_copy(gate0_w[:], bank[3][:, 0:E]).then_inc(kept, 1)

        def row_stats(dve, g, src, ln):
            for t in range(G):
                last = dve.bn_stats(ln.stats[g.p][:, t, :], src[:, t, :])
            last.then_inc(ln.stats_s, 1)
            dve.wait_ge(ln.stats_s, g.n + 1)
            dve.memset(dve_cell[:], 0.0)
            for t in range(G):
                last = dve.bn_aggr(ln.mv[g.p][:, t, :], ln.stats[g.p][:, t, :])
            last.then_inc(ln.mv_s, 1)

        def row_rstd(pool, g, ln):
            pool.wait_ge(ln.mv_s, g.n + 1)
            pool.tensor_tensor(ln.veps[g.p][:], ln.mv[g.p][:, :, 1], epsilon[:], ALU.add).then_inc(ln.veps_s, 1)
            pool.wait_ge(ln.veps_s, g.n + 1)
            pool.tensor_tensor(ln.rstd[g.p][:], ln.veps[g.p][:], minus_half[:], ALU.pow).then_inc(ln.rstd_s, 1)

        def row_apply(dve, g, src, ln):
            dve.wait_ge(ln.rstd_s, g.n + 1)
            for t in range(G):
                last = dve.tensor_scalar(ln.xn[g.p][:, t, :], src[:, t, :], ln.mv[g.p][:, t, 0:1],
                                         ln.rstd[g.p][:, t:t + 1], ALU.subtract, ALU.mult)
            last.then_inc(ln.xn_s, 1)

        class Norm:
            def __init__(self, name, own):
                two = lambda k, shape: [sb(f"{name}_{k}{p}", shape, to=own) for p in range(2)]
                self.stats, self.mv = two("stats", [128, G, 6]), two("mv", [128, G, 2])
                self.veps, self.rstd, self.xn = two("veps", [128, G]), two("rstd", [128, G]), two("xn", [128, G, D])
                self.stats_s, self.mv_s, self.veps_s, self.rstd_s, self.xn_s = (
                    sem(f"{name}_{k}") for k in ("stats", "mv", "veps", "rstd", "xn"))

        def rows(x, g):
            return x[bass.ds(g.n * G, G)].rearrange("b t d -> t b d")

        def project():
            KEYS = 2
            filled = sem("pj_filled")
            x_in, c_in = [sem(f"pj_x_in{p}") for p in range(2)], [sem(f"pj_c_in{p}") for p in range(2)]
            c_turned, x_turned, c_kept, x_kept = sem("pj_c_turned"), sem("pj_x_turned"), sem("pj_c_kept"), sem("pj_x_kept")
            kq_ps, v_ps, ones = sem("pj_kq_ps"), sem("pj_v_ps"), sem("pj_ones")
            part0, rest0, part1, part2 = sem("pj_part0"), sem("pj_rest0"), sem("pj_part1"), sem("pj_part2")
            v_sum, v_part0, v_rest0, v_part1, v_part2 = (
                sem(f"pj_v_{k}") for k in ("sum", "part0", "rest0", "part1", "part2"))
            kq_out = [[sem(f"pj_kq_out{p}{i}") for i in range(3)] for p in range(2)]
            v_out = [[sem(f"pj_v_out{p}{l}") for l in range(2)] for p in range(2)]
            with ExitStack() as own, nc.Block() as block:
                two = lambda k, shape, dt=F32: [sb(f"pj_{k}{p}", shape, dt, own) for p in range(2)]
                ln = Norm("pj_ln", own)
                c_g, x_g, c_t, x_t = two("c", [128, G, D]), two("x", [128, G, D]), two("ct", [128, GT]), two("xt", [128, GT])
                parts = [[sb(f"pj_parts{p}{i}", [128, 3, GT], BF16, own) for i in range(3)] for p in range(2)]
                rest = [sb(f"pj_rest{i}", [128, GT], to=own) for i in range(3)]
                vals = [[sb(f"pj_vals{p}{l}", [128, G * H, VW], BF16, own) for l in range(2)] for p in range(2)]
                v_full = [sb(f"pj_vfull{l}", [128, G * H, DH], to=own) for l in range(2)]
                v_rest = [sb(f"pj_vrest{l}", [128, G * H, DH], to=own) for l in range(2)]
                ct_bank, xt_bank, kq_bank, v_bank = bank[0], bank[1], bank[2:5], bank[5:7]
                items = [(wk[0], bk[0], k_parts[0]), (wk[1], bk[1], k_parts[1]), (wq[0], bq[0], q_parts)]

                @block.sync
                def _(sp):
                    def load(g):
                        sp.wait_ge(c_turned, earlier(g.n - 1))
                        sp.dma_start(c_g[g.p][:], rows(a["ctx_1024"], g)).then_inc(c_in[g.p], 16)
                        sp.wait_ge(ln.xn_s, earlier(g.n - 1))
                        sp.dma_start(x_g[g.p][:], rows(a["x"], g)).then_inc(x_in[g.p], 16)

                    def store(g):
                        for i, (_, _, to) in enumerate(items):
                            sp.wait_ge(part2, g.n * 3 + i + 1)
                            sp.dma_start(to[:, :, bass.ds(g.n * GT, GT)].rearrange("c r t -> r c t"), parts[g.p][i][:]
                                         ).then_inc(kq_out[g.p][i], 16)
                        for l in range(2):
                            sp.wait_ge(v_part2, g.n * 2 + l + 1)
                            sp.dma_start(v_parts[l][bass.ds(g.n * G, G)].rearrange("b t c -> t b c"),
                                         vals[g.p][l][:].rearrange("t (b h) c -> t b (h c)", b=G)
                                         ).then_inc(v_out[g.p][l], 16)

                    def body(g, last=False):
                        if not last:
                            load(g.after().after().after())
                        store(g)
                    load(FIRST)
                    load(FIRST.after())
                    load(FIRST.after().after())
                    sp.dma_start(sorted_in.rearrange("(p n) d -> p (n d)", p=128), padding[:].rearrange("p n d -> p (n d)")
                                 ).then_inc(filled, 16)
                    sp.wait_ge(ones, 4)
                    body(FIRST)
                    with sp.Fori(0, NG // 2 - 2) as i:
                        body(Group(i, 1))
                        body(Group(i + 1, 0))
                    for g in (LAST.before().before(), LAST.before(), LAST):
                        body(g, last=True)
                    sp.wait_ge(filled, 16)
                    for p in range(2):
                        for s in kq_out[p] + v_out[p]:
                            sp.wait_ge(s, 16 * (NG // 2))

                @block.tensor
                def _(pe):
                    def turn(g):
                        pe.wait_ge(c_in[g.p], g.turn * 16 + 16)
                        pe.wait_ge(c_kept, earlier(g.n))
                        for t in range(G):
                            mm = pe.transpose(ct_bank[:, t * T:(t + 1) * T], c_g[g.p][:, t, :], ident[:])
                        mm.then_inc(c_turned, 1)
                        pe.wait_ge(ln.xn_s, g.n + 1)
                        pe.wait_ge(x_kept, earlier(g.n))
                        for t in range(G):
                            mm = pe.transpose(xt_bank[:, t * T:(t + 1) * T], ln.xn[g.p][:, t, :], ident[:])
                        mm.then_inc(x_turned, 1)

                    def products(g):
                        for i, (w, _, _) in enumerate(items):
                            if i < KEYS:
                                pe.wait_ge(c_kept, g.n + 1)
                            else:
                                pe.wait_ge(x_kept, g.n + 1)
                            pe.wait_ge(rest0, earlier((g.n - 1) * 3 + i + 1))
                            pe.matmul(kq_bank[i][:], w[:], (c_t if i < KEYS else x_t)[g.p][:], start=True, stop=True
                                      ).then_inc(kq_ps, 1)
                        for l in range(2):
                            pe.wait_ge(v_sum, earlier((g.n - 1) * 2 + l + 1))
                            for t in range(G):
                                mm = pe.matmul(v_bank[l][:, t * D:(t + 1) * D], c_t[g.p][:, t * T:(t + 1) * T], wv[l][:],
                                               start=True, stop=True)
                            mm.then_inc(v_ps, 1)

                    def body(g):
                        turn(g.after())
                        products(g)
                    turn(FIRST)
                    body(FIRST)
                    middle_groups(pe, body)
                    products(LAST)

                @block.scalar
                def _(act):
                    def keep(g):
                        act.wait_ge(c_turned, g.n + 1)
                        act.wait_ge(v_ps, earlier((g.n - 1) * 2))
                        act.copy(c_t[g.p][:], ct_bank[:]).then_inc(c_kept, 1)
                        act.wait_ge(x_turned, g.n + 1)
                        act.wait_ge(kq_ps, earlier((g.n - 1) * 3))
                        act.copy(x_t[g.p][:], xt_bank[:]).then_inc(x_kept, 1)

                    def first_parts(g):
                        for i, (_, b, _) in enumerate(items):
                            act.wait_ge(kq_ps, g.n * 3 + i + 1)
                            act.wait_ge(kq_out[g.p][i], earlier(g.turn * 16))
                            act.activation(parts[g.p][i][:, 0, :], kq_bank[i][:], ACT.Identity, bias=b[:]).then_inc(part0, 1)

                    def second_parts(g):
                        for i in range(3):
                            act.wait_ge(rest0, g.n * 3 + i + 1)
                            act.copy(parts[g.p][i][:, 1, :], rest[i][:]).then_inc(part1, 1)

                    def first_value_parts(g):
                        for l in range(2):
                            act.wait_ge(v_sum, g.n * 2 + l + 1)
                            act.wait_ge(v_out[g.p][l], earlier(g.turn * 16))
                            act.copy(vals[g.p][l][:, :, 0:DH], v_full[l][:]).then_inc(v_part0, 1)

                    def second_value_parts(g):
                        for l in range(2):
                            act.wait_ge(v_rest0, g.n * 2 + l + 1)
                            act.copy(vals[g.p][l][:, :, DH:2 * DH], v_rest[l][:]).then_inc(v_part1, 1)

                    def body(g, last=False):
                        if not last:
                            keep(g.after())
                        first_parts(g)
                        second_parts(g)
                        first_value_parts(g)
                        second_value_parts(g)
                    keep(FIRST)
                    body(FIRST)
                    middle_groups(act, body)
                    body(LAST, last=True)

                @block.vector
                def _(dve):
                    def stats(g):
                        dve.wait_ge(x_in[g.p], g.turn * 16 + 16)
                        row_stats(dve, g, x_g[g.p], ln)

                    def apply(g):
                        dve.wait_ge(x_turned, earlier(g.n - 1))
                        row_apply(dve, g, x_g[g.p], ln)

                    def rests(g):
                        for i, (_, b, _) in enumerate(items):
                            dve.wait_ge(part0, g.n * 3 + i + 1)
                            dve.wait_ge(part2, earlier((g.n - 1) * 3 + i + 1))
                            dve.scalar_tensor_tensor(out=rest[i][:], in0=kq_bank[i][:], scalar=b[:],
                                                     in1=parts[g.p][i][:, 0, :], op0=ALU.add, op1=ALU.subtract
                                                     ).then_inc(rest0, 1)

                    def values(g):
                        for l in range(2):
                            dve.wait_ge(v_ps, g.n * 2 + l + 1)
                            dve.wait_ge(v_part0, earlier((g.n - 1) * 2 + l + 1))
                            dve.tensor_tensor(
                                v_full[l][:], v_bank[l][:].rearrange("t (h d) -> t h d", d=DH),
                                bv[l][:].unsqueeze(1).broadcast_to([128, G, D]).rearrange("t b (h d) -> t b h d", d=DH),
                                ALU.add).then_inc(v_sum, 1)

                    def value_rests(g):
                        for l in range(2):
                            dve.wait_ge(v_part0, g.n * 2 + l + 1)
                            dve.wait_ge(v_part2, earlier((g.n - 1) * 2 + l + 1))
                            dve.tensor_tensor(v_rest[l][:], v_full[l][:], vals[g.p][l][:, :, 0:DH], ALU.subtract
                                              ).then_inc(v_rest0, 1)

                    for p in range(2):
                        for l in range(2):
                            dve.memset(vals[p][l][:, :, 3 * DH:VW], 1.0).then_inc(ones, 1)
                    for g in (FIRST, FIRST.after()):
                        stats(g)
                        apply(g)

                    def body(g, last=False):
                        if not last:
                            stats(g.after().after())
                        rests(g)
                        if not last:
                            apply(g.after().after())
                        values(g)
                        value_rests(g)
                    body(FIRST)
                    body(FIRST.after())
                    with dve.Fori(1, NG // 2 - 1) as i:
                        body(Group(i, 0))
                        body(Group(i, 1))
                    body(LAST.before(), last=True)
                    body(LAST, last=True)

                @block.gpsimd
                def _(pool):
                    def cut(g, i):
                        pool.wait_ge(part1, g.n * 3 + i + 1)
                        pool.tensor_tensor(parts[g.p][i][:, 2, :], rest[i][:], parts[g.p][i][:, 1, :], ALU.subtract
                                           ).then_inc(part2, 1)

                    def cut_values(g, l):
                        pool.wait_ge(v_part1, g.n * 2 + l + 1)
                        pool.tensor_tensor(vals[g.p][l][:, :, 2 * DH:3 * DH], v_rest[l][:], vals[g.p][l][:, :, DH:2 * DH],
                                           ALU.subtract).then_inc(v_part2, 1)

                    def body(g, last=False):
                        if not last:
                            row_rstd(pool, g.after().after(), ln)
                        cut(g, 0)
                        cut(g, 1)
                        cut(g, 2)
                        cut_values(g, 0)
                        cut_values(g, 1)
                    row_rstd(pool, FIRST, ln)
                    row_rstd(pool, FIRST.after(), ln)
                    body(FIRST)
                    body(FIRST.after())
                    with pool.Fori(1, NG // 2 - 1) as i:
                        body(Group(i, 0))
                        body(Group(i, 1))
                    body(LAST.before(), last=True)
                    body(LAST, last=True)

        def attention(l, x_src, x_dst):
            causal = l == 1
            scale = DH ** -0.5
            s = lambda name: sem(f"a{l}_{name}")
            qk_in, vx_in, mt_in, x_out = ([s(f"{k}{p}") for p in range(2)] for k in ("qk_in", "vx_in", "mt_in", "x_out"))
            s_ps, max_s, hi_s, split_s = s("s_ps"), s("max"), s("hi"), s("split")
            mt_ps, mt_s = s("mt_ps"), s("mt")
            st_ps, exp_s, masked_s, pv_s = s("st_ps"), s("exp"), s("masked"), s("pv")
            folded_s, high_s, low_s = s("folded"), s("high"), [s(f"low{c}") for c in range(NC)]
            ot_s, oq_ps, rec_s, norm_s, on_ps, on_s = s("ot"), s("oq_ps"), s("rec"), s("norm"), s("on_ps"), s("on")
            y_ps, y_s, biased_s, zero_s = s("y_ps"), s("y"), s("biased"), s("zero")
            pool_cuts = (1, 3) if causal else (1, 2, 3)
            QK_IN, VX_IN = 16 * 2 * len(Q_PARTS), 16 * 2
            with ExitStack() as own, nc.Block() as block:
                vv = [sb(f"vv{l}{p}", [128, G, H * VW], BF16, own) for p in range(2)]
                xx = [sb(f"xx{l}{p}", [128, G, D], to=own) for p in range(2)]
                neg_max = [sb(f"nm{l}{p}", [128, H], to=own) for p in range(2)]
                max_parts = [sb(f"mp{l}{p}", [128, 2 * H], BF16, own) for p in range(2)]
                max_t = [sb(f"mt{l}{p}", [2 * H, T], BF16, own) for p in range(2)]
                probs = [sb(f"pr{l}{c}", [128, C4 * T], to=own) for c in range(NC)]
                high = [[sb(f"ph{l}{p}{c}", [128, C4 * T], FP16, own) for c in range(NC)] for p in range(2)]
                low = [[sb(f"pl{l}{p}{c}", [128, C4 * T], FP16, own) for c in range(NC)] for p in range(2)]
                o_t = [sb(f"ot{l}{p}", [128, C4 * T], to=own) for p in range(2)]
                rec = [sb(f"rc{l}{p}", [128, H], to=own) for p in range(2)]
                o_sum = [sb(f"os{l}{p}", [128, H, DH], to=own) for p in range(2)]
                o_n = [sb(f"on{l}{p}", [128, D], to=own) for p in range(2)]
                o_nt = [sb(f"ont{l}{p}", [128, T], to=own) for p in range(2)]
                s_bank, st_bank, o_bank, oq_bank, m_bank = bank[0:2], bank[2:4], bank[4:6], bank[6], bank[7]
                max_bank = m_bank[0:2 * H, 0:T // 2].bitcast(BF16)

                @block.sync
                def _(sp):
                    def load_qk(g):
                        sp.wait_ge(st_ps, earlier((g.n - 1) * G * NC))
                        for side, src, which in ((qq, q_parts, Q_PARTS), (kk, k_parts[l], K_PARTS)):
                            for r, part in enumerate(which):
                                sp.dma_start(side[g.p][r * DH:(r + 1) * DH, :, :],
                                             src[part].rearrange("(h d) t -> d h t", d=DH)[:, :, bass.ds(g.n * GT, GT)]
                                             ).then_inc(qk_in[g.p], 16)

                    def load_vx(g):
                        sp.wait_ge(pv_s, earlier((g.n - 1) * G * NC))
                        sp.dma_start(vv[g.p][:], v_parts[l][bass.ds(g.n * G, G)].rearrange("b t c -> t b c")
                                     ).then_inc(vx_in[g.p], 16)
                        sp.wait_ge(x_out[g.p], earlier(g.turn * 16))
                        sp.dma_start(xx[g.p][:], x_src[bass.ds(g.n * G, G)].rearrange("b t d -> t b d")
                                     ).then_inc(vx_in[g.p], 16)

                    def store(g):
                        sp.wait_ge(y_s, (g.n + 1) * G)
                        sp.dma_start(x_dst[bass.ds(g.n * G, G)].rearrange("b t d -> t b d"), xx[g.p][:]
                                     ).then_inc(x_out[g.p], 16)

                    def place_maxima(q):
                        sp.wait_ge(mt_s, q.m + 1)
                        sp.dma_start(qq[q.g.p][MAX_ROW:ROWS, :, q.b * T:(q.b + 1) * T], max_t[q.p][:]
                                     ).then_inc(mt_in[q.p], 16)

                    def body(g, first=False, last=False):
                        for b in range(G):
                            if not (last and b + 1 >= G):
                                place_maxima(Seq(g, b).ahead(1))
                            if b == 0 and not last:
                                load_qk(g.after())
                            if b == 2 and not first:
                                store(g.before())
                            if b == 3 and not last:
                                load_vx(g.after())

                    load_qk(FIRST)
                    load_vx(FIRST)
                    place_maxima(Seq(FIRST, 0))
                    body(FIRST, first=True)
                    middle_groups(sp, body)
                    body(LAST, last=True)
                    store(LAST)
                    for p in range(2):
                        sp.wait_ge(x_out[p], 16 * (NG // 2))

                @block.tensor
                def _(pe):
                    def scores(q, c):
                        if c == 0 and q.b == 0:
                            pe.wait_ge(qk_in[q.g.p], (q.g.turn + 1) * QK_IN)
                        pe.wait_ge(max_s, earlier(q.m * NC + c - 1))
                        to, t = s_bank[c % 2], slice(q.b * T, (q.b + 1) * T)
                        if causal:
                            pe.matmul(to[:], future[:], ident4[:].rearrange("p a b -> p (a b)"), start=True, stop=True)
                        for j in range(C4):
                            mm = pe.matmul(to[:, j * T:(j + 1) * T], qq[q.g.p][0:MAX_ROW, c * C4 + j, t],
                                           kk[q.g.p][0:MAX_ROW, c * C4 + j, t], start=not causal, stop=True,
                                           skip_group_check=causal)
                        mm.then_inc(s_ps, 1)

                    def turn_maxima(q):
                        pe.wait_ge(split_s, q.m + 1)
                        pe.wait_ge(mt_s, earlier(q.m))
                        pe.wait_ge(y_s, earlier(q.m - 3))
                        pe.transpose(max_bank, max_parts[q.p][:], ident4[:, 0, :]).then_inc(mt_ps, 1)

                    def scores_t(q, c):
                        if c == 0:
                            pe.wait_ge(mt_in[q.p], (q.turn + 1) * 16)
                        pe.wait_ge(exp_s if causal else high_s, earlier(q.m * NC + c - 1))
                        t = slice(q.b * T, (q.b + 1) * T)
                        for j in range(C4):
                            mm = pe.matmul(st_bank[c % 2][:, j * T:(j + 1) * T], kk[q.g.p][0:ROWS, c * C4 + j, t],
                                           qq[q.g.p][0:ROWS, c * C4 + j, t], start=True, stop=True)
                        mm.then_inc(st_ps, 1)

                    def mix(q, c):
                        if c == 0 and q.b == 0:
                            pe.wait_ge(vx_in[q.g.p], (q.g.turn + 1) * VX_IN)
                        if c == 0:
                            pe.wait_ge(ot_s, earlier(q.m - 1))
                        pe.wait_ge(low_s[c], q.m + 1)
                        for j in range(C4):
                            h = c * C4 + j
                            for k, part in enumerate((high, low)):
                                mm = pe.matmul(o_bank[q.p][32 * j:32 * j + VW, c * T:(c + 1) * T],
                                               vv[q.g.p][:, q.b, h * VW:(h + 1) * VW], part[q.p][c][:, j * T:(j + 1) * T],
                                               start=(k == 0), stop=(k == 1))
                        mm.then_inc(pv_s, 1)

                    def turn_output(q):
                        pe.wait_ge(ot_s, q.m + 1)
                        pe.wait_ge(norm_s, earlier(q.m))
                        for c in range(NC):
                            mm = pe.transpose(oq_bank[:, c * T:(c + 1) * T], o_t[q.p][:, c * T:(c + 1) * T], ident[:])
                        mm.then_inc(oq_ps, 1)

                    def turn_normalised(q):
                        pe.wait_ge(norm_s, q.m + 1)
                        pe.wait_ge(mt_s, min(q.m + 4, B) if isinstance(q.m, int) else q.m + 4)
                        pe.transpose(m_bank[:, 0:T], o_n[q.p][:], ident[:]).then_inc(on_ps, 1)

                    def project(q):
                        pe.wait_ge(on_s, q.m + 1)
                        pe.matmul(m_bank[:, 0:D], o_nt[q.p][:], wo[l][:], start=True, stop=True).then_inc(y_ps, 1)

                    def body(g, first=False, last=False):
                        for b in range(G):
                            q = Seq(g, b)
                            past = None if first and b < 1 else q.ahead(-1)
                            before_past = None if first and b < 2 else q.ahead(-2)
                            following = None if last and b + 1 >= G else q.ahead(1)
                            to_come = None if last and b + 2 >= G else q.ahead(2)
                            for c in range(NC):
                                scores_t(q, c)
                                if to_come:
                                    scores(to_come, c)
                                if past:
                                    mix(past, c)
                                if c == 0 and following:
                                    turn_maxima(following)
                                if c == 0 and before_past:
                                    turn_output(before_past)
                                if c == 2 and before_past:
                                    turn_normalised(before_past)
                                if c == 3 and before_past:
                                    project(before_past)

                    pe.wait_ge(zero_s, 2)
                    for b in range(2):
                        for c in range(NC):
                            scores(Seq(FIRST, b), c)
                        if b == 0:
                            turn_maxima(Seq(FIRST, b))
                    body(FIRST, first=True)
                    middle_groups(pe, body)
                    body(LAST, last=True)
                    for c in range(NC):
                        mix(Seq(LAST, G - 1), c)
                    for b in (G - 2, G - 1):
                        turn_output(Seq(LAST, b))
                        turn_normalised(Seq(LAST, b))
                        project(Seq(LAST, b))

                @block.scalar
                def _(act):
                    def exponential(q, c):
                        act.wait_ge(st_ps, q.m * NC + c + 1)
                        act.wait_ge(low_s[c], earlier(q.m))
                        act.activation(probs[c][:], st_bank[c % 2][:], ACT.Exp, scale=scale).then_inc(exp_s, 1)

                    def high_part(q, c):
                        if causal:
                            act.wait_ge(masked_s, q.m * NC + c + 1)
                        act.wait_ge(pv_s, earlier((q.m - 2) * NC + c + 1))
                        if causal:
                            act.copy(high[q.p][c][:], probs[c][:]).then_inc(high_s, 1)
                        else:
                            act.activation(high[q.p][c][:], st_bank[c % 2][:], ACT.Exp, scale=scale).then_inc(high_s, 1)

                    def keep_output(q):
                        act.wait_ge(pv_s, (q.m + 1) * NC)
                        act.wait_ge(oq_ps, earlier(q.m - 1))
                        act.copy(o_t[q.p][:], o_bank[q.p][:]).then_inc(ot_s, 1)

                    def keep_normalised(q):
                        act.wait_ge(on_ps, q.m + 1)
                        act.wait_ge(y_ps, earlier(q.m - 1))
                        act.copy(o_nt[q.p][:], m_bank[:, 0:T]).then_inc(on_s, 1)

                    def keep_maxima(q):
                        act.wait_ge(mt_ps, q.m + 1)
                        act.wait_ge(mt_in[q.p], earlier(q.turn * 16))
                        act.copy(max_t[q.p][:], max_bank).then_inc(mt_s, 1)

                    def body(g, first=False, last=False):
                        for b in range(G):
                            q = Seq(g, b)
                            past = None if first and b < 1 else q.ahead(-1)
                            before_past = None if first and b < 2 else q.ahead(-2)
                            if before_past:
                                keep_output(before_past)
                            exponential(q, 0)
                            if not causal:
                                high_part(q, 0)
                            elif past:
                                high_part(past, NC - 1)
                            if not (last and b + 1 >= G):
                                keep_maxima(q.ahead(1))
                            for c in range(1, NC):
                                exponential(q, c)
                                high_part(q, c - 1 if causal else c)
                                if c == 2 and before_past:
                                    keep_normalised(before_past)

                    keep_maxima(Seq(FIRST, 0))
                    body(FIRST, first=True)
                    middle_groups(act, body)
                    body(LAST, last=True)
                    if causal:
                        high_part(Seq(LAST, G - 1), NC - 1)
                    for b in (G - 2, G - 1):
                        keep_output(Seq(LAST, b))
                        keep_normalised(Seq(LAST, b))

                @block.vector
                def _(dve):
                    def reduce_chunk(q, c):
                        dve.wait_ge(s_ps, q.m * NC + c + 1)
                        if c == 0:
                            dve.wait_ge(split_s, earlier(q.m - 1))
                        dve.tensor_reduce(neg_max[q.p][:, c * C4:(c + 1) * C4],
                                          s_bank[c % 2][:].rearrange("q (h k) -> q h k", h=C4), AX_X, ALU.max,
                                          negate=True).then_inc(max_s, 1)

                    def cut_maxima(q):
                        dve.wait_ge(max_s, (q.m + 1) * NC)
                        dve.wait_ge(mt_ps, earlier(q.m - 1))
                        dve.tensor_copy(max_parts[q.p][:, 0:H], neg_max[q.p][:]).then_inc(hi_s, 1)
                        dve.wait_ge(hi_s, q.m + 1)
                        dve.tensor_tensor(max_parts[q.p][:, H:2 * H], neg_max[q.p][:], max_parts[q.p][:, 0:H],
                                          ALU.subtract).then_inc(split_s, 1)

                    def normalise(q):
                        view = oq_bank[:].rearrange("q (h w) -> q h w", w=32)
                        dve.wait_ge(oq_ps, q.m + 1)
                        dve.tensor_reduce(o_sum[q.p][:], view[:, :, 0:3 * DH].rearrange("q h (s d) -> q h d s", d=DH),
                                          AX_X, ALU.add).then_inc(folded_s, 1)
                        dve.reciprocal(rec[q.p][:].unsqueeze(2), view[:, :, 3 * DH:VW]).then_inc(rec_s, 1)
                        dve.wait_ge(folded_s, q.m + 1)
                        dve.wait_ge(rec_s, q.m + 1)
                        dve.wait_ge(on_ps, earlier(q.m - 1))
                        dve.tensor_tensor(o_n[q.p][:].rearrange("q (h d) -> q h d", d=DH), o_sum[q.p][:],
                                          rec[q.p][:].unsqueeze(2).broadcast_to([128, H, DH]), ALU.mult
                                          ).then_inc(norm_s, 1)

                    def add(q):
                        dve.wait_ge(y_ps, q.m + 1)
                        dve.wait_ge(biased_s, q.g.n + 1)
                        rows = xx[q.g.p][:, q.b, :]
                        dve.tensor_tensor(rows, m_bank[:, 0:D], rows, ALU.add).then_inc(y_s, 1)

                    def low_part(q, c):
                        dve.wait_ge(high_s, q.m * NC + c + 1)
                        dve.tensor_tensor(low[q.p][c][:], probs[c][:], high[q.p][c][:], ALU.subtract).then_inc(low_s[c], 1)

                    def body(g, first=False, last=False):
                        for b in range(G):
                            q = Seq(g, b)
                            past = None if first and b < 1 else q.ahead(-1)
                            before_past = None if first and b < 2 else q.ahead(-2)
                            to_come = None if last and b + 2 >= G else q.ahead(2)
                            if to_come:
                                reduce_chunk(to_come, 0)
                            if causal and past:
                                low_part(past, NC - 1)
                            if before_past:
                                normalise(before_past)
                            if to_come:
                                reduce_chunk(to_come, 1)
                            for c in range(NC - causal):
                                if c in (1, 2) and to_come:
                                    reduce_chunk(to_come, c + 1)
                                if c == 2 and to_come:
                                    cut_maxima(to_come)
                                if c not in pool_cuts:
                                    low_part(q, c)
                            if before_past:
                                add(before_past)

                    for p in range(2):
                        dve.memset(o_bank[p][:], 0.0).then_inc(zero_s, 1)
                    for b in range(2):
                        for c in range(NC):
                            reduce_chunk(Seq(FIRST, b), c)
                        cut_maxima(Seq(FIRST, b))
                    body(FIRST, first=True)
                    middle_groups(dve, body)
                    body(LAST, last=True)
                    if causal:
                        low_part(Seq(LAST, G - 1), NC - 1)
                    for b in (G - 2, G - 1):
                        normalise(Seq(LAST, b))
                        add(Seq(LAST, b))

                @block.gpsimd
                def _(pool):
                    def bias(g):
                        pool.wait_ge(vx_in[g.p], (g.turn + 1) * VX_IN)
                        pool.tensor_tensor(xx[g.p][:], xx[g.p][:], bo[l][:].unsqueeze(1).broadcast_to([128, G, D]),
                                           ALU.add).then_inc(biased_s, 1)

                    def mask(q, c):
                        pool.wait_ge(exp_s, q.m * NC + c + 1)
                        pool.tensor_tensor(pool_cell[:, c:c + 1], epsilon[:, 0:1], epsilon[:, 0:1], ALU.mult)
                        pool.affine_select(out=probs[c][:], in_=probs[c][:], compare_op=ALU.is_ge, fill=0.0, base=0,
                                           pattern=[[0, C4], [1, T]], channel_multiplier=-1).then_inc(masked_s, 1)

                    def low_part(q, c):
                        pool.wait_ge(high_s, q.m * NC + c + 1)
                        pool.tensor_tensor(low[q.p][c][:], probs[c][:], high[q.p][c][:], ALU.subtract).then_inc(low_s[c], 1)

                    def body(g):
                        for b in range(G):
                            for c in range(NC):
                                if causal:
                                    mask(Seq(g, b), c)
                                if c - causal in pool_cuts:
                                    low_part(Seq(g, b), c - causal)
                            if b == 0:
                                bias(g)
                    all_groups(pool, body)

        def experts0(x_src, x_dst):
            s = lambda name: sem(f"e0_{name}")
            x_in, x_out, q_out = ([s(f"{k}{p}") for p in range(2)] for k in ("x_in", "x_out", "q_out"))
            sum_s, turned, kept, sc_ps = s("sum"), s("turned"), s("kept"), s("sc_ps")
            top_s, tie_s, rank_s, best_s, hot_s = s("top"), s("tie"), s("rank"), s("best"), s("hot")
            hot_ps, chosen_s, y_ps, y_s, z_ps, z_s = s("hot_ps"), s("chosen"), s("y_ps"), s("y"), s("z_ps"), s("z")
            q_turned, q_kept, q_ps = s("q_turned"), s("q_kept"), s("q_ps")
            part0, rest0, part1, part2 = s("part0"), s("rest0"), s("part1"), s("part2")
            with ExitStack() as own, nc.Block() as block:
                two = lambda name, shape, dt=F32: [sb(f"e0{name}{p}", shape, dt, own) for p in range(2)]
                ln, q_ln = Norm("e0_ln", own), Norm("e0_qln", own)
                x_g, x_sum, xn_t, q_t = (two(k, [128, G * D]) for k in ("x", "xs", "xt", "qt"))
                top, best = two("top", [128, G]), two("best", [128, G])
                tie, ranked = two("tie", [128, G, E]), two("rk", [128, G, E])
                hot = two("hot", [128, G, E], BF16)
                chosen, y_t = two("ch", [128, GT]), sb("e0y", [128, GT], to=own)
                parts, rest = two("parts", [128, 3, GT], BF16), sb("e0rest", [128, GT], to=own)
                t_bank, sc_bank, hot_bank, y_bank, z_bank, qt_bank, q_bank = (
                    bank[0], bank[1], bank[2:4], bank[4], bank[5], bank[6], bank[7])

                def by_seq(tile):
                    return tile[:].rearrange("t (g d) -> t g d", g=G)

                @block.sync
                def _(sp):
                    def load(g):
                        sp.wait_ge(sum_s, earlier(g.n - 1))
                        sp.dma_start(by_seq(x_g[g.p]), rows(x_src, g)).then_inc(x_in[g.p], 16)

                    def store(g):
                        sp.wait_ge(z_s, g.n + 1)
                        sp.dma_start(rows(x_dst, g), by_seq(x_sum[g.p])).then_inc(x_out[g.p], 16)

                    def store_queries(g):
                        sp.wait_ge(part2, g.n + 1)
                        sp.dma_start(q_parts[:, :, bass.ds(g.n * GT, GT)].rearrange("c r t -> r c t"), parts[g.p][:]
                                     ).then_inc(q_out[g.p], 16)

                    load(FIRST)
                    load(FIRST.after())
                    store(FIRST)

                    def body(g):
                        load(g.after())
                        store_queries(g.before())
                        store(g)
                    middle_groups(sp, body)
                    store_queries(LAST.before())
                    store(LAST)
                    store_queries(LAST)
                    for p in range(2):
                        sp.wait_ge(x_out[p], 16 * (NG // 2))
                        sp.wait_ge(q_out[p], 16 * (NG // 2))

                @block.gpsimd
                def _(pool):
                    def add_rows(g):
                        pool.wait_ge(ln.xn_s, g.n + 1)
                        pool.wait_ge(q_ln.xn_s, earlier(g.n - 1))
                        pool.wait_ge(x_out[g.p], earlier(g.turn * 16))
                        pool.tensor_tensor(x_sum[g.p][:], x_g[g.p][:], ln.xn[g.p][:].rearrange("t g d -> t (g d)"), ALU.add
                                           ).then_inc(sum_s, 1)

                    def cut(g):
                        pool.wait_ge(part1, g.n + 1)
                        pool.tensor_tensor(parts[g.p][:, 2, :], rest[:], parts[g.p][:, 1, :], ALU.subtract).then_inc(part2, 1)

                    row_rstd(pool, FIRST, ln)
                    add_rows(FIRST)
                    row_rstd(pool, FIRST.after(), ln)
                    add_rows(FIRST.after())

                    def body(g, last=False):
                        row_rstd(pool, g.before(), q_ln)
                        if not last:
                            row_rstd(pool, g.after(), ln)
                            add_rows(g.after())
                        cut(g.before())
                    middle_groups(pool, body)
                    body(LAST, last=True)
                    row_rstd(pool, LAST, q_ln)
                    cut(LAST)

                @block.vector
                def _(dve):
                    def stats(g):
                        dve.wait_ge(x_in[g.p], g.turn * 16 + 16)
                        row_stats(dve, g, by_seq(x_g[g.p]), ln)

                    def apply(g):
                        dve.wait_ge(turned, earlier(g.n - 1))
                        dve.wait_ge(sum_s, earlier(g.n - 1))
                        row_apply(dve, g, by_seq(x_g[g.p]), ln)

                    def route(g):
                        view, p = sc_bank[:, 0:G * E].rearrange("t (g e) -> t g e", e=E), g.p
                        dve.wait_ge(sc_ps, g.n + 1)
                        dve.tensor_reduce(top[p][:], view, AX_X, ALU.max).then_inc(top_s, 1)
                        dve.wait_ge(top_s, g.n + 1)
                        dve.tensor_tensor(tie[p][:], view, top[p][:].unsqueeze(2).broadcast_to([128, G, E]), ALU.is_ge
                                          ).then_inc(tie_s, 1)
                        dve.wait_ge(tie_s, g.n + 1)
                        dve.tensor_tensor(ranked[p][:], tie[p][:], rank[:], ALU.mult).then_inc(rank_s, 1)
                        dve.wait_ge(rank_s, g.n + 1)
                        dve.tensor_reduce(best[p][:], ranked[p][:], AX_X, ALU.max).then_inc(best_s, 1)
                        dve.wait_ge(best_s, g.n + 1)
                        dve.wait_ge(hot_ps, earlier((g.n - 1) * E))
                        dve.tensor_tensor(hot[p][:], ranked[p][:], best[p][:].unsqueeze(2).broadcast_to([128, G, E]),
                                          ALU.is_equal).then_inc(hot_s, 1)

                    def choose(g, e):
                        dve.wait_ge(hot_ps, g.n * E + e + 1)
                        dve.wait_ge(y_ps, earlier(g.n * E + e - 1))
                        dve.tensor_tensor(chosen[e % 2][:], hot_bank[e % 2][:], xn_t[g.p][:], ALU.mult).then_inc(chosen_s, 1)

                    def add(g):
                        dve.wait_ge(z_ps, g.n + 1)
                        dve.wait_ge(sum_s, g.n + 1)
                        dve.tensor_tensor(x_sum[g.p][:], z_bank[:], x_sum[g.p][:], ALU.add).then_inc(z_s, 1)

                    def query_stats(g):
                        dve.wait_ge(z_s, g.n + 1)
                        row_stats(dve, g, by_seq(x_sum[g.p]), q_ln)

                    def query_apply(g):
                        dve.wait_ge(q_turned, earlier(g.n))
                        row_apply(dve, g, by_seq(x_sum[g.p]), q_ln)

                    def query_rest(g):
                        dve.wait_ge(part0, g.n + 1)
                        dve.wait_ge(part2, earlier(g.n))
                        dve.scalar_tensor_tensor(out=rest[:], in0=q_bank[:], scalar=bq[1][:], in1=parts[g.p][:, 0, :],
                                                 op0=ALU.add, op1=ALU.subtract).then_inc(rest0, 1)

                    def body(g, first=False, last=False):
                        choose(g, 0)
                        if not first:
                            query_stats(g.before())
                        choose(g, 1)
                        if not last:
                            stats(g.after())
                        choose(g, 2)
                        if not first:
                            query_apply(g.before())
                        choose(g, 3)
                        if not last:
                            apply(g.after())
                        choose(g, 4)
                        choose(g, 5)
                        if not first:
                            query_rest(g.before())
                        choose(g, 6)
                        choose(g, 7)
                        if not last:
                            route(g.after())
                        add(g)

                    stats(FIRST)
                    apply(FIRST)
                    route(FIRST)
                    body(FIRST, first=True)
                    middle_groups(dve, body)
                    body(LAST, last=True)
                    query_stats(LAST)
                    query_apply(LAST)
                    query_rest(LAST)

                @block.tensor
                def _(pe):
                    def turn(g):
                        pe.wait_ge(ln.xn_s, g.n + 1)
                        pe.wait_ge(kept, earlier(g.n))
                        for t in range(G):
                            mm = pe.transpose(t_bank[:, t * T:(t + 1) * T], ln.xn[g.p][:, t, :], ident[:])
                        mm.then_inc(turned, 1)

                    def score(g):
                        pe.wait_ge(kept, g.n + 1)
                        pe.wait_ge(tie_s, earlier(g.n))
                        for t in range(G):
                            mm = pe.matmul(sc_bank[:, t * E:(t + 1) * E], xn_t[g.p][:, t * T:(t + 1) * T], gate0_w[:],
                                           start=True, stop=True)
                        mm.then_inc(sc_ps, 1)

                    def spread(g, e):
                        if e == 0:
                            pe.wait_ge(hot_s, g.n + 1)
                        pe.wait_ge(chosen_s, earlier(g.n * E + e - 1))
                        for t in range(G):
                            mm = pe.matmul(hot_bank[e % 2][:, t * T:(t + 1) * T],
                                           hot[g.p][:, t, e:e + 1].broadcast_to([128, 128]), ident4[:, 0, :],
                                           start=True, stop=True)
                        mm.then_inc(hot_ps, 1)

                    def expert(g, e):
                        pe.wait_ge(chosen_s, g.n * E + e + 1)
                        if e == 0:
                            pe.wait_ge(y_s, earlier(g.n))
                        pe.matmul(y_bank[:], expert0_w[:, e, :], chosen[e % 2][:], start=(e == 0), stop=(e == E - 1)
                                  ).then_inc(y_ps, 1)

                    def turn_back(g):
                        pe.wait_ge(y_s, g.n + 1)
                        pe.wait_ge(z_s, earlier(g.n))
                        for t in range(G):
                            mm = pe.transpose(z_bank[:, t * T:(t + 1) * T], y_t[:, t * T:(t + 1) * T], ident[:])
                        mm.then_inc(z_ps, 1)

                    def turn_queries(g):
                        pe.wait_ge(q_ln.xn_s, g.n + 1)
                        pe.wait_ge(q_kept, earlier(g.n))
                        for t in range(G):
                            mm = pe.transpose(qt_bank[:, t * T:(t + 1) * T], q_ln.xn[g.p][:, t, :], ident[:])
                        mm.then_inc(q_turned, 1)

                    def queries(g):
                        pe.wait_ge(q_kept, g.n + 1)
                        pe.wait_ge(rest0, earlier(g.n))
                        pe.matmul(q_bank[:], wq[1][:], q_t[g.p][:], start=True, stop=True).then_inc(q_ps, 1)

                    def body(g, first=False, last=False):
                        if first:
                            spread(g, 0)
                        spread(g, 1)
                        for e in range(E):
                            expert(g, e)
                            if e + 2 < E:
                                spread(g, e + 2)
                            if e == 3 and not first:
                                turn_queries(g.before())
                            if e == 4 and not first:
                                queries(g.before())
                            if e == 4 and not last:
                                turn(g.after())
                            if e == 6 and not last:
                                score(g.after())
                        turn_back(g)
                        if not last:
                            spread(g.after(), 0)

                    turn(FIRST)
                    score(FIRST)
                    body(FIRST, first=True)
                    middle_groups(pe, body)
                    body(LAST, last=True)
                    turn_queries(LAST)
                    queries(LAST)

                @block.scalar
                def _(act):
                    def keep_turned(g):
                        act.wait_ge(turned, g.n + 1)
                        act.wait_ge(sc_ps, earlier(g.n - 1))
                        act.wait_ge(chosen_s, earlier((g.n - 1) * E))
                        act.copy(xn_t[g.p][:], t_bank[:]).then_inc(kept, 1)

                    def keep_sum(g):
                        act.wait_ge(y_ps, (g.n + 1) * E)
                        act.wait_ge(z_ps, earlier(g.n))
                        act.copy(y_t[:], y_bank[:]).then_inc(y_s, 1)

                    def query_parts(g):
                        act.wait_ge(q_ps, g.n + 1)
                        act.wait_ge(q_out[g.p], earlier(g.turn * 16))
                        act.activation(parts[g.p][:, 0, :], q_bank[:], ACT.Identity, bias=bq[1][:]).then_inc(part0, 1)

                    def query_second(g):
                        act.wait_ge(rest0, g.n + 1)
                        act.copy(parts[g.p][:, 1, :], rest[:]).then_inc(part1, 1)

                    def keep_queries(g):
                        act.wait_ge(q_turned, g.n + 1)
                        act.wait_ge(q_ps, earlier(g.n))
                        act.copy(q_t[g.p][:], qt_bank[:]).then_inc(q_kept, 1)

                    def body(g, first=False, last=False):
                        if not first:
                            keep_queries(g.before())
                            query_parts(g.before())
                        if not last:
                            keep_turned(g.after())
                        if not first:
                            query_second(g.before())
                        keep_sum(g)

                    keep_turned(FIRST)
                    body(FIRST, first=True)
                    middle_groups(act, body)
                    body(LAST, last=True)
                    keep_queries(LAST)
                    query_parts(LAST)
                    query_second(LAST)

        def experts1(x_src, x_dst):
            s = lambda name: sem(f"e1_{name}")
            with ExitStack() as own:
                gate_w, up_w = sb("gate_w", [128, E, F], to=own), sb("up_w", [128, E, F], to=own)
                down_w = sb("down_w", [128, E, len(FCH), D], to=own)
                router_w = sb("router_w", [128, E], to=own)
                tile_expert = sb("tile_expert", [128, SLOTS], I32, own)
                w_in, router_in = s("w_in"), s("router_in")
                score_rows(x_src, own, router_w, router_in)
                place_rows(tile_expert)
                sort_rows(gate_w, up_w, down_w, w_in)
                run_experts(gate_w, up_w, down_w, w_in, tile_expert)
                combine(x_src, x_dst)

        def score_rows(x_src, own, router_w, router_in):
            s = lambda name: sem(f"sr_{name}")
            x_in, n_out, sc_out = ([s(f"{k}{p}") for p in range(2)] for k in ("x_in", "n_out", "sc_out"))
            turned, kept, sc_ps, sc_s = s("turned"), s("kept"), s("sc_ps"), s("sc")
            with ExitStack() as mine, nc.Block() as block:
                two = lambda name, shape, dt=F32: [sb(f"sr{name}{p}", shape, dt, mine) for p in range(2)]
                ln = Norm("sr_ln", mine)
                x_g, xn_t, sc = two("x", [128, G, D]), two("xt", [128, GT]), two("sc", [128, G * E])
                t_bank, sc_bank = bank[0:2], bank[2:4]

                @block.sync
                def _(sp):
                    def load(g):
                        sp.wait_ge(ln.xn_s, earlier(g.n - 1))
                        sp.dma_start(x_g[g.p][:], rows(x_src, g)).then_inc(x_in[g.p], 16)

                    def store(g):
                        sp.wait_ge(ln.xn_s, g.n + 1)
                        sp.dma_start(rows(x_norm, g), ln.xn[g.p][:]).then_inc(n_out[g.p], 16)

                    def store_scores(g):
                        sp.wait_ge(sc_s, g.n + 1)
                        sp.dma_start(scores_d[:, bass.ds(g.n * G * E, G * E)], sc[g.p][:]).then_inc(sc_out[g.p], 16)

                    def body(g, first=False, last=False):
                        store(g)
                        if not last:
                            load(g.after().after())
                        if not first:
                            store_scores(g.before())
                    load(FIRST)
                    load(FIRST.after())
                    sp.dma_start(router_w[:], a["L1_ffn_router_w"]).then_inc(router_in, 16)
                    body(FIRST, first=True)
                    body(FIRST.after())
                    with sp.Fori(1, NG // 2 - 1) as i:
                        body(Group(i, 0))
                        body(Group(i, 1))
                    body(LAST.before(), last=True)
                    store(LAST)
                    store_scores(LAST.before())
                    store_scores(LAST)
                    for p in range(2):
                        sp.wait_ge(n_out[p], 16 * (NG // 2))
                        sp.wait_ge(sc_out[p], 16 * (NG // 2))

                @block.gpsimd
                def _(pool):
                    all_groups(pool, lambda g: row_rstd(pool, g, ln))

                @block.vector
                def _(dve):
                    def stats(g):
                        dve.wait_ge(x_in[g.p], g.turn * 16 + 16)
                        row_stats(dve, g, x_g[g.p], ln)

                    def apply(g):
                        dve.wait_ge(turned, earlier(g.n - 1))
                        dve.wait_ge(n_out[g.p], earlier(g.turn * 16))
                        row_apply(dve, g, x_g[g.p], ln)

                    def body(g):
                        stats(g.after())
                        apply(g)
                    stats(FIRST)
                    body(FIRST)
                    middle_groups(dve, body)
                    apply(LAST)

                @block.tensor
                def _(pe):
                    def turn(g):
                        pe.wait_ge(ln.xn_s, g.n + 1)
                        pe.wait_ge(kept, earlier(g.n - 1))
                        for t in range(G):
                            mm = pe.transpose(t_bank[g.p][:, t * T:(t + 1) * T], ln.xn[g.p][:, t, :], ident[:])
                        mm.then_inc(turned, 1)

                    def score(g):
                        pe.wait_ge(kept, g.n + 1)
                        pe.wait_ge(sc_s, earlier(g.n - 1))
                        for t in range(G):
                            mm = pe.matmul(sc_bank[g.p][:, t * E:(t + 1) * E], xn_t[g.p][:, t * T:(t + 1) * T], router_w[:],
                                           start=True, stop=True)
                        mm.then_inc(sc_ps, 1)

                    def body(g):
                        turn(g.after())
                        score(g)
                    pe.wait_ge(router_in, 16)
                    turn(FIRST)
                    body(FIRST)
                    middle_groups(pe, body)
                    score(LAST)

                @block.scalar
                def _(act):
                    def keep_turned(g):
                        act.wait_ge(turned, g.n + 1)
                        act.wait_ge(sc_ps, earlier(g.n - 1))
                        act.copy(xn_t[g.p][:], t_bank[g.p][:]).then_inc(kept, 1)

                    def keep_scores(g):
                        act.wait_ge(sc_ps, g.n + 1)
                        act.wait_ge(sc_out[g.p], earlier(g.turn * 16))
                        act.copy(sc[g.p][:], sc_bank[g.p][:, 0:G * E]).then_inc(sc_s, 1)

                    def body(g):
                        keep_turned(g.after())
                        keep_scores(g)
                    keep_turned(FIRST)
                    body(FIRST)
                    middle_groups(act, body)
                    keep_scores(LAST)

        def place_rows(tile_expert):
            s = lambda name: sem(f"pr_{name}")
            sc_in, small, exp_s, both_s, count_ps, out_s, numbered = (
                s(k) for k in ("sc_in", "small", "exp", "both", "count_ps", "out", "numbered"))
            with ExitStack() as mine, nc.Block() as block:
                new = lambda name, shape, dt=F32: sb(f"pr{name}", shape, dt, mine)
                BE = [128, B, E]
                scores, shifted, probs, left, ranked, pos = (new(k, BE) for k in ("sc", "sh", "pr", "lf", "rk", "ps"))
                hot = [new(f"hot{k}", BE) for k in range(2)]
                both, scan = new("both", BE, BF16), [new(f"scan{i}", BE) for i in range(2)]
                top, total, over, best = (new(k, [128, B]) for k in ("top", "total", "over", "best"))
                high = [new(f"high{k}", [128, B]) for k in range(2)]
                place, place_i = new("place", [128, B * 2]), new("pli", [128, B * 2], I32)
                tags, result = new("tags", [128, B * 2, 2], I32), new("result", [128, B * 2], I32)
                share = tags[:, :, 0].bitcast(F32).rearrange("t (b k) -> t b k", k=2)
                tiles, first = new("tiles", [128, E]), new("first", [128, E])
                ends = [new(f"ends{i}", [128, E]) for i in range(2)]
                more, passed, expert = new("more", [128, E, B]), new("passed", [128, SLOTS, E]), new("ex", [128, SLOTS])
                before_ps, tile_ps = (bank[i][:, 0:B * E].rearrange("t (b e) -> t b e", e=E) for i in range(2))
                exp_at = 2

                @block.sync
                def _(sp):
                    sp.dma_start(scores[:], scores_d.rearrange("t (b e) -> t b e", e=E)).then_inc(sc_in, 16)
                    sp.wait_ge(out_s, 1)
                    sp.dma_start(tags_d, tags[:]).then_inc(sc_in, 16)
                    sp.dma_start(place_d, place_i[:]).then_inc(sc_in, 16)
                    sp.wait_ge(sc_in, 48)

                @block.gpsimd
                def _(pool):
                    pool.iota(result[:], pattern=[[2 * T, B], [1, 2]], base=0, channel_multiplier=2).then_inc(numbered, 1)

                @block.tensor
                def _(pe):
                    pe.wait_ge(both_s, 1)
                    flat = both[:].rearrange("t b e -> t (b e)")
                    pe.matmul(bank[0][:, 0:B * E], earlier_tokens[:], flat, start=True, stop=True).then_inc(count_ps, 1)
                    pe.matmul(bank[1][:, 0:B * E], all_tokens[:], flat, start=True, stop=True).then_inc(count_ps, 1)

                @block.scalar
                def _(act):
                    act.wait_ge(small, exp_at)
                    act.activation(probs[:], shifted[:], ACT.Exp).then_inc(exp_s, 1)

                @block.vector
                def _(dve):
                    done = [0]

                    def step(ins):
                        ins.then_inc(small, 1)
                        done[0] = done[0] + 1
                        dve.wait_ge(small, done[0])

                    def wide(x):
                        return x[:].unsqueeze(2).broadcast_to(BE)

                    dve.wait_ge(sc_in, 16)
                    step(dve.tensor_reduce(top[:], scores[:], AX_X, ALU.max))
                    step(dve.tensor_tensor(shifted[:], scores[:], wide(top), ALU.subtract))
                    dve.wait_ge(exp_s, 1)
                    step(dve.tensor_reduce(total[:], probs[:], AX_X, ALU.add))
                    step(dve.reciprocal(over[:], total[:]))
                    step(dve.tensor_tensor(shifted[:], probs[:], wide(over), ALU.mult))
                    for k in range(2):
                        from_ = shifted if k == 0 else left
                        step(dve.tensor_reduce(high[k][:], from_[:], AX_X, ALU.max))
                        step(dve.tensor_tensor(ranked[:], from_[:], wide(high[k]), ALU.is_ge))
                        step(dve.tensor_tensor(ranked[:], ranked[:], rank[:, 0:1, :].broadcast_to(BE), ALU.mult))
                        step(dve.tensor_reduce(best[:], ranked[:], AX_X, ALU.max))
                        step(dve.tensor_tensor(hot[k][:], ranked[:], wide(best), ALU.is_equal))
                        if k == 0:
                            step(dve.scalar_tensor_tensor(out=left[:], in0=hot[0][:], scalar=-2.0, in1=shifted[:],
                                                          op0=ALU.mult, op1=ALU.add))
                    dve.tensor_tensor(both[:], hot[0][:], hot[1][:], ALU.add).then_inc(both_s, 1)
                    step(dve.tensor_tensor(total[:], high[0][:], high[1][:], ALU.add))
                    step(dve.reciprocal(over[:], total[:]))
                    for k in range(2):
                        dve.tensor_tensor(share[:, :, k], high[k][:], over[:], ALU.mult)
                    dve.wait_ge(numbered, 1)
                    dve.tensor_copy(tags[:, :, 1], result[:])

                    dve.wait_ge(count_ps, 2)
                    step(dve.tensor_copy(scan[0][:], tile_ps))
                    at, reach = 0, 1
                    while reach < B:
                        dve.tensor_copy(scan[1 - at][:, 0:reach, :], scan[at][:, 0:reach, :])
                        step(dve.tensor_tensor(scan[1 - at][:, reach:B, :], scan[at][:, reach:B, :],
                                               scan[at][:, 0:B - reach, :], ALU.add))
                        at, reach = 1 - at, 2 * reach
                    upto = scan[at]
                    count = upto[:, B - 1, :].unsqueeze(2).broadcast_to([128, E, B])
                    edges = tile_no[:, 0:B].unsqueeze(1).broadcast_to([128, E, B])
                    step(dve.scalar_tensor_tensor(out=more[:], in0=edges, scalar=float(T), in1=count,
                                                  op0=ALU.mult, op1=ALU.is_lt))
                    step(dve.tensor_reduce(tiles[:], more[:], AX_X, ALU.add))
                    step(dve.tensor_copy(ends[0][:], tiles[:]))
                    end, reach = 0, 1
                    while reach < E:
                        dve.tensor_copy(ends[1 - end][:, 0:reach], ends[end][:, 0:reach])
                        step(dve.tensor_tensor(ends[1 - end][:, reach:E], ends[end][:, reach:E],
                                               ends[end][:, 0:E - reach], ALU.add))
                        end, reach = 1 - end, 2 * reach
                    last_tile = ends[end]
                    step(dve.tensor_tensor(first[:], last_tile[:], tiles[:], ALU.subtract))
                    step(dve.tensor_scalar(first[:], first[:], float(T), None, ALU.mult))
                    step(dve.tensor_tensor(pos[:], upto[:], tile_ps, ALU.subtract))
                    step(dve.tensor_tensor(pos[:], pos[:], before_ps, ALU.add))
                    step(dve.tensor_tensor(pos[:], pos[:], first[:].unsqueeze(1).broadcast_to(BE), ALU.add))
                    for k in range(2):
                        step(dve.tensor_tensor(ranked[:], hot[k][:], pos[:], ALU.mult))
                        step(dve.tensor_reduce(place[:].rearrange("t (b k) -> t b k", k=2)[:, :, k], ranked[:], AX_X, ALU.add))
                    dve.tensor_copy(place_i[:], place[:]).then_inc(out_s, 1)
                    step(dve.tensor_tensor(passed[:], tile_no[:].unsqueeze(2).broadcast_to([128, SLOTS, E]),
                                           last_tile[:].unsqueeze(1).broadcast_to([128, SLOTS, E]), ALU.is_ge))
                    step(dve.tensor_reduce(expert[:], passed[:], AX_X, ALU.add))
                    step(dve.tensor_scalar(expert[:], expert[:], float(E - 1), None, ALU.min))
                    step(dve.tensor_copy(tile_expert[:], expert[:]))

        def sort_rows(gate_w, up_w, down_w, w_in):
            s = lambda name: sem(f"so_{name}")
            x_in, moved = ([s(f"{k}{p}") for p in range(2)] for k in ("x_in", "moved"))
            with ExitStack() as mine, nc.Block() as block:
                two = lambda name, shape, dt=F32: [sb(f"so{name}{p}", shape, dt, mine) for p in range(2)]
                row, place = two("x", [128, G * 2, ROW]), two("pl", [128, G * 2], I32)
                LOADS = 16 * 4
                SENT = 16 * 2 * G
                begun = s("begun")

                @block.sync
                def _(sp):
                    def load(g):
                        sp.wait_ge(moved[g.p], earlier(g.turn * SENT))
                        of_choice = row[g.p][:].rearrange("t (b k) d -> t b k d", k=2)
                        for k in range(2):
                            sp.dma_start(of_choice[:, :, k, 0:D], rows(x_norm, g)).then_inc(x_in[g.p], 16)
                        sp.dma_start(row[g.p][:, :, D:ROW].bitcast(I32), tags_d[:, bass.ds(g.n * G * 2, G * 2), :]
                                     ).then_inc(x_in[g.p], 16)
                        sp.dma_start(place[g.p][:], place_d[:, bass.ds(g.n * G * 2, G * 2)]).then_inc(x_in[g.p], 16)
                    all_groups(sp, load)

                @block.scalar
                def _(act):
                    act.dma_start(gate_w[:], a["L1_ffn_gate_proj"].rearrange("e d f -> d e f")).then_inc(w_in, 16)
                    act.dma_start(up_w[:], a["L1_ffn_up_proj"].rearrange("e d f -> d e f")).then_inc(w_in, 16)
                    for f, (f0, fn) in enumerate(FCH):
                        act.dma_start(down_w[0:fn, :, f, :],
                                      a["L1_ffn_down_proj"][:, f0:f0 + fn, :].rearrange("e f d -> f e d")).then_inc(w_in, 16)
                    act.wait_ge(w_in, 16 * (2 + len(FCH)))

                @block.gpsimd
                def _(pool):
                    def move(g):
                        pool.wait_ge(x_in[g.p], (g.turn + 1) * LOADS)
                        pool.wait_ge(begun, earlier(g.n - 1))
                        pool.tensor_tensor(pool_cell[:, g.p:g.p + 1], epsilon[:, 0:1], epsilon[:, 0:1], ALU.mult
                                           ).then_inc(begun, 1)
                        for i in range(2 * G):
                            pool.indirect_dma_start(
                                sorted_in[:], bass.IndirectOffsetOnAxis(ap=place[g.p][:, i:i + 1], axis=0),
                                row[g.p][:, i, :], None).then_inc(moved[g.p], 16)
                    all_groups(pool, move)
                    for p in range(2):
                        pool.wait_ge(moved[p], NG // 2 * SENT)

        def run_experts(gate_w, up_w, down_w, w_in, tile_expert):
            s = lambda name: sem(f"ex_{name}")
            x_in, y_out = ([s(f"{k}{p}") for p in range(2)] for k in ("x_in", "y_out"))
            tags_s, begun = s("tags"), s("begun")
            turned, kept, gate_ps, up_ps, silu_s, act_s = (s(k) for k in ("turned", "kept", "gate", "up", "silu", "act"))
            hidden_ps, hidden_s, down_ps, y_s = (s(k) for k in ("hidden_ps", "hidden", "down", "y"))
            with ExitStack() as mine, nc.Block() as block:
                two = lambda name, shape, dt=F32: [sb(f"ex{name}{p}", shape, dt, mine) for p in range(2)]
                x_g, x_t, y_g = two("x", [128, G, ROW]), two("xt", [128, GT]), two("y", [128, D])
                share, result = two("sh", [128, G]), two("re", [128, G], I32)
                silu, acts = two("si", [128, F]), two("ac", [128, F])
                acts_t = two("at", [128, len(FCH) * T])
                t_bank, gate_bank, up_bank, hidden_bank, y_bank = bank[0], bank[1:3], bank[3:5], bank[5], bank[6:8]
                whole = 2 * T
                rest_rows = FCH[2][1]

                def tiles_of(x, g):
                    return x[bass.ds(g.n * GT, GT)].rearrange("(t p) d -> p t d", p=T)

                def expert_of(eng, q):
                    return eng.value_load(tile_expert[0:1, bass.ds(q.m, 1)], min_val=0, max_val=E - 1)

                @block.sync
                def _(sp):
                    def load(g):
                        sp.wait_ge(turned, earlier(g.n - 1))
                        sp.wait_ge(tags_s, earlier(g.n - 1))
                        sp.dma_start(x_g[g.p][:], tiles_of(sorted_in, g)).then_inc(x_in[g.p], 16)
                    all_groups(sp, load, NQ)

                @block.gpsimd
                def _(pool):
                    def send(q):
                        pool.wait_ge(begun, earlier(q.m - 1))
                        pool.wait_ge(y_s, q.m + 1)
                        pool.tensor_tensor(pool_cell[:, q.p:q.p + 1], epsilon[:, 0:1], epsilon[:, 0:1], ALU.mult
                                           ).then_inc(begun, 1)
                        pool.indirect_dma_start(
                            results[:], bass.IndirectOffsetOnAxis(ap=result[q.g.p][:, q.b:q.b + 1], axis=0),
                            y_g[q.p][:], None).then_inc(y_out[q.p], 16)

                    def body(g):
                        for t in range(G):
                            send(Seq(g, t))
                    all_groups(pool, body, NQ)
                    for p in range(2):
                        pool.wait_ge(y_out[p], 16 * (SLOTS // 2))

                @block.tensor
                def _(pe):
                    def turn(g):
                        pe.wait_ge(x_in[g.p], g.turn * 16 + 16)
                        pe.wait_ge(kept, earlier(g.n))
                        for t in range(G):
                            mm = pe.transpose(t_bank[:, t * T:(t + 1) * T], x_g[g.p][:, t, 0:D], ident[:])
                        mm.then_inc(turned, 1)

                    def gate_up(q):
                        e = expert_of(pe, q)
                        x = x_t[q.g.p][:, q.b * T:(q.b + 1) * T]
                        if q.b == 0:
                            pe.wait_ge(kept, q.g.n + 1)
                        pe.wait_ge(silu_s, earlier(q.m - 1))
                        pe.matmul(gate_bank[q.p][:, 0:F], x, gate_w[:, bass.ds(e, 1), :].rearrange("d e f -> d (e f)"),
                                  start=True, stop=True).then_inc(gate_ps, 1)
                        pe.wait_ge(act_s, earlier(q.m - 1))
                        pe.matmul(up_bank[q.p][:, 0:F], x, up_w[:, bass.ds(e, 1), :].rearrange("d e f -> d (e f)"),
                                  start=True, stop=True).then_inc(up_ps, 1)

                    def turn_hidden(q):
                        pe.wait_ge(act_s, q.m + 1)
                        pe.wait_ge(hidden_s, earlier(2 * q.m))
                        for f, (f0, fn) in enumerate(FCH):
                            mm = pe.transpose(hidden_bank[0:fn, f * T:(f + 1) * T], acts[q.p][:, f0:f0 + fn], ident[:])
                        mm.then_inc(hidden_ps, 1)

                    def down(q):
                        e = expert_of(pe, q)
                        pe.wait_ge(hidden_s, 2 * (q.m + 1))
                        pe.wait_ge(y_s, earlier(q.m - 1))
                        for f, (f0, fn) in enumerate(FCH):
                            mm = pe.matmul(y_bank[q.p][:, 0:D], acts_t[q.p][0:fn, f * T:(f + 1) * T],
                                           down_w[0:fn, bass.ds(e, 1), f, :].rearrange("f e d -> f (e d)"),
                                           start=(f == 0), stop=(f == len(FCH) - 1))
                        mm.then_inc(down_ps, 1)

                    def body(g, first=False, last=False):
                        for t in range(G):
                            q = Seq(g, t)
                            gate_up(q)
                            if not (first and t < 2):
                                down(q.ahead(-2))
                            if not (first and t < 1):
                                turn_hidden(q.ahead(-1))
                            if t == 1 and not last:
                                turn(g.after())

                    turn(FIRST)
                    body(FIRST, first=True)
                    middle_groups(pe, body, NQ)
                    body(LAST_TILES, last=True)
                    down(Seq(LAST_TILES, G - 2))
                    turn_hidden(Seq(LAST_TILES, G - 1))
                    down(Seq(LAST_TILES, G - 1))

                @block.scalar
                def _(act):
                    def keep_turned(g):
                        act.wait_ge(turned, g.n + 1)
                        act.wait_ge(up_ps, earlier((g.n - 1) * G))
                        act.copy(x_t[g.p][:], t_bank[:]).then_inc(kept, 1)

                    def gate(q):
                        act.wait_ge(gate_ps, q.m + 1)
                        act.wait_ge(act_s, earlier(q.m - 1))
                        act.activation(silu[q.p][:], gate_bank[q.p][:, 0:F], ACT.Silu).then_inc(silu_s, 1)

                    def keep_hidden(q):
                        act.wait_ge(hidden_ps, q.m + 1)
                        act.wait_ge(down_ps, earlier(q.m - 1))
                        act.copy(acts_t[q.p][:, 0:whole], hidden_bank[:, 0:whole]).then_inc(hidden_s, 1)
                        act.copy(acts_t[q.p][0:rest_rows, whole:whole + T],
                                 hidden_bank[0:rest_rows, whole:whole + T]).then_inc(hidden_s, 1)

                    def keep_out(q):
                        if q.b == 0:
                            act.wait_ge(tags_s, q.g.n + 1)
                        act.wait_ge(down_ps, q.m + 1)
                        act.wait_ge(y_out[q.p], earlier(q.turn * 16))
                        act.activation(y_g[q.p][:], y_bank[q.p][:, 0:D], ACT.Copy, scale=share[q.g.p][:, q.b:q.b + 1]
                                       ).then_inc(y_s, 1)

                    def body(g, first=False, last=False):
                        for t in range(G):
                            q = Seq(g, t)
                            gate(q)
                            if not (first and t < 2):
                                keep_out(q.ahead(-2))
                            if not (first and t < 1):
                                keep_hidden(q.ahead(-1))
                            if t == 1 and not last:
                                keep_turned(g.after())

                    keep_turned(FIRST)
                    body(FIRST, first=True)
                    middle_groups(act, body, NQ)
                    body(LAST_TILES, last=True)
                    keep_out(Seq(LAST_TILES, G - 2))
                    keep_hidden(Seq(LAST_TILES, G - 1))
                    keep_out(Seq(LAST_TILES, G - 1))

                @block.vector
                def _(dve):
                    def activate(q):
                        dve.wait_ge(silu_s, q.m + 1)
                        dve.wait_ge(up_ps, q.m + 1)
                        dve.wait_ge(hidden_ps, earlier(q.m - 1))
                        dve.tensor_tensor(acts[q.p][:], up_bank[q.p][:, 0:F], silu[q.p][:], ALU.mult).then_inc(act_s, 1)

                    def keep_tags(g):
                        dve.wait_ge(x_in[g.p], g.turn * 16 + 16)
                        for p in range(2):
                            dve.wait_ge(y_out[p], earlier((g.n - 1) * 16 * (G // 2)))
                        dve.tensor_copy(share[g.p][:].unsqueeze(2), x_g[g.p][:, :, D:D + 1])
                        dve.tensor_copy(result[g.p][:].unsqueeze(2), x_g[g.p][:, :, D + 1:ROW].bitcast(I32)).then_inc(tags_s, 1)

                    def body(g, last=False):
                        for t in range(G):
                            activate(Seq(g, t))
                            if t == G - 1 and not last:
                                keep_tags(g.after())
                    keep_tags(FIRST)
                    body(FIRST)
                    middle_groups(dve, body, NQ)
                    body(LAST_TILES, last=True)

        def combine(x_src, x_dst):
            s = lambda name: sem(f"co_{name}")
            x_in, x_out = ([s(f"{k}{p}") for p in range(2)] for k in ("x_in", "x_out"))
            first_s, sum_s = s("first"), s("sum")
            with ExitStack() as mine, nc.Block() as block:
                two = lambda name, shape, dt=F32: [sb(f"co{name}{p}", shape, dt, mine) for p in range(2)]
                x_g, x_sum, y_g = two("x", [128, G, D]), two("xs", [128, G, D]), two("y", [128, G, 2 * D])
                by_token = results[0:SPARE].rearrange("(b t k) d -> b t (k d)", t=T, k=2)

                @block.sync
                def _(sp):
                    def load(g):
                        sp.wait_ge(sum_s, earlier(g.n - 1))
                        sp.dma_start(x_g[g.p][:], rows(x_src, g)).then_inc(x_in[g.p], 16)
                        sp.dma_start(y_g[g.p][:], rows(by_token, g)).then_inc(x_in[g.p], 16)
                    all_groups(sp, load)

                @block.scalar
                def _(act):
                    def store(g):
                        act.wait_ge(sum_s, g.n + 1)
                        act.dma_start(rows(x_dst, g), x_sum[g.p][:]).then_inc(x_out[g.p], 16)
                    all_groups(act, store)
                    for p in range(2):
                        act.wait_ge(x_out[p], 16 * (NG // 2))

                @block.vector
                def _(dve):
                    def add(g):
                        dve.wait_ge(x_in[g.p], (g.turn + 1) * 32)
                        dve.wait_ge(x_out[g.p], earlier(g.turn * 16))
                        dve.tensor_tensor(x_sum[g.p][:], x_g[g.p][:], y_g[g.p][:, :, 0:D], ALU.add).then_inc(first_s, 1)
                        dve.wait_ge(first_s, g.n + 1)
                        dve.tensor_tensor(x_sum[g.p][:], x_sum[g.p][:], y_g[g.p][:, :, D:2 * D], ALU.add).then_inc(sum_s, 1)
                    all_groups(dve, add)

        prepare()
        project()
        early.close()
        attention(0, a["x"], x_attn0)
        experts0(x_attn0, x_ffn0)
        clear_semaphores()
        attention(1, x_ffn0, x_attn1)
        clear_semaphores()
        experts1(x_attn1, out)


INS = ["x", "ctx_1024",
       "L0_xattn_w_q", "L0_xattn_b_q", "L0_xattn_w_k", "L0_xattn_b_k", "L0_xattn_w_v", "L0_xattn_b_v",
       "L0_xattn_w_o", "L0_xattn_b_o", "L0_ffn_gate_w", "L0_ffn_expert_w",
       "L1_xattn_Wq", "L1_xattn_bq", "L1_xattn_Wk", "L1_xattn_bk", "L1_xattn_Wv", "L1_xattn_bv",
       "L1_xattn_Wo", "L1_xattn_bo", "L1_ffn_router_w", "L1_ffn_gate_proj", "L1_ffn_up_proj", "L1_ffn_down_proj"]


def kernel(**inputs):
    import numpy as np
    import concourse.bacc as bacc
    from concourse.bass_utils import run_bass_kernel_spmd

    nc = bacc.Bacc("TRN2", target_bir_lowering=False, num_devices=1)
    arrays, aps = {}, {}
    for name in INS:
        arrays[name] = np.ascontiguousarray(inputs[name])
        aps[name] = nc.dram_tensor(name, arrays[name].shape, mybir.dt.from_np(arrays[name].dtype), kind="ExternalInput").ap()
    out = nc.dram_tensor("out", (B, T, D), F32, kind="ExternalOutput").ap()
    build(nc, aps, out)
    ran = run_bass_kernel_spmd(nc, [arrays], core_ids=[0])
    return ran.results[0]["out"]
```
